# Optimizing a Trainium2 kernel written in Bass

```python
import numpy as np
import jax
import jax.numpy as jnp

def _softmax(x, axis=-1):
    return jax.nn.softmax(x, axis=axis)

def _gelu(x):
    return jax.nn.gelu(x, approximate=True)

def _silu(x):
    return jax.nn.silu(x)

def _sigmoid(x):
    return jax.nn.sigmoid(x)

def _layernorm(x, axis=-1, eps=1e-05):
    m = jnp.mean(x, axis=axis, keepdims=True)
    v = jnp.var(x, axis=axis, keepdims=True)
    return (x - m) / jnp.sqrt(v + eps)

def _scatter_add(tgt, idx, src, axis=0):
    return tgt.at[idx].add(src)

def _segment_sum(src, seg, n):
    return jax.ops.segment_sum(src, seg, n)
kernel_name = 'mk_decoder_postln_d4_seqx_r8_b98486'

def setup_inputs(seed: int=0):
    np.random.seed(seed)
    _w = jnp.asarray

    def _rec_inputs():
        import jax
        import jax.numpy as jnp
        _rk = jax.random.key(seed)
        x = -0.0001033 + 0.9999 * jax.random.normal(jax.random.fold_in(_rk, 1), (2, 512, 128), jnp.float32)
        _lenS = 512 - jax.random.randint(jax.random.fold_in(_rk, 7), (2,), 0, max(1, 512 // 4) + 1, jnp.int32)
        _lenS2 = 77 - jax.random.randint(jax.random.fold_in(_rk, 8), (2,), 0, max(1, 77 // 4) + 1, jnp.int32)
        _ctx_1024P = jax.random.normal(jax.random.fold_in(_rk, 11), (2, 16, 128), jnp.float32)
        _ctx_1024c = jax.random.dirichlet(jax.random.fold_in(_rk, 511), 0.3 * jnp.ones((16,), jnp.float32), (2, 77))
        _ctx_1024t = jnp.einsum('bsk,bkd->bsd', _ctx_1024c, _ctx_1024P)
        _ctx_1024t = _ctx_1024t * jax.lax.rsqrt(jnp.mean(jnp.square(_ctx_1024t)) + 1e-12) * 0.953939
        ctx_1024 = -0.000292821 + 1.00034 * (_ctx_1024t + 0.3 * jax.random.normal(jax.random.fold_in(_rk, 611), (2, 77, 128), jnp.float32))
        _validS = jnp.arange(512)[None, :] < _lenS[:, None]
        _validS2 = jnp.arange(77)[None, :] < _lenS2[:, None]
        _causal = jnp.tril(jnp.ones((512, 512), dtype=bool))
        mask_1x1xSxS2_if1 = jnp.where(jnp.ones((1, 1, 512, 77), dtype=bool), 1, 0).astype(jnp.int32)
        mask_Bx1xSxS2_ik1 = jnp.where(jnp.broadcast_to(_validS2[:, None, None, :], (2, 1, 512, 77)), 1, 0).astype(jnp.int32)
        mask_BxS2_bk0 = jnp.logical_not(jnp.broadcast_to(_validS2[:, :], (2, 77)))
        return (x, ctx_1024, mask_1x1xSxS2_if1, mask_Bx1xSxS2_ik1, mask_BxS2_bk0)
    x, ctx_1024, mask_1x1xSxS2_if1, mask_Bx1xSxS2_ik1, mask_BxS2_bk0 = _rec_inputs()

    def _L0_attn_setup():
        import jax, jax.numpy as jnp
        import numpy as np
        D_MODEL = 128
        NHEAD = 16
        HEAD_DIM = D_MODEL // NHEAD
        SCALE = HEAD_DIM ** (-0.5)
        EPS_LN = 1e-05
        key = jax.random.key(seed)
        ks = jax.random.split(key, 7)
        B, T, D = (2, 256, D_MODEL)
        x = jax.random.normal(ks[0], (B, T, D), dtype=jnp.float32)
        ln_gamma = jnp.ones((D,), dtype=jnp.float32)
        ln_beta = jnp.zeros((D,), dtype=jnp.float32)
        s = 1.0 / np.sqrt(D)
        W_qkv = jax.random.uniform(ks[1], (D, 3 * D), minval=-s, maxval=s, dtype=jnp.float32)
        b_qkv = jax.random.uniform(ks[2], (3 * D,), minval=-s, maxval=s, dtype=jnp.float32)
        W_proj = jax.random.uniform(ks[3], (D, D), minval=-s, maxval=s, dtype=jnp.float32)
        b_proj = jax.random.uniform(ks[4], (D,), minval=-s, maxval=s, dtype=jnp.float32)
        return {'x': x, 'ln_gamma': ln_gamma, 'ln_beta': ln_beta, 'W_qkv': W_qkv, 'b_qkv': b_qkv, 'W_proj': W_proj, 'b_proj': b_proj}
    _L0_attn_all = _L0_attn_setup()
    _L0_attn_in = {k: v for k, v in _L0_attn_all.items() if k in ('ln_gamma', 'ln_beta', 'W_qkv', 'b_qkv', 'W_proj', 'b_proj')}
    del _L0_attn_all

    def _L0_xattn_setup():
        import jax, jax.numpy as jnp
        import numpy as np
        from jax import lax
        B, T, F = (32, 128, 128)
        CONV_UNITS = 256
        SHORT_UNITS = 256
        RATE = 4
        key = jax.random.key(seed)
        k1, k2, k3 = jax.random.split(key, 3)
        inputs = jax.random.normal(k1, (B, T, F), dtype=jnp.float32)
        memory = jax.random.normal(k2, (B, CONV_UNITS + SHORT_UNITS, F), dtype=jnp.float32)
        conv_w = jax.random.normal(k3, (RATE, F, F), dtype=jnp.float32) * 0.02
        conv_b = jnp.zeros((F,), dtype=jnp.float32)
        return {'inputs': inputs, 'memory': memory, 'conv_w': conv_w, 'conv_b': conv_b, 'conv_units': CONV_UNITS, 'short_units': SHORT_UNITS, 'rate': RATE}
    _L0_xattn_all = _L0_xattn_setup()
    _L0_xattn_in = {k: v for k, v in _L0_xattn_all.items() if k in ('conv_w', 'conv_b')}
    del _L0_xattn_all

    def _L0_ffn_setup():
        import jax, jax.numpy as jnp
        import numpy as np
        B, L, D = (4, 64, 128)
        E, TOP_K = (16, 4)
        F = 4 * D
        key = jax.random.key(seed)
        ks = jax.random.split(key, 6)
        scale = 0.02
        return {'x': jax.random.normal(ks[0], (B, L, D), jnp.float32), 'keys': jax.random.normal(ks[1], (E, D), jnp.float32), 'w1': jax.random.normal(ks[2], (E, F, D), jnp.float32) * scale, 'b1': jnp.zeros((E, F), jnp.float32), 'w2': jax.random.normal(ks[3], (E, D, F), jnp.float32) * scale, 'b2': jnp.zeros((E, D), jnp.float32), 'rw': jax.random.normal(ks[4], (E, D), jnp.float32) * scale, 'rb': jnp.zeros((E,), jnp.float32)}
    _L0_ffn_all = _L0_ffn_setup()
    _L0_ffn_in = {k: v for k, v in _L0_ffn_all.items() if k in ('keys', 'w1', 'b1', 'w2', 'b2', 'rw', 'rb')}
    del _L0_ffn_all

    def _L1_attn_setup():
        import jax, jax.numpy as jnp
        import numpy as np
        DIM = 128
        HEADS = 16
        DHEAD = 64
        INNER = HEADS * DHEAD
        B, N = (1, 256)
        ROPE_BASE = 10000.0
        LN_EPS = 1e-05

        def rope_tables(seq_len, d, dtype):
            theta = 1.0 / ROPE_BASE ** (jnp.arange(0, d, 2, dtype=dtype) / d)
            pos = jnp.arange(seq_len, dtype=dtype)
            freqs = pos[:, None] * theta[None, :]
            emb = jnp.concatenate([freqs, freqs], axis=-1)
            return (jnp.cos(emb), jnp.sin(emb))

        def apply_rotary(x, cos, sin):
            x1, x2 = (x[..., ::2], x[..., 1::2])
            x_rot = jnp.stack([-x2, x1], axis=-1).reshape(x.shape)
            return x * cos + x_rot * sin
        key = jax.random.key(seed)
        ks = jax.random.split(key, 6)
        x = jax.random.normal(ks[0], (B, N, DIM), dtype=jnp.float32)
        gamma = jnp.ones((DIM,), dtype=jnp.float32)
        Wq = jax.random.normal(ks[1], (DIM, INNER), dtype=jnp.float32) * 0.02
        Wkv = jax.random.normal(ks[2], (DIM, 2 * INNER), dtype=jnp.float32) * 0.02
        W_bilinear = jnp.eye(DHEAD, dtype=jnp.float32)[None] + jax.random.normal(ks[3], (HEADS, DHEAD, DHEAD), dtype=jnp.float32) * 0.02
        Wo = jax.random.normal(ks[4], (INNER, DIM), dtype=jnp.float32) * 0.02
        return {'x': x, 'gamma': gamma, 'Wq': Wq, 'Wkv': Wkv, 'W_bilinear': W_bilinear, 'Wo': Wo}
    _L1_attn_all = _L1_attn_setup()
    _L1_attn_in = {k: v for k, v in _L1_attn_all.items() if k in ('gamma', 'Wq', 'Wkv', 'W_bilinear', 'Wo')}
    del _L1_attn_all

    def _L1_xattn_setup():
        import jax, jax.numpy as jnp
        import numpy as np
        import math
        D_MODEL = 128
        N_HEADS = 16
        HEAD_DIM = D_MODEL // N_HEADS
        BATCH = 2
        SEQ = 512
        key = jax.random.key(seed)
        ks = jax.random.split(key, 12)
        s = 0.02
        inp = {'query': jax.random.normal(ks[0], (BATCH, SEQ, D_MODEL), jnp.float32), 'key': jax.random.normal(ks[1], (BATCH, SEQ, D_MODEL), jnp.float32), 'value': jax.random.normal(ks[2], (BATCH, SEQ, D_MODEL), jnp.float32), 'mask': jnp.ones((1, 1, SEQ, SEQ), jnp.int32), 'Wq': jax.random.normal(ks[3], (D_MODEL, D_MODEL), jnp.float32) * s, 'bq': jax.random.normal(ks[4], (D_MODEL,), jnp.float32) * s, 'Wk': jax.random.normal(ks[5], (D_MODEL, D_MODEL), jnp.float32) * s, 'bk': jax.random.normal(ks[6], (D_MODEL,), jnp.float32) * s, 'Wv': jax.random.normal(ks[7], (D_MODEL, D_MODEL), jnp.float32) * s, 'bv': jax.random.normal(ks[8], (D_MODEL,), jnp.float32) * s, 'Wo': jax.random.normal(ks[9], (D_MODEL, D_MODEL), jnp.float32) * s, 'bo': jax.random.normal(ks[10], (D_MODEL,), jnp.float32) * s}
        return inp
    _L1_xattn_all = _L1_xattn_setup()
    _L1_xattn_in = {k: v for k, v in _L1_xattn_all.items() if k in ('Wq', 'bq', 'Wk', 'bk', 'Wv', 'bv', 'Wo', 'bo')}
    del _L1_xattn_all

    def _L1_ffn_setup():
        import jax, jax.numpy as jnp
        import numpy as np
        IN_F = 128
        OUT_F = 128
        B, S = (8, 512)

        def _pack_ternary(tern):
            enc = (tern + 1.0).astype(jnp.int32).reshape(-1)
            return (enc[0::4] | enc[1::4] << 2 | enc[2::4] << 4 | enc[3::4] << 6).astype(jnp.int32)
        key = jax.random.key(seed)
        kx, kw = jax.random.split(key)
        x = jax.random.normal(kx, (B, S, IN_F), dtype=jnp.float32)
        w = jax.random.normal(kw, (OUT_F, IN_F), dtype=jnp.float32) * 0.02
        scale = jnp.maximum(jnp.mean(jnp.abs(w)), 1e-05)
        wn = w / scale
        tern = jnp.sign(wn) * (jnp.abs(wn) > 0.5).astype(jnp.float32)
        packed = _pack_ternary(tern)
        bias = jnp.zeros((OUT_F,), dtype=jnp.float32)
        return {'x': x, 'packed_weight': packed, 'weight_scale': scale.reshape(1), 'bias': bias}
    _L1_ffn_all = _L1_ffn_setup()
    _L1_ffn_in = {k: v for k, v in _L1_ffn_all.items() if k in ('packed_weight', 'weight_scale', 'bias')}
    del _L1_ffn_all

    def _L2_attn_setup():
        import jax, jax.numpy as jnp
        import numpy as np
        D_MODEL, N_HEADS, BATCH, SEQ = (128, 16, 2, 256)

        def get_freqs(seq, n_dim):
            inv_freq = 1.0 / 10000.0 ** (jnp.arange(0, n_dim, 2, dtype=jnp.float32) / n_dim)
            pos = jnp.arange(seq, dtype=jnp.float32)
            return pos[:, None] * inv_freq[None, :]

        def rope(x, freq):
            cos = jnp.cos(freq)[None, :, None, :]
            sin = jnp.sin(freq)[None, :, None, :]
            x1, x2 = (x[..., ::2], x[..., 1::2])
            r1 = x1 * cos - x2 * sin
            r2 = x1 * sin + x2 * cos
            return jnp.stack([r1, r2], axis=-1).reshape(x.shape)
        key = jax.random.key(seed)
        ks = jax.random.split(key, 5)
        w_scale = 0.01
        return {'x': jax.random.normal(ks[0], (BATCH, SEQ, D_MODEL), dtype=jnp.float32), 'qw': jax.random.normal(ks[1], (D_MODEL, D_MODEL), dtype=jnp.float32) * w_scale, 'kw': jax.random.normal(ks[2], (D_MODEL, D_MODEL), dtype=jnp.float32) * w_scale, 'vw': jax.random.normal(ks[3], (D_MODEL, D_MODEL), dtype=jnp.float32) * w_scale, 'ow': jax.random.normal(ks[4], (D_MODEL, D_MODEL), dtype=jnp.float32) * w_scale}
    _L2_attn_all = _L2_attn_setup()
    _L2_attn_in = {k: v for k, v in _L2_attn_all.items() if k in ('qw', 'kw', 'vw', 'ow')}
    del _L2_attn_all

    def _L2_xattn_setup():
        import jax, jax.numpy as jnp
        import numpy as np
        EMBED = 128
        HEADS = 16
        HEAD_DIM = EMBED // HEADS
        key = jax.random.key(seed)
        ks = jax.random.split(key, 9)
        N, Q, K = (2, 256, 256)
        queries = jax.random.normal(ks[0], (N, Q, EMBED), dtype=jnp.float32)
        keys_ = jax.random.normal(ks[1], (N, K, EMBED), dtype=jnp.float32)
        values = jax.random.normal(ks[2], (N, K, EMBED), dtype=jnp.float32)
        mask = jax.random.randint(ks[3], (N, 1, Q, K), 0, 2, dtype=jnp.int32)
        s = 1.0 / np.sqrt(EMBED)
        Wq = jax.random.normal(ks[4], (EMBED, EMBED), dtype=jnp.float32) * s
        Wk = jax.random.normal(ks[5], (EMBED, EMBED), dtype=jnp.float32) * s
        Wv = jax.random.normal(ks[6], (EMBED, EMBED), dtype=jnp.float32) * s
        Wo = jax.random.normal(ks[7], (EMBED, EMBED), dtype=jnp.float32) * s
        bo = jax.random.normal(ks[8], (EMBED,), dtype=jnp.float32) * s
        return {'queries': queries, 'keys': keys_, 'values': values, 'mask': mask, 'Wq': Wq, 'Wk': Wk, 'Wv': Wv, 'Wo': Wo, 'bo': bo}
    _L2_xattn_all = _L2_xattn_setup()
    _L2_xattn_in = {k: v for k, v in _L2_xattn_all.items() if k in ('Wq', 'Wk', 'Wv', 'Wo', 'bo')}
    del _L2_xattn_all

    def _L2_ffn_setup():
        import jax, jax.numpy as jnp
        import numpy as np
        L, E, H, F, K = (4, 4, 128, 512, 2)
        B, S = (4, 256)
        EPS = 1e-05

        def _moe_layer(x, rw, rb, g, b, w1, b1, w2, b2):
            logits = jnp.einsum('bsh,he->bse', x, rw) + rb
            probs = jax.nn.softmax(logits, axis=-1)
            vals, idx = jax.lax.top_k(probs, K)
            vals = vals / vals.sum(axis=-1, keepdims=True)
            mu = x.mean(axis=-1, keepdims=True)
            xc = x - mu
            xhat = xc * jax.lax.rsqrt((xc * xc).mean(axis=-1, keepdims=True) + EPS)
            xe = xhat[None] * g[:, None, None, :] + b[:, None, None, :]
            h = jax.nn.gelu(jnp.einsum('ebsh,ehf->ebsf', xe, w1) + b1[:, None, None, :], approximate=False)
            y = jnp.einsum('ebsf,efh->ebsh', h, w2) + b2[:, None, None, :]
            expert_out = x[None] + y
            comb = jnp.einsum('bsk,bske->bse', vals, jax.nn.one_hot(idx, E, dtype=x.dtype))
            return jnp.einsum('bse,ebsh->bsh', comb, expert_out)
        key = jax.random.key(seed)
        ks = jax.random.split(key, 4)
        return {'hidden_states': jax.random.normal(ks[0], (B, S, H), jnp.float32), 'router_w': 0.02 * jax.random.normal(ks[1], (L, H, E), jnp.float32), 'router_b': jnp.zeros((L, E), jnp.float32), 'ln_g': jnp.ones((L, E, H), jnp.float32), 'ln_b': jnp.zeros((L, E, H), jnp.float32), 'w1': 0.02 * jax.random.normal(ks[2], (L, E, H, F), jnp.float32), 'b1': jnp.zeros((L, E, F), jnp.float32), 'w2': 0.02 * jax.random.normal(ks[3], (L, E, F, H), jnp.float32), 'b2': jnp.zeros((L, E, H), jnp.float32)}
    _L2_ffn_all = _L2_ffn_setup()
    _L2_ffn_in = {k: v for k, v in _L2_ffn_all.items() if k in ('router_w', 'router_b', 'ln_g', 'ln_b', 'w1', 'b1', 'w2', 'b2')}
    del _L2_ffn_all

    def _L3_attn_setup():
        import jax, jax.numpy as jnp
        import numpy as np
        D_MODEL = 128
        NUM_HEADS = 16
        DEPTH = D_MODEL // NUM_HEADS
        B, T = (2, 256)

        def _rope(x):
            H = x.shape[1]
            D = x.shape[-1]
            inv_freq = 1.0 / 10000.0 ** (jnp.arange(0, D, 2, dtype=jnp.float32) / D)
            freqs = jnp.arange(H, dtype=jnp.float32)[:, None] * inv_freq[None, :]
            sin = jnp.sin(freqs)[:, None, :]
            cos = jnp.cos(freqs)[:, None, :]
            x1 = x[..., ::2]
            x2 = x[..., 1::2]
            rot = jnp.stack([x1 * cos - x2 * sin, x1 * sin + x2 * cos], axis=-1)
            return rot.reshape(x.shape)
        key = jax.random.key(seed)
        k_x, k_wq, k_bq, k_wf, k_bf = jax.random.split(key, 5)
        lim_qkv = 1.0 / np.sqrt(D_MODEL)
        lim_fc = 1.0 / np.sqrt(D_MODEL)
        return {'x': jax.random.normal(k_x, (B, T, D_MODEL), dtype=jnp.float32), 'w_qkv': jax.random.uniform(k_wq, (D_MODEL, 3 * D_MODEL), jnp.float32, -lim_qkv, lim_qkv), 'b_qkv': jax.random.uniform(k_bq, (3 * D_MODEL,), jnp.float32, -lim_qkv, lim_qkv), 'w_fc': jax.random.uniform(k_wf, (D_MODEL, D_MODEL), jnp.float32, -lim_fc, lim_fc), 'b_fc': jax.random.uniform(k_bf, (D_MODEL,), jnp.float32, -lim_fc, lim_fc)}
    _L3_attn_all = _L3_attn_setup()
    _L3_attn_in = {k: v for k, v in _L3_attn_all.items() if k in ('w_qkv', 'b_qkv', 'w_fc', 'b_fc')}
    del _L3_attn_all

    def _L3_xattn_setup():
        import jax, jax.numpy as jnp
        import numpy as np
        B, LQ, LKV = (8, 128, 256)
        QDIM, KDIM, HID = (128, 128, 128)
        key = jax.random.key(seed)
        ks = jax.random.split(key, 12)
        s = lambda d: 1.0 / np.sqrt(d)
        return {'query': jax.random.normal(ks[0], (B, LQ, QDIM), jnp.float32), 'key_value': jax.random.normal(ks[1], (B, LKV, KDIM), jnp.float32), 'key_mask': jax.random.randint(ks[2], (B, LKV), 0, 2).astype(bool), 'Wq': jax.random.uniform(ks[3], (QDIM, HID), jnp.float32, -s(QDIM), s(QDIM)), 'bq': jax.random.uniform(ks[4], (HID,), jnp.float32, -s(QDIM), s(QDIM)), 'Wk': jax.random.uniform(ks[5], (KDIM, HID), jnp.float32, -s(KDIM), s(KDIM)), 'bk': jax.random.uniform(ks[6], (HID,), jnp.float32, -s(KDIM), s(KDIM)), 'Wv': jax.random.uniform(ks[7], (KDIM, HID), jnp.float32, -s(KDIM), s(KDIM)), 'bv': jax.random.uniform(ks[8], (HID,), jnp.float32, -s(KDIM), s(KDIM)), 'Wo': jax.random.uniform(ks[9], (HID, QDIM), jnp.float32, -s(HID), s(HID)), 'bo': jax.random.uniform(ks[10], (QDIM,), jnp.float32, -s(HID), s(HID))}
    _L3_xattn_all = _L3_xattn_setup()
    _L3_xattn_in = {k: v for k, v in _L3_xattn_all.items() if k in ('Wq', 'bq', 'Wk', 'bk', 'Wv', 'bv', 'Wo', 'bo')}
    del _L3_xattn_all

    def _L3_ffn_setup():
        import jax, jax.numpy as jnp
        import numpy as np
        B, S, D = (2, 128, 128)
        H = 64
        E = 16
        K = 2
        HS = 2 * H
        ROUTE_SCALE = 1.0

        def _gated_mlp_act(y):
            u, g = jnp.split(y, 2, axis=-1)
            return u * jax.nn.silu(g)
        key = jax.random.key(seed)
        ks = jax.random.split(key, 6)
        s = 0.02
        return {'x': jax.random.normal(ks[0], (B, S, D), dtype=jnp.float32), 'Wg': jax.random.normal(ks[1], (E, D), dtype=jnp.float32) * s, 'W1': jax.random.normal(ks[2], (E, D, 2 * H), dtype=jnp.float32) * s, 'W2': jax.random.normal(ks[3], (E, H, D), dtype=jnp.float32) * s, 'Ws1': jax.random.normal(ks[4], (D, 2 * HS), dtype=jnp.float32) * s, 'Ws2': jax.random.normal(ks[5], (HS, D), dtype=jnp.float32) * s}
    _L3_ffn_all = _L3_ffn_setup()
    _L3_ffn_in = {k: v for k, v in _L3_ffn_all.items() if k in ('Wg', 'W1', 'W2', 'Ws1', 'Ws2')}
    del _L3_ffn_all
    return {'x': x, 'ctx_1024': ctx_1024, 'mask_1x1xSxS2_if1': mask_1x1xSxS2_if1, 'mask_Bx1xSxS2_ik1': mask_Bx1xSxS2_ik1, 'mask_BxS2_bk0': mask_BxS2_bk0, 'L0_attn_ln_gamma': _L0_attn_in['ln_gamma'], 'L0_attn_ln_beta': _L0_attn_in['ln_beta'], 'L0_attn_W_qkv': _L0_attn_in['W_qkv'], 'L0_attn_b_qkv': _L0_attn_in['b_qkv'], 'L0_attn_W_proj': _L0_attn_in['W_proj'], 'L0_attn_b_proj': _L0_attn_in['b_proj'], 'L0_xattn_conv_w': _L0_xattn_in['conv_w'], 'L0_xattn_conv_b': _L0_xattn_in['conv_b'], 'L0_ffn_keys': _L0_ffn_in['keys'], 'L0_ffn_w1': _L0_ffn_in['w1'], 'L0_ffn_b1': _L0_ffn_in['b1'], 'L0_ffn_w2': _L0_ffn_in['w2'], 'L0_ffn_b2': _L0_ffn_in['b2'], 'L0_ffn_rw': _L0_ffn_in['rw'], 'L0_ffn_rb': _L0_ffn_in['rb'], 'L1_attn_gamma': _L1_attn_in['gamma'], 'L1_attn_Wq': _L1_attn_in['Wq'], 'L1_attn_Wkv': _L1_attn_in['Wkv'], 'L1_attn_W_bilinear': _L1_attn_in['W_bilinear'], 'L1_attn_Wo': _L1_attn_in['Wo'], 'L1_xattn_Wq': _L1_xattn_in['Wq'], 'L1_xattn_bq': _L1_xattn_in['bq'], 'L1_xattn_Wk': _L1_xattn_in['Wk'], 'L1_xattn_bk': _L1_xattn_in['bk'], 'L1_xattn_Wv': _L1_xattn_in['Wv'], 'L1_xattn_bv': _L1_xattn_in['bv'], 'L1_xattn_Wo': _L1_xattn_in['Wo'], 'L1_xattn_bo': _L1_xattn_in['bo'], 'L1_ffn_packed_weight': _L1_ffn_in['packed_weight'], 'L1_ffn_weight_scale': _L1_ffn_in['weight_scale'], 'L1_ffn_bias': _L1_ffn_in['bias'], 'L2_attn_qw': _L2_attn_in['qw'], 'L2_attn_kw': _L2_attn_in['kw'], 'L2_attn_vw': _L2_attn_in['vw'], 'L2_attn_ow': _L2_attn_in['ow'], 'L2_xattn_Wq': _L2_xattn_in['Wq'], 'L2_xattn_Wk': _L2_xattn_in['Wk'], 'L2_xattn_Wv': _L2_xattn_in['Wv'], 'L2_xattn_Wo': _L2_xattn_in['Wo'], 'L2_xattn_bo': _L2_xattn_in['bo'], 'L2_ffn_router_w': _L2_ffn_in['router_w'], 'L2_ffn_router_b': _L2_ffn_in['router_b'], 'L2_ffn_ln_g': _L2_ffn_in['ln_g'], 'L2_ffn_ln_b': _L2_ffn_in['ln_b'], 'L2_ffn_w1': _L2_ffn_in['w1'], 'L2_ffn_b1': _L2_ffn_in['b1'], 'L2_ffn_w2': _L2_ffn_in['w2'], 'L2_ffn_b2': _L2_ffn_in['b2'], 'L3_attn_w_qkv': _L3_attn_in['w_qkv'], 'L3_attn_b_qkv': _L3_attn_in['b_qkv'], 'L3_attn_w_fc': _L3_attn_in['w_fc'], 'L3_attn_b_fc': _L3_attn_in['b_fc'], 'L3_xattn_Wq': _L3_xattn_in['Wq'], 'L3_xattn_bq': _L3_xattn_in['bq'], 'L3_xattn_Wk': _L3_xattn_in['Wk'], 'L3_xattn_bk': _L3_xattn_in['bk'], 'L3_xattn_Wv': _L3_xattn_in['Wv'], 'L3_xattn_bv': _L3_xattn_in['bv'], 'L3_xattn_Wo': _L3_xattn_in['Wo'], 'L3_xattn_bo': _L3_xattn_in['bo'], 'L3_ffn_Wg': _L3_ffn_in['Wg'], 'L3_ffn_W1': _L3_ffn_in['W1'], 'L3_ffn_W2': _L3_ffn_in['W2'], 'L3_ffn_Ws1': _L3_ffn_in['Ws1'], 'L3_ffn_Ws2': _L3_ffn_in['Ws2']}

def reference(x, ctx_1024, mask_1x1xSxS2_if1, mask_Bx1xSxS2_ik1, mask_BxS2_bk0, L0_attn_ln_gamma, L0_attn_ln_beta, L0_attn_W_qkv, L0_attn_b_qkv, L0_attn_W_proj, L0_attn_b_proj, L0_xattn_conv_w, L0_xattn_conv_b, L0_ffn_keys, L0_ffn_w1, L0_ffn_b1, L0_ffn_w2, L0_ffn_b2, L0_ffn_rw, L0_ffn_rb, L1_attn_gamma, L1_attn_Wq, L1_attn_Wkv, L1_attn_W_bilinear, L1_attn_Wo, L1_xattn_Wq, L1_xattn_bq, L1_xattn_Wk, L1_xattn_bk, L1_xattn_Wv, L1_xattn_bv, L1_xattn_Wo, L1_xattn_bo, L1_ffn_packed_weight, L1_ffn_weight_scale, L1_ffn_bias, L2_attn_qw, L2_attn_kw, L2_attn_vw, L2_attn_ow, L2_xattn_Wq, L2_xattn_Wk, L2_xattn_Wv, L2_xattn_Wo, L2_xattn_bo, L2_ffn_router_w, L2_ffn_router_b, L2_ffn_ln_g, L2_ffn_ln_b, L2_ffn_w1, L2_ffn_b1, L2_ffn_w2, L2_ffn_b2, L3_attn_w_qkv, L3_attn_b_qkv, L3_attn_w_fc, L3_attn_b_fc, L3_xattn_Wq, L3_xattn_bq, L3_xattn_Wk, L3_xattn_bk, L3_xattn_Wv, L3_xattn_bv, L3_xattn_Wo, L3_xattn_bo, L3_ffn_Wg, L3_ffn_W1, L3_ffn_W2, L3_ffn_Ws1, L3_ffn_Ws2):
    import jax
    import jax.numpy as jnp

    def _L0_attn_ref(x, ln_gamma, ln_beta, W_qkv, b_qkv, W_proj, b_proj):
        import jax, jax.numpy as jnp
        import numpy as np
        D_MODEL = 128
        NHEAD = 16
        HEAD_DIM = D_MODEL // NHEAD
        SCALE = HEAD_DIM ** (-0.5)
        EPS_LN = 1e-05
        B, T, D = x.shape
        h, dh = (NHEAD, HEAD_DIM)
        mu = jnp.mean(x, axis=-1, keepdims=True)
        var = jnp.mean(jnp.square(x - mu), axis=-1, keepdims=True)
        x_n = (x - mu) * jax.lax.rsqrt(var + EPS_LN) * ln_gamma + ln_beta
        qkv = x_n @ W_qkv + b_qkv
        q, k, v = jnp.split(qkv, 3, axis=-1)
        q = q.reshape(B, T, h, dh).transpose(0, 2, 1, 3)
        k = k.reshape(B, T, h, dh).transpose(0, 2, 1, 3)
        v = v.reshape(B, T, h, dh).transpose(0, 2, 1, 3)
        scores = jnp.einsum('bhqd,bhkd->bhqk', q, k) * SCALE
        scores = scores - jnp.max(scores, axis=-1, keepdims=True)
        attn = jnp.exp(scores)
        attn = attn / jnp.maximum(jnp.sum(attn, axis=-1, keepdims=True), 1e-12)
        ctx = jnp.einsum('bhqk,bhkd->bhqd', attn, v)
        ctx = ctx.transpose(0, 2, 1, 3).reshape(B, T, D)
        return ctx @ W_proj + b_proj

    def _L0_xattn_ref(inputs, memory, conv_w, conv_b, conv_units, short_units, rate):
        import jax, jax.numpy as jnp
        import numpy as np
        from jax import lax
        B, T, F = (32, 128, 128)
        CONV_UNITS = 256
        SHORT_UNITS = 256
        RATE = 4
        b, t, f = inputs.shape
        conv_mem = memory[:, :conv_units]
        short_mem = memory[:, -short_units:]
        old_memory = short_mem[:, :t]
        compression = lax.conv_general_dilated(old_memory, conv_w, window_strides=(rate,), padding='VALID', dimension_numbers=('NWC', 'WIO', 'NWC')) + conv_b
        tc = compression.shape[1]
        new_short = jnp.concatenate([short_mem[:, t:], inputs], axis=1)
        new_conv = jnp.concatenate([conv_mem[:, tc:], compression], axis=1)
        return jnp.concatenate([new_conv, new_short], axis=1)

    def _L0_ffn_ref(x, keys, w1, b1, w2, b2, rw, rb):
        import jax, jax.numpy as jnp
        import numpy as np
        B, L, D = (4, 64, 128)
        E, TOP_K = (16, 4)
        F = 4 * D
        diff = x[:, :, None, :] - keys
        dist2 = jnp.sum(diff * diff, axis=-1)
        logits = -dist2 + jnp.einsum('bld,ed->ble', x, rw) + rb
        topv, topi = jax.lax.top_k(logits, TOP_K)
        w = jax.nn.softmax(topv, axis=-1)
        hidden = jax.nn.gelu(jnp.einsum('bld,efd->blef', x, w1) + b1, approximate=False)
        exp_out = jnp.einsum('blef,edf->bled', hidden, w2) + b2
        sel = jnp.take_along_axis(exp_out, topi[..., None], axis=2)
        fused = jnp.sum(w[..., None] * sel, axis=2)
        return fused

    def _L1_attn_ref(x, gamma, Wq, Wkv, W_bilinear, Wo):
        import jax, jax.numpy as jnp
        import numpy as np
        DIM = 128
        HEADS = 16
        DHEAD = 64
        INNER = HEADS * DHEAD
        B, N = (1, 256)
        ROPE_BASE = 10000.0
        LN_EPS = 1e-05

        def rope_tables(seq_len, d, dtype):
            theta = 1.0 / ROPE_BASE ** (jnp.arange(0, d, 2, dtype=dtype) / d)
            pos = jnp.arange(seq_len, dtype=dtype)
            freqs = pos[:, None] * theta[None, :]
            emb = jnp.concatenate([freqs, freqs], axis=-1)
            return (jnp.cos(emb), jnp.sin(emb))

        def apply_rotary(x, cos, sin):
            x1, x2 = (x[..., ::2], x[..., 1::2])
            x_rot = jnp.stack([-x2, x1], axis=-1).reshape(x.shape)
            return x * cos + x_rot * sin
        b, n, _ = x.shape
        mu = jnp.mean(x, axis=-1, keepdims=True)
        var = jnp.var(x, axis=-1, keepdims=True)
        xn = (x - mu) / jnp.sqrt(var + LN_EPS) * gamma
        q = xn @ Wq
        kv = xn @ Wkv
        k, v = jnp.split(kv, 2, axis=-1)

        def to_heads(t):
            return t.reshape(b, n, HEADS, DHEAD).transpose(0, 2, 1, 3)
        q, k, v = map(to_heads, (q, k, v))
        cos, sin = rope_tables(n, DHEAD, x.dtype)
        q = apply_rotary(q, cos, sin) * DHEAD ** (-0.5)
        k = apply_rotary(k, cos, sin)
        kt = jnp.einsum('bhnd,hde->bhne', k, W_bilinear)
        sim = jnp.einsum('bhid,bhjd->bhij', q, kt)
        attn = jax.nn.softmax(sim, axis=-1)
        out = jnp.einsum('bhij,bhjd->bhid', attn, v)
        out = out.transpose(0, 2, 1, 3).reshape(b, n, INNER)
        return out @ Wo

    def _L1_xattn_ref(query, key, value, mask, Wq, bq, Wk, bk, Wv, bv, Wo, bo):
        import jax, jax.numpy as jnp
        import numpy as np
        import math
        D_MODEL = 128
        N_HEADS = 16
        HEAD_DIM = D_MODEL // N_HEADS
        BATCH = 2
        SEQ = 512
        B, S, D = query.shape
        scale = 1.0 / math.sqrt(HEAD_DIM)

        def proj_split(x, W, b):
            y = x @ W.T + b
            return y.reshape(B, -1, N_HEADS, HEAD_DIM).transpose(0, 2, 1, 3)
        q = proj_split(query, Wq, bq)
        k = proj_split(key, Wk, bk)
        v = proj_split(value, Wv, bv)
        scores = jnp.einsum('bhqd,bhkd->bhqk', q, k) * scale
        scores = jnp.where(mask == 0, jnp.float32(-1000000000.0), scores)
        probs = jax.nn.softmax(scores, axis=-1)
        attn = jnp.einsum('bhqk,bhkd->bhqd', probs, v)
        out = attn.transpose(0, 2, 1, 3).reshape(B, S, D)
        return out @ Wo.T + bo

    def _L1_ffn_ref(x, packed_weight, weight_scale, bias):
        import jax, jax.numpy as jnp
        import numpy as np
        IN_F = 128
        OUT_F = 128
        B, S = (8, 512)

        def _pack_ternary(tern):
            enc = (tern + 1.0).astype(jnp.int32).reshape(-1)
            return (enc[0::4] | enc[1::4] << 2 | enc[2::4] << 4 | enc[3::4] << 6).astype(jnp.int32)
        n = OUT_F * IN_F
        shifts = jnp.array([0, 2, 4, 6], dtype=jnp.int32)
        enc = (packed_weight[None, :] >> shifts[:, None] & 3).reshape(-1)[:n]
        w = (enc.astype(jnp.float32) - 1.0).reshape(OUT_F, IN_F) * weight_scale
        act_scale = 127.0 / jnp.maximum(jnp.max(jnp.abs(x), axis=-1, keepdims=True), 1e-05)
        x_dq = jnp.clip(jnp.round(x * act_scale), -128.0, 127.0) / act_scale
        return jnp.einsum('bsi,oi->bso', x_dq, w) + bias

    def _L2_attn_ref(x, qw, kw, vw, ow):
        import jax, jax.numpy as jnp
        import numpy as np
        D_MODEL, N_HEADS, BATCH, SEQ = (128, 16, 2, 256)

        def get_freqs(seq, n_dim):
            inv_freq = 1.0 / 10000.0 ** (jnp.arange(0, n_dim, 2, dtype=jnp.float32) / n_dim)
            pos = jnp.arange(seq, dtype=jnp.float32)
            return pos[:, None] * inv_freq[None, :]

        def rope(x, freq):
            cos = jnp.cos(freq)[None, :, None, :]
            sin = jnp.sin(freq)[None, :, None, :]
            x1, x2 = (x[..., ::2], x[..., 1::2])
            r1 = x1 * cos - x2 * sin
            r2 = x1 * sin + x2 * cos
            return jnp.stack([r1, r2], axis=-1).reshape(x.shape)
        batch, seq, dim = x.shape
        n_heads = N_HEADS
        n_dim = dim // n_heads
        Q = (x @ qw).astype(jnp.float32).reshape(batch, seq, n_heads, n_dim)
        K = (x @ kw).astype(jnp.float32).reshape(batch, seq, n_heads, n_dim)
        V = (x @ vw).astype(jnp.float32).reshape(batch, seq, n_heads, n_dim)
        freq = get_freqs(seq, n_dim)
        Q = rope(Q, freq)
        K = rope(K, freq)
        Q = jnp.transpose(Q, (0, 2, 1, 3))
        K = jnp.transpose(K, (0, 2, 1, 3))
        V = jnp.transpose(V, (0, 2, 1, 3))
        scale = jnp.sqrt(jnp.float32(n_dim))
        score = jnp.einsum('bhqd,bhkd->bhqk', Q, K) / scale
        causal = jnp.tril(jnp.ones((1, 1, seq, seq), dtype=jnp.float32))
        score = score - 10000000000.0 * (1.0 - causal)
        score = score - jnp.max(score, axis=-1, keepdims=True)
        weights = jax.nn.softmax(score, axis=-1)
        attn = jnp.einsum('bhqk,bhkd->bhqd', weights, V)
        merged = jnp.transpose(attn, (0, 2, 1, 3)).reshape(batch, seq, dim)
        return (merged @ ow).astype(x.dtype)

    def _L2_xattn_ref(queries, keys, values, mask, Wq, Wk, Wv, Wo, bo):
        import jax, jax.numpy as jnp
        import numpy as np
        EMBED = 128
        HEADS = 16
        HEAD_DIM = EMBED // HEADS
        N, Qlen, _ = queries.shape
        Klen = keys.shape[1]
        q = (queries @ Wq.T).reshape(N, Qlen, HEADS, HEAD_DIM)
        k = (keys @ Wk.T).reshape(N, Klen, HEADS, HEAD_DIM)
        v = (values @ Wv.T).reshape(N, Klen, HEADS, HEAD_DIM)
        energy = jnp.einsum('nqhd,nkhd->nhqk', q, k)
        energy = jnp.where(mask == 0, jnp.float32(-1e+20), energy)
        attention = jax.nn.softmax(energy / jnp.sqrt(jnp.float32(EMBED)), axis=3)
        out = jnp.einsum('nhqk,nkhd->nqhd', attention, v).reshape(N, Qlen, EMBED)
        return out @ Wo.T + bo

    def _L2_ffn_ref(hidden_states, router_w, router_b, ln_g, ln_b, w1, b1, w2, b2):
        import jax, jax.numpy as jnp
        import numpy as np
        L, E, H, F, K = (4, 4, 128, 512, 2)
        B, S = (4, 256)
        EPS = 1e-05

        def _moe_layer(x, rw, rb, g, b, w1, b1, w2, b2):
            logits = jnp.einsum('bsh,he->bse', x, rw) + rb
            probs = jax.nn.softmax(logits, axis=-1)
            vals, idx = jax.lax.top_k(probs, K)
            vals = vals / vals.sum(axis=-1, keepdims=True)
            mu = x.mean(axis=-1, keepdims=True)
            xc = x - mu
            xhat = xc * jax.lax.rsqrt((xc * xc).mean(axis=-1, keepdims=True) + EPS)
            xe = xhat[None] * g[:, None, None, :] + b[:, None, None, :]
            h = jax.nn.gelu(jnp.einsum('ebsh,ehf->ebsf', xe, w1) + b1[:, None, None, :], approximate=False)
            y = jnp.einsum('ebsf,efh->ebsh', h, w2) + b2[:, None, None, :]
            expert_out = x[None] + y
            comb = jnp.einsum('bsk,bske->bse', vals, jax.nn.one_hot(idx, E, dtype=x.dtype))
            return jnp.einsum('bse,ebsh->bsh', comb, expert_out)
        x = hidden_states
        for l in range(L):
            x = _moe_layer(x, router_w[l], router_b[l], ln_g[l], ln_b[l], w1[l], b1[l], w2[l], b2[l])
        return x

    def _L3_attn_ref(x, w_qkv, b_qkv, w_fc, b_fc):
        import jax, jax.numpy as jnp
        import numpy as np
        D_MODEL = 128
        NUM_HEADS = 16
        DEPTH = D_MODEL // NUM_HEADS
        B, T = (2, 256)

        def _rope(x):
            H = x.shape[1]
            D = x.shape[-1]
            inv_freq = 1.0 / 10000.0 ** (jnp.arange(0, D, 2, dtype=jnp.float32) / D)
            freqs = jnp.arange(H, dtype=jnp.float32)[:, None] * inv_freq[None, :]
            sin = jnp.sin(freqs)[:, None, :]
            cos = jnp.cos(freqs)[:, None, :]
            x1 = x[..., ::2]
            x2 = x[..., 1::2]
            rot = jnp.stack([x1 * cos - x2 * sin, x1 * sin + x2 * cos], axis=-1)
            return rot.reshape(x.shape)
        Bs, Ts, C = x.shape
        H, D = (NUM_HEADS, DEPTH)
        qkv = x @ w_qkv + b_qkv
        qkv = qkv.reshape(Bs, Ts, 3, H, D)
        qkv = jnp.transpose(qkv, (2, 0, 3, 1, 4))
        q, k, v = (qkv[0], qkv[1], qkv[2])
        q = _rope(q)
        k = _rope(k)
        scores = jnp.einsum('bhtd,bhsd->bhts', q, k) / jnp.sqrt(jnp.float32(D))
        attn = jax.nn.softmax(scores, axis=-1)
        out = jnp.einsum('bhts,bhsd->bhtd', attn, v)
        out = jnp.transpose(out, (0, 2, 1, 3)).reshape(Bs, Ts, C)
        return out @ w_fc + b_fc

    def _L3_xattn_ref(query, key_value, key_mask, Wq, bq, Wk, bk, Wv, bv, Wo, bo):
        import jax, jax.numpy as jnp
        import numpy as np
        B, LQ, LKV = (8, 128, 256)
        QDIM, KDIM, HID = (128, 128, 128)
        Q = query @ Wq + bq
        K = key_value @ Wk + bk
        V = key_value @ Wv + bv
        hid = Q.shape[-1]
        scores = jnp.einsum('bqh,bkh->bqk', Q, K) / jnp.sqrt(jnp.float32(hid))
        scores = jnp.where(key_mask[:, None, :], scores, jnp.float32(-1000000000.0))
        attn = jax.nn.softmax(scores, axis=-1)
        context = jnp.einsum('bqk,bkh->bqh', attn, V)
        return context @ Wo + bo

    def _L3_ffn_ref(x, Wg, W1, W2, Ws1, Ws2):
        import jax, jax.numpy as jnp
        import numpy as np
        B, S, D = (2, 128, 128)
        H = 64
        E = 16
        K = 2
        HS = 2 * H
        ROUTE_SCALE = 1.0

        def _gated_mlp_act(y):
            u, g = jnp.split(y, 2, axis=-1)
            return u * jax.nn.silu(g)
        x_shape = x.shape
        xf = x.reshape(-1, D)
        scores = jax.nn.softmax(xf @ Wg.T, axis=-1)
        wk, idx = jax.lax.top_k(scores, K)
        wk = wk * ROUTE_SCALE
        cw = jnp.sum(jax.nn.one_hot(idx, E, dtype=xf.dtype) * wk[..., None], axis=1)
        h = _gated_mlp_act(jnp.einsum('td,edh->teh', xf, W1))
        z = jnp.einsum('te,teh,ehd->td', cw, h, W2)
        ys = _gated_mlp_act(xf @ Ws1) @ Ws2
        return (z + ys).reshape(x_shape)
    x = _layernorm(x + _L0_attn_ref(x, L0_attn_ln_gamma, L0_attn_ln_beta, L0_attn_W_qkv, L0_attn_b_qkv, L0_attn_W_proj, L0_attn_b_proj), axis=-1)
    x = _layernorm(x + _L0_xattn_ref(ctx_1024, x, L0_xattn_conv_w, L0_xattn_conv_b, 256, 256, 4), axis=-1)
    x = _layernorm(x + _L0_ffn_ref(x, L0_ffn_keys, L0_ffn_w1, L0_ffn_b1, L0_ffn_w2, L0_ffn_b2, L0_ffn_rw, L0_ffn_rb), axis=-1)
    x = _layernorm(x + _L1_attn_ref(x, L1_attn_gamma, L1_attn_Wq, L1_attn_Wkv, L1_attn_W_bilinear, L1_attn_Wo), axis=-1)
    x = _layernorm(x + _L1_xattn_ref(x, ctx_1024, ctx_1024, mask_1x1xSxS2_if1, L1_xattn_Wq, L1_xattn_bq, L1_xattn_Wk, L1_xattn_bk, L1_xattn_Wv, L1_xattn_bv, L1_xattn_Wo, L1_xattn_bo), axis=-1)
    x = _layernorm(x + _L1_ffn_ref(x, L1_ffn_packed_weight, L1_ffn_weight_scale, L1_ffn_bias), axis=-1)
    x = _layernorm(x + _L2_attn_ref(x, L2_attn_qw, L2_attn_kw, L2_attn_vw, L2_attn_ow), axis=-1)
    x = _layernorm(x + _L2_xattn_ref(x, ctx_1024, ctx_1024, mask_Bx1xSxS2_ik1, L2_xattn_Wq, L2_xattn_Wk, L2_xattn_Wv, L2_xattn_Wo, L2_xattn_bo), axis=-1)
    x = _layernorm(x + _L2_ffn_ref(x, L2_ffn_router_w, L2_ffn_router_b, L2_ffn_ln_g, L2_ffn_ln_b, L2_ffn_w1, L2_ffn_b1, L2_ffn_w2, L2_ffn_b2), axis=-1)
    x = _layernorm(x + _L3_attn_ref(x, L3_attn_w_qkv, L3_attn_b_qkv, L3_attn_w_fc, L3_attn_b_fc), axis=-1)
    x = _layernorm(x + _L3_xattn_ref(x, ctx_1024, mask_BxS2_bk0, L3_xattn_Wq, L3_xattn_bq, L3_xattn_Wk, L3_xattn_bk, L3_xattn_Wv, L3_xattn_bv, L3_xattn_Wo, L3_xattn_bo), axis=-1)
    x = _layernorm(x + _L3_ffn_ref(x, L3_ffn_Wg, L3_ffn_W1, L3_ffn_W2, L3_ffn_Ws1, L3_ffn_Ws2), axis=-1)
    return x

_drawn_inputs = setup_inputs


def setup_inputs(seed=0):
    import zlib

    import numpy as np

    out = dict(_drawn_inputs(seed))
    spreads = {'L0_attn_ln_gamma': (1.0, 0.6),
     'L0_attn_ln_beta': (0.0, 0.1),
     'L0_xattn_conv_b': (0.0, 0.461),
     'L0_ffn_b1': (0.0, 0.362),
     'L0_ffn_b2': (0.0, 0.1),
     'L0_ffn_rb': (0.0, 0.8),
     'L1_attn_gamma': (1.0, 0.6),
     'L1_ffn_bias': (0.0, 0.1),
     'L2_ffn_router_b': (0.0, 0.1),
     'L2_ffn_ln_g': (1.0, 0.6),
     'L2_ffn_ln_b': (0.0, 0.8),
     'L2_ffn_b1': (0.0, 0.411),
     'L2_ffn_b2': (0.0, 0.1)}
    factors = {'L0_ffn_rw': 8.0,
     'L1_attn_Wq': 8.0,
     'L1_attn_Wkv': 3.297,
     'L1_attn_W_bilinear': 8.0,
     'L1_attn_Wo': 3.569,
     'L1_xattn_Wq': 8.0,
     'L1_xattn_bq': 33.42,
     'L1_xattn_Wk': 8.0,
     'L1_xattn_bk': 64.0,
     'L1_xattn_bv': 8.0,
     'L2_attn_qw': 8.0,
     'L2_attn_kw': 8.0,
     'L2_attn_vw': 8.0,
     'L2_attn_ow': 8.0,
     'L3_xattn_bq': 8.0,
     'L3_xattn_bk': 64.0,
     'L3_ffn_Wg': 8.0,
     'L3_ffn_W1': 8.0,
     'L3_ffn_W2': 8.0,
     'L3_ffn_Ws1': 8.0,
     'L3_ffn_Ws2': 8.0}
    for name, (base, spread) in spreads.items():
        noise = np.random.default_rng([zlib.crc32(name.encode()), seed]).standard_normal(out[name].shape)
        drawn = base * np.exp(spread * noise) if base else spread * noise
        out[name] = jnp.asarray(drawn.astype(out[name].dtype))
    for name, factor in factors.items():
        out[name] = (out[name] * factor).astype(out[name].dtype)
    return out
```

```python
from contextlib import ExitStack

import concourse.bass as bass
from concourse import mybir
import numpy as np

F32 = mybir.dt.float32
F32R = mybir.dt.float32r
BF16 = mybir.dt.bfloat16
I32 = mybir.dt.int32
U8 = mybir.dt.uint8
ACT = mybir.ActivationFunctionType
ALU = mybir.AluOpType
X_AXIS = mybir.AxisListType.X

P = 128
B, S, D = 2, 512, 128
T = B * S
NT = T // P
QT = S // P
SC = 77
H, DH = 16, 8
WH = 64
HF = 512
EPS = 1e-5
HUGE = 3.0e38


WEIGHTS = [
    ("l0_qkv", 384), ("l0_proj", 128), ("l0_conv", 512), ("l0_keys", 16), ("l0_rw", 16), ("l0_b2", 128),
    ("l1x", 512), ("l2_attn", 512), ("l2x", 512), ("l2_rw", 16), ("l2_b2", 512), ("l3x", 512),
]
WEIGHTS_1 = [
    ("l1_wq", 1024), ("l1_wk", 1024), ("l1_wv", 1024), ("l1_bil", 1024), ("l1_wo", 1024),
]
WEIGHTS_3 = [
    ("l3_qkv", 384), ("l3_fc", 128), ("l3_wg", 16), ("l3_w1", 2048), ("l3_w2", 1024),
    ("l3_ws1", 256), ("l3_ws2", 128),
]
COLS = [
    ("l0_g", 1), ("l0_b", 1), ("l0_bqkv", 3), ("conv_b", 1), ("l0_b1", 64), ("l1_g", 1), ("l1x_bq", 1),
    ("l1x_bk", 1), ("l2_g", 16), ("l2_b", 16), ("l2_b1", 64), ("l3_bqkv", 3), ("l3x_bq", 1), ("l3x_bk", 1),
]
ROWS = [
    ("l0_bv", 128), ("l0_bproj", 128), ("l0_rb", 16), ("l1x_bv", 128), ("l1x_bo", 128), ("l1f_bias", 128),
    ("l1f_scale", 1), ("l2x_bo", 128), ("l2_rb", 16), ("l3_bv", 128), ("l3_bfc", 128), ("l3x_bv", 128),
    ("l3x_bo", 128),
]
CONSTS = [
    ("ident", 128), ("rot", 128), ("headmask", 16), ("sel", 16), ("marks", 4), ("stack", 4), ("causal_s", 128),
    ("causal_st", 128), ("l1_cos", 512), ("l1_sin", 512), ("l2_cos", 512), ("l2_sin", 512), ("l3_cos", 1),
    ("l3_sin", 1),
]


def offsets(parts):
    at, out = 0, {}
    for name, n in parts:
        out[name] = (at, n)
        at += n
    return out, at


W_AT, W_N = offsets(WEIGHTS)
W1_AT, W1_N = offsets(WEIGHTS_1)
W3_AT, W3_N = offsets(WEIGHTS_3)
C_AT, C_N = offsets(COLS)
R_AT, R_N = offsets(ROWS)
K_AT, K_N = offsets(CONSTS)

CAUSAL = -1.0e10


def shape_constants():
    k = np.zeros((P, K_N), np.float32)

    def put(name, a):
        at, n = K_AT[name]
        k[:, at:at + n] = a

    put("ident", np.eye(P))
    rot = np.zeros((P, P))
    for i in range(0, P, 2):
        rot[i + 1, i] = -1.0
        rot[i, i + 1] = 1.0
    put("rot", rot)
    feature = np.arange(P)
    put("headmask", feature[:, None] // DH == np.arange(H)[None, :])
    row = np.arange(P)[:, None]
    put("sel", (row == np.arange(16)) | (row == 32 + np.arange(16)))
    put("marks", (row == 96 + np.arange(4)) | (row == 100 + np.arange(4)))
    put("stack", (row % 32 // DH == np.arange(4)) & (row < 96))
    token = np.arange(P)
    put("causal_s", np.where(token[None, :] > token[:, None], CAUSAL * np.sqrt(DH), 0.0))
    put("causal_st", np.where(token[:, None] > token[None, :], CAUSAL * np.sqrt(DH), 0.0))
    pos = np.arange(S, dtype=np.float32)
    theta = (1.0 / np.float32(10000.0) ** (np.arange(0, WH, 2, dtype=np.float32) / np.float32(WH))).astype(np.float32)
    freq = (pos[:, None] * theta[None, :]).astype(np.float32)
    emb = np.concatenate([freq, freq], -1).T
    put("l1_cos", np.tile(np.cos(emb), (2, 1)))
    put("l1_sin", np.tile(np.sin(emb), (2, 1)))
    inv = (1.0 / np.float32(10000.0) ** (np.arange(0, DH, 2, dtype=np.float32) / np.float32(DH))).astype(np.float32)
    f2 = np.repeat((pos[:, None] * inv[None, :]).astype(np.float32).T, 2, axis=0)
    put("l2_cos", np.tile(np.cos(f2), (H, 1)))
    put("l2_sin", np.tile(np.sin(f2), (H, 1)))
    f3 = np.repeat(np.arange(H, dtype=np.float32)[:, None] * inv[None, :], 2, axis=1).reshape(P, 1)
    put("l3_cos", np.cos(f3))
    put("l3_sin", np.sin(f3))
    return k


class Signal:

    def __init__(self, nc, name):
        self.sem = nc.alloc_semaphore(name)
        self.base = 0
        self.total = 0

    def up(self, n=1):
        self.total += n
        return self.sem, n

    def at(self, n):
        return self.sem, self.base + n


class Signals:
    def __init__(self, nc):
        self.nc, self.by_name = nc, {}

    def __call__(self, name):
        if name not in self.by_name:
            self.by_name[name] = Signal(self.nc, name)
        return self.by_name[name]

    def settle(self):
        for s in self.by_name.values():
            s.base = s.total


def build(nc, x_in, ctx_in, mask1_in, mask2_in, mask3_in, packed_in, const_in, weights_in, weights1_in, weights3_in, cols_in,
          rows_in,           l0_experts, l2_experts, out):
    ctx = ExitStack()

    def sb(name, shape, dt=F32):
        return ctx.enter_context(nc.sbuf_tensor(name, shape, dt))

    signals = Signals(nc)
    bank = ctx.enter_context(nc.psum_tensor("bank", [P, 8, HF], F32))

    consts = sb("consts", [P, K_N])
    weights = sb("weights", [P, W_N])
    weights13 = sb("weights13", [P, max(W1_N, W3_N)])
    cols = sb("cols", [P, C_N])
    rows = sb("rows", [P, R_N])

    def K(name):
        at, n = K_AT[name]
        return consts[:, at:at + n]

    def W(name, a=0, b=None):
        table, tile = (W_AT, weights) if name in W_AT else (W1_AT if name in W1_AT else W3_AT, weights13)
        at, n = table[name]
        return tile[:, at + a:at + (n if b is None else b)]

    def C(name, i=0):
        at, _ = C_AT[name]
        return cols[:, at + i:at + i + 1]

    def R(name, a=0, b=None):
        at, n = R_AT[name]
        return rows[:, at + a:at + (n if b is None else b)]

    ident = K("ident")
    x_tok = sb("x_tok", [P, NT, D])
    x_feat = sb("x_feat", [P, T])
    hat_feat = sb("hat_feat", [P, T])
    y_feat = sb("y_feat", [P, T])
    stats = sb("stats", [P, NT, 6])
    moments = sb("moments", [P, NT, 2])
    rstd = sb("rstd", [P, NT])
    ctx_tok = sb("ctx_tok", [P, B, D])
    ctx_feat = sb("ctx_feat", [P, B * SC])
    identb = sb("identb", [P, P], BF16)
    causal_s = sb("causal_s", [P, P], BF16)
    causal_st = sb("causal_st", [P, P], BF16)
    ones32 = sb("ones32", [P, 32])
    q_feat = sb("q_feat", [P, T])
    k_feat = sb("k_feat", [P, T])
    operands = sb("operands", [P, 4, T])
    parts = {n: operands[:, i, :].bitcast(F32R) for i, n in enumerate(("q_hi", "q_lo", "k_hi", "k_lo"))}
    wide_q = operands[:, 0:2, :].rearrange("p b (a n) -> p b a n", a=2)
    wide_k = operands[:, 2:4, :].rearrange("p b (a n) -> p b a n", a=2)
    rot_tmp = y_feat
    res_tok = operands[:, 0, :].rearrange("p (t d) -> p t d", d=D)
    sum_tok = k_feat[:, :].rearrange("p (t d) -> p t d", d=D)
    KS = sb("KS", [P, 2, 4, HF], F32R)
    QM = sb("QM", [P, 2, HF], F32R)
    v_aug = sb("v_aug", [P, NT, H, 32])
    v_wide = v_aug[:, :, :, :].rearrange("p a b c -> p (a b c)")[:, 0:T].rearrange("p (t n) -> p t n", t=NT)
    probs = sb("probs", [P, 2, 4, HF])
    neg_max = sb("neg_max", [P, QT, 4])
    max_parts = sb("max_parts", [P, QT, 8], F32R)
    max_wide = sb("max_wide", [P, QT, P])
    o_feat = sb("o_feat", [P, HF])
    o_sums = sb("o_sums", [P, HF])
    o_tok = sb("o_tok", [P, B, QT, P])
    rsum = sb("rsum", [P, QT, 4])
    att_feat = sb("att_feat", [P, 8, T])
    NW = 4
    wring = probs[:, :, :, :].rearrange("p a b n -> p (a b n)").rearrange("p (w n) -> p w n", w=NW)
    sel = sb("sel", [P, 16, P], F32R)
    gate_parts = sb("gate_parts", [P, T], F32R)
    gate_rows = q_feat[0:16, :]
    gates = sb("gates", [P, NT, 16])
    gate_sum = sb("gate_sum", [P, NT])

    flat = att_feat[:, :, :].rearrange("p a n -> p (a n)")
    scratch = flat[:, 2 * T:2 * T + 7 * HF]
    x_keep = att_feat[:, 7, :].rearrange("p (t d) -> p t d", d=D)
    zeros = o_sums
    lg = sb("lg", [P, NT, 24])
    lg_rep = sb("lg_rep", [P, NT, 24])
    top8 = sb("top8", [P, NT, 8])
    top_in = sb("top_in", [P, NT, 8])
    picked = sb("picked", [P, NT, 16])
    small = sb("small", [P, NT, 4])

    loads = {n: nc.alloc_semaphore(n) for n in ("ld_const", "ld_x", "ld_w", "ld_w1", "ld_w3", "ld_ctx")}
    expert_loaded = [nc.alloc_semaphore(f"expert_loaded{i}") for i in range(NW)]
    expert_total = [0]

    done_q = signals("dve_step")

    def steps(eng, sig):
        def step(ins):
            ins.then_inc(*sig.up())
            eng.wait_ge(sig.sem, sig.total)
        return step

    with nc.Block() as block:
        t_done, init_done = signals("t_done"), signals("init_done")

        @block.sync
        def _(sp):
            sp.dma_start(consts[:, :], const_in).then_inc(loads["ld_const"], 16)
            sp.dma_start(x_tok[:, :, :], x_in.rearrange("b (t p) d -> p (b t) d", p=P)).then_inc(loads["ld_x"], 16)
            sp.dma_start(cols[:, :], cols_in).then_inc(loads["ld_const"], 16)
            sp.dma_start(rows[:, :], rows_in.partition_broadcast(P)).then_inc(loads["ld_const"], 16)
            sp.dma_start(ctx_tok[0:SC, :, :], ctx_in.rearrange("b s d -> s b d")).then_inc(loads["ld_ctx"], 16)
            sp.dma_start(weights[:, :], weights_in).then_inc(loads["ld_w"], 16)
            sp.dma_start(weights13[:, 0:W1_N], weights1_in).then_inc(loads["ld_w1"], 16)

        @block.gpsimd
        def _(pool):
            pool.memset(KS[:, :, :, :].bitcast(F32), 0.0).then_inc(*init_done.up())
            pool.memset(QM[:, :, :].bitcast(F32), 0.0)
            pool.memset(v_aug[:, :, :, :], 0.0).then_inc(*init_done.up())
            pool.memset(max_wide[:, :, :], 0.0)
            pool.memset(ones32[:, :], 1.0)
            pool.memset(gate_parts[:, :].bitcast(F32), 0.0)
            pool.memset(zeros[:, :], 0.0).then_inc(*init_done.up())
            pool.wait_ge(*init_done.at(3))
            pool.memset(v_aug[:, :, :, DH:DH + 1], 1.0)

        @block.vector
        def _(dve):
            dve.wait_ge(loads["ld_const"], 48)
            dve.tensor_copy(identb[:, :], ident)
            dve.tensor_copy(causal_s[:, :], K("causal_s"))
            dve.tensor_copy(causal_st[:, :], K("causal_st"))
            dve.wait_ge(*init_done.at(3))
            for j in range(4):
                for s in range(2):
                    dve.tensor_scalar(KS[96:128, s, j, :], zeros[96:128, :], K("marks")[96:128, j:j + 1], None,
                                      ALU.add)
            for e in range(16):
                dve.tensor_scalar(sel[:, e, :], zeros[:, 0:P], K("sel")[:, e:e + 1], None, ALU.add)

        @block.tensor
        def _(pe):
            pe.wait_ge(loads["ld_const"], 48)
            pe.wait_ge(loads["ld_x"], 16)
            for hf in range(2):
                for q in range(QT):
                    ins = pe.transpose(bank[:, hf, q * P:(q + 1) * P], x_tok[:, hf * QT + q, :], ident)
                ins.then_inc(*t_done.up())
            pe.wait_ge(loads["ld_ctx"], 16)
            for b in range(B):
                ins = pe.transpose(bank[:, 2, b * SC:(b + 1) * SC], ctx_tok[0:SC, b, :], ident[0:SC, 0:SC])
            ins.then_inc(*t_done.up())

        @block.scalar
        def _(act):
            for hf in range(2):
                act.wait_ge(*t_done.at(hf + 1))
                act.copy(x_feat[:, hf * HF:(hf + 1) * HF], bank[:, hf, :])
            act.wait_ge(*t_done.at(3))
            act.copy(ctx_feat[:, :], bank[:, 2, 0:B * SC])
    signals.settle()

    def weights_here(pe):
        pe.wait_ge(loads["ld_w"], 16)
        for name in layer_loads:
            pe.wait_ge(loads[name], 16)

    layer_loads = []

    def norm_stage(terms=None, bias=None, residual_scale=None, norm=True, target="x", affine=None, store=False,
                   plus=None):
        y_done, res_done, std_in, std_out, tok_done, t_done = (
            signals(n) for n in ("y_done", "res_done", "std_in", "std_out", "tok_done", "t_done"))
        step_sig = signals("dve_step")
        dest = x_tok if target == "x" else sum_tok
        feat = x_feat if target == "x" else hat_feat
        stored = signals("stored")
        with nc.Block() as block:
            if terms is not None:
                @block.gpsimd
                def _(pool):
                    if bias is not None:
                        for hf in range(2):
                            half = slice(hf * QT, (hf + 1) * QT)
                            pool.tensor_tensor(res_tok[:, half, :], x_tok[:, half, :],
                                               bias.unsqueeze(1).broadcast_to([P, QT, D]), ALU.add
                                               ).then_inc(*res_done.up())

            @block.tensor
            def _(pe):
                weights_here(pe)
                if terms is not None:
                    for hf in range(2):
                        for q in range(QT):
                            t = hf * QT + q
                            for n, (operand, w) in enumerate(terms):
                                ins = pe.matmul(bank[:, hf, q * P:(q + 1) * P], operand[:, t * P:(t + 1) * P], w,
                                                start=(n == 0), stop=(n == len(terms) - 1))
                        ins.then_inc(*y_done.up())
                for hf in range(2):
                    pe.wait_ge(*tok_done.at(hf + 1))
                    for q in range(QT):
                        t = hf * QT + q
                        ins = pe.transpose(bank[:, 2 + hf, q * P:(q + 1) * P], dest[:, t, :], ident)
                    ins.then_inc(*t_done.up())

            @block.vector
            def _(dve):
                step = steps(dve, step_sig)
                for hf in range(2):
                    half = slice(hf * QT, (hf + 1) * QT)
                    y = bank[:, hf, :].rearrange("p (q d) -> p q d", d=D)
                    if terms is not None:
                        dve.wait_ge(*y_done.at(hf + 1))
                        into = sum_tok if norm else x_tok
                        if residual_scale is not None:
                            for q in range(QT):
                                ins = dve.scalar_tensor_tensor(out=into[:, hf * QT + q, :],
                                                               in0=x_tok[:, hf * QT + q, :],
                                                               scalar=residual_scale[:, hf * QT + q:hf * QT + q + 1],
                                                               in1=y[:, q, :], op0=ALU.mult, op1=ALU.add)
                        else:
                            if bias is not None:
                                dve.wait_ge(*res_done.at(hf + 1))
                            ins = dve.tensor_tensor(into[:, half, :], y,
                                                    (res_tok if bias is not None else x_tok)[:, half, :], ALU.add)
                        if not norm:
                            ins.then_inc(*tok_done.up())
                            continue
                        step(ins)
                        if plus is not None:
                            step(dve.tensor_tensor(into[:, half, :], into[:, half, :], plus[:, half, :], ALU.add))
                    source = sum_tok if terms is not None else x_tok
                    for q in range(QT):
                        ins = dve.bn_stats(stats[:, hf * QT + q, :], source[:, hf * QT + q, :])
                    step(ins)
                    for q in range(QT):
                        ins = dve.bn_aggr(moments[:, hf * QT + q, :], stats[:, hf * QT + q, :])
                    step(ins)
                    dve.tensor_scalar(rstd[:, half], moments[:, half, 1], EPS, None, ALU.add
                                      ).then_inc(*std_in.up())
                    dve.wait_ge(*std_out.at(hf + 1))
                    step(dve.reciprocal(rstd[:, half], rstd[:, half]))
                    for q in range(QT):
                        t = hf * QT + q
                        ins = dve.tensor_scalar(dest[:, t, :], source[:, t, :], moments[:, t, 0:1], rstd[:, t:t + 1],
                                                ALU.subtract, ALU.mult)
                    ins.then_inc(*tok_done.up())

            @block.scalar
            def _(act):
                if norm:
                    for hf in range(2):
                        act.wait_ge(*std_in.at(hf + 1))
                        act.activation(rstd[:, hf * QT:(hf + 1) * QT], rstd[:, hf * QT:(hf + 1) * QT],
                                       ACT.Sqrt).then_inc(*std_out.up())
                for hf in range(2):
                    act.wait_ge(*t_done.at(hf + 1))
                    o = feat[:, hf * HF:(hf + 1) * HF]
                    if affine is not None and affine[1] is not None:
                        act.activation(o, bank[:, 2 + hf, :], ACT.Identity, bias=affine[1], scale=affine[0])
                    elif affine is not None:
                        act.activation(o, bank[:, 2 + hf, :], ACT.Copy, scale=affine[0])
                    else:
                        act.copy(o, bank[:, 2 + hf, :])

            if store:
                @block.sync
                def _(sp):
                    view = out.rearrange("b (t p) d -> p (b t) d", p=P)
                    for hf in range(2):
                        sp.wait_ge(*tok_done.at(hf + 1))
                        half = slice(hf * QT, (hf + 1) * QT)
                        sp.dma_start(view[:, half, :], x_tok[:, half, :]).then_inc(*stored.up(16))
                    sp.wait_ge(*stored.at(32))
        signals.settle()

    def project_stage(source, wq, wk, wv, bq, bk, bv, cos=None, sin=None, bilinear=None, wide=False):
        proj, proj_used, raw, v_done, rotated, rot_used = (
            signals(n) for n in ("proj", "proj_used", "raw", "v_done", "rotated", "rot_used"))
        final, hi_done, bil_in = signals("final"), signals("hi_done"), signals("bil_in")
        step_sig = signals("dve_step")
        rotary = cos is not None
        ready = {}
        items = [(n, hf) for n in range(2) for hf in range(2)]
        feats = (q_feat, k_feat)

        with nc.Block() as block:
            @block.tensor
            def _(pe):
                weights_here(pe)
                for i, (n, hf) in enumerate(items):
                    pe.matmul(bank[:, i, :], (wq, wk)[n], source[:, hf * HF:(hf + 1) * HF], start=True,
                              stop=True).then_inc(*proj.up())
                for t in range(NT):
                    ins = pe.matmul(bank[:, 6 + t // QT, (t % QT) * P:(t % QT + 1) * P], source[:, t * P:(t + 1) * P],
                                    wv, start=True, stop=True)
                    if t % QT == QT - 1:
                        ins.then_inc(*v_done.up())
                if rotary:
                    for i, (n, hf) in enumerate(items):
                        pe.wait_ge(*raw.at(i + 1))
                        if i >= 2:
                            pe.wait_ge(*rot_used.at(i - 1))
                        pe.matmul(bank[:, 4 + i % 2, :], K("rot"), feats[n][:, hf * HF:(hf + 1) * HF], start=True,
                                  stop=True).then_inc(*rotated.up())
                if bilinear is not None:
                    for hf in range(2):
                        pe.wait_ge(*rot_used.at(3 + hf))
                        pe.matmul(bank[:, hf, :], bilinear, k_feat[:, hf * HF:(hf + 1) * HF], start=True,
                                  stop=True).then_inc(*bil_in.up())

            @block.scalar
            def _(act):
                for i, (n, hf) in enumerate(items):
                    act.wait_ge(*proj.at(i + 1))
                    bias = (bq, bk)[n]
                    o = feats[n][:, hf * HF:(hf + 1) * HF]
                    if bias is not None:
                        ins = act.activation(o, bank[:, i, :], ACT.Identity, bias=bias)
                    else:
                        ins = act.copy(o, bank[:, i, :])
                    ins.then_inc(*raw.up())
                if wide:
                    for hf in range(2):
                        act.wait_ge(*rot_used.at(1 + hf))
                        for a, r in ((0, 0), (1, 64)):
                            act.copy(wide_q[r:r + 64, hf, a, :], q_feat[r:r + 64, hf * HF:(hf + 1) * HF])
                    for hf in range(2):
                        act.wait_ge(*bil_in.at(1 + hf))
                        for a, r in ((0, 0), (1, 64)):
                            act.copy(wide_k[r:r + 64, hf, a, :], bank[r:r + 64, hf, :])
                else:
                    for i, (n, hf) in enumerate(items):
                        act.wait_ge(*(rot_used if rotary else raw).at(i + 1))
                        hi = parts[("q_hi", "k_hi")[n]]
                        act.copy(hi[:, hf * HF:(hf + 1) * HF], feats[n][:, hf * HF:(hf + 1) * HF]
                                 ).then_inc(*hi_done.up())

            @block.vector
            def _(dve):
                step = steps(dve, step_sig)
                for hf in range(2):
                    dve.wait_ge(*v_done.at(hf + 1))
                    half = slice(hf * QT, (hf + 1) * QT)
                    v = bank[:, 6 + hf, :]
                    if wide:
                        dve.tensor_copy(v_wide[:, half, :], v.rearrange("p (t n) -> p t n", n=P))
                        continue
                    for q in range(QT):
                        o = v_aug[:, hf * QT + q, :, 0:DH]
                        vq = v[:, q * P:(q + 1) * P].rearrange("p (h d) -> p h d", d=DH)
                        if bv is not None:
                            dve.tensor_tensor(o, vq, bv.rearrange("p (h d) -> p h d", d=DH), ALU.add)
                        else:
                            dve.tensor_copy(o, vq)
                if rotary:
                    for i, (n, hf) in enumerate(items):
                        f = feats[n][:, hf * HF:(hf + 1) * HF]
                        tmp = rot_tmp[:, hf * HF:(hf + 1) * HF]
                        dve.wait_ge(*rotated.at(i + 1))
                        dve.tensor_tensor(tmp, bank[:, 4 + i % 2, :], sin, ALU.mult)
                        step(dve.tensor_tensor(f, f, cos, ALU.mult))
                        dve.tensor_tensor(f, f, tmp, ALU.add).then_inc(*rot_used.up())
                if not wide:
                    for i, (n, hf) in enumerate(items):
                        dve.wait_ge(*hi_done.at(i + 1))
                        sl = slice(hf * HF, (hf + 1) * HF)
                        dve.tensor_tensor(parts[("q_lo", "k_lo")[n]][:, sl], feats[n][:, sl],
                                          parts[("q_hi", "k_hi")[n]][:, sl].bitcast(F32), ALU.subtract)

            if wide:
                @block.gpsimd
                def _(pool):
                    for hf in range(2):
                        pool.memset(wide_q[64:65, hf, 0, :], 0.0)
                        pool.memset(wide_q[0:1, hf, 1, :], 0.0)
        signals.settle()

    def attention_stage(scale, causal=False, wide=False, guard=False, chunk=0):
        NJ = 2 if wide else 4
        units = [(b, 0) for b in range(B)] if wide else [(b, g) for g in range(4) for b in range(B)]
        NU = len(units)
        MX_BANKS = [0, 1] if wide else [0, 1, 2]
        ST_BANKS = [2, 3] if wide else [3, 4, 5]
        NX, NS = len(MX_BANKS), len(ST_BANKS)
        NG = QT * NJ
        PVB, MISC, SUMS, SUMT = 6, 7, 5, 4
        LEAD = 1 if wide else 3
        TURN = NG - LEAD
        START = 0 if wide else 2
        COPY, RESULT, FLUSH = (1, 3, 5) if wide else (2, 5, 9)

        def maxima_of(n):
            a, w = n - START, TURN - START
            return range(a * NG // w, (a + 1) * NG // w) if 0 <= a < w else range(0)

        (mx_done, mx_used, mp_done, mt_done, m_ready, st_done, exp_done, pv_done, o_ready, ot_done, on_done,
         fl_done, fl_used, built) = (signals(n) for n in (
             "mx_done", "mx_used", "mp_done", "mt_done", "m_ready", "st_done", "exp_done", "pv_done", "o_ready",
             "ot_done", "on_done", "fl_done", "fl_used", "built"))
        NB_ = 3
        base_loaded = [signals(f"base_loaded{i}") for i in range(NB_)]
        step_sig = signals("dve_step")

        def key_op(u, j):
            return wide_k[:, u, j, :] if wide else KS[:, u % 2, j, :]

        def query_op(u, j):
            return wide_q[:, u, j, :] if wide else QM[:, u % 2, :]

        def q_base(g):
            return att_feat[:, 1 + g % NB_, :]

        def k_base(g):
            return att_feat[:, 1 + NB_ + g % NB_, :]

        def flush_of(u):
            return wide or units[u][1] == 3

        NFL = NU if wide else B

        with nc.Block() as block:
            if not wide:
                @block.sync
                def _(sp):
                    for g in range(4):
                        if g >= NB_:
                            sp.wait_ge(*built.at(5 * B * (g - NB_ + 1)))
                        for base, names in ((q_base(g), ("q_hi", "q_lo", "q_hi")), (k_base(g), ("k_hi", "k_hi", "k_lo"))):
                            for blk, name in enumerate(names):
                                sp.dma_start(base[32 * blk:32 * blk + 32, :],
                                             parts[name][32 * g:32 * g + 32, :].bitcast(F32)
                                             ).then_inc(*base_loaded[g % NB_].up(16))

                @block.gpsimd
                def _(pool):
                    for u, (b, g) in enumerate(units):
                        s, tok = u % 2, slice(b * S, (b + 1) * S)
                        if b == 0:
                            pool.wait_ge(*base_loaded[g % NB_].at(96 * (g // NB_ + 1)))
                        if u >= 2:
                            pool.wait_ge(*st_done.at((u - 1) * NG))
                        pool.tensor_copy(QM[0:96, s, :], q_base(g)[0:96, tok]).then_inc(*built.up())
                        for j in range(4):
                            pool.tensor_scalar(KS[0:96, s, j, :], k_base(g)[0:96, tok], K("stack")[0:96, j:j + 1],
                                               None, ALU.mult).then_inc(*built.up())

            @block.tensor
            def _(pe):
                def max_step(u, i):
                    j, q = divmod(i, QT)
                    n = u * NJ * QT + i
                    if q == 0 and not wide:
                        pe.wait_ge(*built.at(5 * u + 2 + j))
                    if n >= NX:
                        pe.wait_ge(*mx_used.at(n - NX + 1))
                    keys = (q + 1) * P if causal else S
                    kr = slice(0, P) if wide else slice(0, 96)
                    ins = pe.matmul(bank[:, MX_BANKS[n % NX], 0:keys], query_op(u, j)[kr, q * P:(q + 1) * P],
                                    key_op(u, j)[kr, 0:keys], start=True, stop=True)
                    if causal:
                        ins = pe.matmul(bank[:, MX_BANKS[n % NX], q * P:(q + 1) * P], identb[:, :], causal_s[:, :], start=False,
                                        stop=True, skip_group_check=True)
                    ins.then_inc(*mx_done.up())

                def misc_free(pe, units_done):
                    if units_done > 0:
                        pe.wait_ge(*on_done.at(units_done))
                    nf = sum(flush_of(v) for v in range(units_done))
                    if nf:
                        pe.wait_ge(*fl_used.at(nf))

                def turn_maxima(u):
                    pe.wait_ge(*mp_done.at(u + 1))
                    misc_free(pe, u - 1)
                    for q in range(QT):
                        if wide:
                            ins = pe.transpose(bank[:, MISC, q * P:(q + 1) * P], max_wide[:, q, :], ident)
                        else:
                            ins = pe.transpose(bank[0:8, MISC, q * P:(q + 1) * P], max_parts[:, q, :].bitcast(F32),
                                               ident)
                    ins.then_inc(*mt_done.up())

                def scores(u, n):
                    kt, j = divmod(n, NJ)
                    m = u * NG + n
                    if n == 0:
                        pe.wait_ge(*m_ready.at(u + 1))
                    if m >= NS:
                        pe.wait_ge(*exp_done.at(m - NS + 1))
                    lo = kt * P if causal else 0
                    st = bank[:, ST_BANKS[m % NS], :]
                    ins = pe.matmul(st[:, lo:S], key_op(u, j)[:, kt * P:(kt + 1) * P], query_op(u, j)[:, lo:S],
                                    start=True, stop=True)
                    if causal:
                        ins = pe.matmul(st[:, lo:lo + P], identb[:, :], causal_st[:, :], start=False, stop=True,
                                        skip_group_check=True)
                    ins.then_inc(*st_done.up())

                def values(u, kt):
                    b, g = units[u]
                    pe.wait_ge(*exp_done.at(u * NG + (kt + 1) * NJ))
                    if kt == 0 and u >= 1:
                        pe.wait_ge(*o_ready.at(u))
                    lo = kt * P if causal else 0
                    for j in range(NJ):
                        p = probs[:, kt % 2, j, lo:S]
                        if wide:
                            pe.matmul(bank[64 * j:64 * j + 64, PVB, lo:S], v_wide[:, b * QT + kt, 64 * j:64 * j + 64],
                                      p, start=(kt == 0), stop=(kt == QT - 1))
                        else:
                            ins = pe.matmul(bank[32 * j:32 * j + 32, PVB, lo:S],
                                            v_aug[:, b * QT + kt, 4 * g + j, :], p, start=(kt == 0),
                                            stop=(kt == QT - 1))
                    if wide:
                        for j in range(NJ):
                            ins = pe.matmul(bank[32 * j:32 * j + 32, SUMS, :], ones32[:, :], probs[:, kt % 2, j, :],
                                            start=(kt == 0), stop=(kt == QT - 1))
                    ins.then_inc(*pv_done.up())

                def turn_result(u):
                    pe.wait_ge(*o_ready.at(u + 1))
                    if u + 1 < NU:
                        pe.wait_ge(*m_ready.at(u + 2))
                    misc_free(pe, u)
                    for q in range(QT):
                        ins = pe.transpose(bank[:, MISC, q * P:(q + 1) * P], o_feat[:, q * P:(q + 1) * P], ident)
                    if wide:
                        for q in range(QT):
                            ins = pe.transpose(bank[:, SUMT, q * 64:(q + 1) * 64], o_sums[0:64, q * P:(q + 1) * P],
                                               ident[0:64, 0:64])
                    ins.then_inc(*ot_done.up())

                def flush(u):
                    b = units[u][0]
                    pe.wait_ge(*on_done.at(u + 1))
                    for q in range(QT):
                        ins = pe.transpose(bank[:, MISC, q * P:(q + 1) * P], o_tok[:, b, q, :], ident)
                    ins.then_inc(*fl_done.up())

                for i in range(NG):
                    max_step(0, i)
                turn_maxima(0)
                for u in range(NU):
                    for n in range(NG):
                        scores(u, n)
                        if u + 1 < NU:
                            for i in maxima_of(n):
                                max_step(u + 1, i)
                        if n % NJ == 1 and u * QT + n // NJ >= 1:
                            values(*divmod(u * QT + n // NJ - 1, QT))
                        if n == RESULT and u >= 1:
                            turn_result(u - 1)
                        if n == FLUSH and u >= 1 and flush_of(u - 1):
                            flush(u - 1)
                        if n == TURN and u + 1 < NU:
                            turn_maxima(u + 1)
                values(NU - 1, QT - 1)
                turn_result(NU - 1)
                flush(NU - 1)

            @block.vector
            def _(dve):
                step = steps(dve, step_sig)

                def reduce_step(u, i):
                    j, q = divmod(i, QT)
                    n = u * NJ * QT + i
                    keys = (q + 1) * P if causal else S
                    dve.wait_ge(*mx_done.at(n + 1))
                    if wide:
                        o = max_wide[:, q, (64, 0)[j]:(64, 0)[j] + 1]
                        if i == 0 and u >= 1:
                            dve.wait_ge(*mt_done.at(u))
                    else:
                        o = neg_max[:, q, j:j + 1]
                    ins = dve.tensor_reduce(o, bank[:, MX_BANKS[n % NX], 0:keys], X_AXIS, ALU.max, negate=True)
                    ins.then_inc(*mx_used.up())
                    return ins

                def split_maxima(u):
                    if wide:
                        dve.wait_ge(*mx_used.at((u + 1) * NJ * QT))
                        dve.sem_inc(*mp_done.up())
                        return
                    dve.wait_ge(*mx_used.at((u + 1) * NJ * QT))
                    if u >= 1:
                        dve.wait_ge(*mt_done.at(u))
                    step(dve.tensor_copy(max_parts[:, :, 0:4], neg_max[:, :, :]))
                    dve.tensor_tensor(max_parts[:, :, 4:8], neg_max[:, :, :], max_parts[:, :, 0:4].bitcast(F32),
                                      ALU.subtract).then_inc(*mp_done.up())

                def normalise(u):
                    b, g = units[u]
                    dve.wait_ge(*ot_done.at(u + 1))
                    if wide:
                        o = bank[:, MISC, :].rearrange("p (q j d) -> p q j d", q=QT, j=2)
                        r = bank[:, SUMT, 0:4 * 64].rearrange("p (q j d) -> p q j d", q=QT, j=2)[:, :, :, 0]
                        dest = o_tok[:, b, :, :].rearrange("p q (j d) -> p q j d", j=2)
                        width = WH
                    else:
                        o = bank[:, MISC, :].rearrange("p (q j d) -> p q j d", q=QT, j=4)
                        r = o[:, :, :, DH]
                        o = o[:, :, :, 0:DH]
                        dest = o_tok[:, b, :, 32 * g:32 * g + 32].rearrange("p q (j d) -> p q j d", j=4)
                        width = DH
                    rs = rsum[:, :, 0:NJ]
                    if guard:
                        step(dve.tensor_scalar(rs, r, 1e-12, None, ALU.max))
                        step(dve.reciprocal(rs, rs))
                    else:
                        step(dve.reciprocal(rs, r))
                    dve.tensor_tensor(dest, o, rs.unsqueeze(3).broadcast_to([P, QT, NJ, width]), ALU.mult
                                      ).then_inc(*on_done.up())

                for i in range(NG):
                    reduce_step(0, i)
                split_maxima(0)
                for u in range(NU):
                    for n in range(NG):
                        if u + 1 < NU:
                            for i in maxima_of(n):
                                reduce_step(u + 1, i)
                        if n == RESULT and u >= 1:
                            normalise(u - 1)
                        if n == TURN - 1 and u + 1 < NU:
                            split_maxima(u + 1)
                normalise(NU - 1)

            @block.scalar
            def _(act):
                def maxima_rows(u):
                    act.wait_ge(*mt_done.at(u + 1))
                    if wide:
                        act.copy(wide_q[64:65, u, 0, :], bank[64:65, MISC, :])
                        act.copy(wide_q[0:1, u, 1, :], bank[0:1, MISC, :]).then_inc(*m_ready.up())
                    else:
                        act.copy(QM[96:104, u % 2, :], bank[0:8, MISC, :]).then_inc(*m_ready.up())

                def exponentials(u, n):
                    kt, j = divmod(n, NJ)
                    m = u * NG + n
                    act.wait_ge(*st_done.at(m + 1))
                    if j == 0 and u * QT + kt >= 2:
                        act.wait_ge(*pv_done.at(u * QT + kt - 1))
                    lo = kt * P if causal else 0
                    act.activation(probs[:, kt % 2, j, lo:S], bank[:, ST_BANKS[m % NS], lo:S], ACT.Exp, scale=scale).then_inc(*exp_done.up())

                def copy_result(u):
                    act.wait_ge(*pv_done.at((u + 1) * QT))
                    if u >= 1:
                        act.wait_ge(*ot_done.at(u))
                    if wide:
                        act.copy(o_sums[0:64, :], bank[0:64, SUMS, :])
                    act.copy(o_feat[:, :], bank[:, PVB, :]).then_inc(*o_ready.up())

                def flush_copy(u, k):
                    b = units[u][0]
                    act.wait_ge(*fl_done.at(k))
                    act.copy(att_feat[:, chunk, b * S:(b + 1) * S], bank[:, MISC, :]).then_inc(*fl_used.up())

                k = 0
                maxima_rows(0)
                for u in range(NU):
                    for n in range(NG):
                        exponentials(u, n)
                        if n == COPY and u >= 1:
                            copy_result(u - 1)
                        if n == FLUSH and u >= 1 and flush_of(u - 1):
                            k += 1
                            flush_copy(u - 1, k)
                        if n == TURN and u + 1 < NU:
                            maxima_rows(u + 1)
                copy_result(NU - 1)
                flush_copy(NU - 1, k + 1)
        signals.settle()

    def cross_stage(wname, bq, bk, bv, mask_src, mask_bool, heads, scale, fill, mask_tiles):
        wq, wk, wv = (W(wname, 128 * i, 128 * i + 128) for i in range(3))
        dh = P // heads
        HB = max(heads // 4, 1)
        NB = heads // HB
        width = heads * SC
        (m_ld, kq, kq_used, kbd_done, q_ready, s_done, s_used, sh_done, mx_ok, e_done, et_done, et_used, o_done,
         o_used, ot_done, ot_used, nb_done, v_ok) = (signals(n) for n in (
             "m_ld", "kq", "kq_used", "kbd_done", "q_ready", "s_done", "s_used", "sh_done", "mx_ok", "e_done",
             "et_done", "et_used", "o_done", "o_used", "ot_done", "ot_used", "nb_done", "v_ok"))
        step_sig, e_used, msk = signals("dve_step"), signals("e_used"), signals("msk")
        pool_step = signals("pool_step")
        at = [T]

        def take(n):
            at[0] += n
            return flat[:, at[0] - n:at[0]]

        kbd = take(B * width).rearrange("p (b h k) -> p b h k", b=B, k=SC)
        v_ctx = take(B * P)[0:SC, :].rearrange("p (b n) -> p b n", b=B)
        k_ctx = take(B * SC)
        neg = take(NT * SC).rearrange("p (t k) -> p t k", k=SC)
        masks = take(NT * SC).rearrange("p (t k) -> p t k", k=SC)
        sc = take(width).rearrange("p (h k) -> p h k", k=SC)
        ex_flat = take(max(width, NT * SC))
        raw_mask = ex_flat[:, 0:NT * SC].rearrange("p (t k) -> p t k", k=SC)
        ex = ex_flat[:, 0:width].rearrange("p (h k) -> p h k", k=SC)
        et = probs[0:SC, :, :, :].rearrange("p a b c -> p (a b c)").rearrange("p (h q) -> p h q", q=P)
        stat = rsum
        mx = picked[:, 0, 0:heads]
        rs = picked[:, 1, 0:heads]
        tiles = mask_tiles

        def m01(t):
            return masks[:, tiles(t), :]

        with nc.Block() as block:
            @block.sync
            def _(sp):
                n, dst = mask_src(raw_mask)
                sp.dma_start(dst, n).then_inc(*m_ld.up(16))

            @block.tensor
            def _(pe):
                pe.matmul(bank[:, 4, 0:B * SC], wk, ctx_feat[:, :], start=True, stop=True).then_inc(*kq.up())
                for b in range(B):
                    ins = pe.matmul(bank[0:SC, 5, b * P:(b + 1) * P], ctx_feat[:, b * SC:(b + 1) * SC], wv, start=True,
                                    stop=True)
                ins.then_inc(*kq.up())
                for hf in range(2):
                    pe.matmul(bank[:, 6 + hf, :], wq, x_feat[:, hf * HF:(hf + 1) * HF], start=True, stop=True
                              ).then_inc(*kq.up())
                pe.wait_ge(*q_ready.at(2))
                pe.wait_ge(*kbd_done.at(1))
                pe.wait_ge(*v_ok.at(1))
                for t in range(NT + 1):
                    if t < NT:
                        if t >= 1:
                            pe.wait_ge(*s_used.at(t))
                        for n in range(NB):
                            ins = pe.matmul(bank[:, n, 0:HB * SC], q_feat[:, t * P:(t + 1) * P],
                                            kbd[:, t // QT, n * HB:(n + 1) * HB, :], start=True, stop=True)
                        ins.then_inc(*s_done.up())
                    if t >= 1:
                        u = t - 1
                        pe.wait_ge(*e_done.at(u + 1))
                        for n in range(NB):
                            m = u * NB + n
                            if m >= 2:
                                pe.wait_ge(*et_used.at(m - 1))
                            for h in range(HB):
                                ins = pe.transpose(bank[0:SC, 4 + m % 2, h * P:(h + 1) * P], ex[:, n * HB + h, :],
                                                   ident)
                            ins.then_inc(*et_done.up())
                        pe.wait_ge(*et_used.at((u + 1) * NB))
                        if u >= 1:
                            pe.wait_ge(*o_used.at(u))
                        for h in range(heads):
                            ins = pe.matmul(bank[:, 6, h * dh:(h + 1) * dh], et[:, h, :],
                                            v_ctx[:, u // QT, h * dh:(h + 1) * dh], start=True, stop=True)
                        ins.then_inc(*o_done.up())
                        pe.wait_ge(*o_used.at(u + 1))
                        if u % QT == 0 and u:
                            pe.wait_ge(*ot_used.at(u // QT))
                        ins = pe.transpose(bank[:, 7, (u % QT) * P:(u % QT + 1) * P], o_tok[:, u // QT, u % QT, :],
                                           ident)
                        if u % QT == QT - 1:
                            ins.then_inc(*ot_done.up())

            @block.scalar
            def _(act):
                act.wait_ge(*kq.at(1))
                if bk is not None:
                    act.activation(k_ctx, bank[:, 4, 0:B * SC], ACT.Identity, bias=bk).then_inc(*kq_used.up())
                else:
                    act.copy(k_ctx, bank[:, 4, 0:B * SC]).then_inc(*kq_used.up())
                for hf in range(2):
                    act.wait_ge(*kq.at(3 + hf))
                    o = q_feat[:, hf * HF:(hf + 1) * HF]
                    if bq is not None:
                        act.activation(o, bank[:, 6 + hf, :], ACT.Identity, bias=bq).then_inc(*q_ready.up())
                    else:
                        act.copy(o, bank[:, 6 + hf, :]).then_inc(*q_ready.up())
                for t in range(NT):
                    act.wait_ge(*sh_done.at(t + 1))
                    if t >= 1:
                        act.wait_ge(*et_done.at(t * NB))
                        act.wait_ge(*e_used.at(t))
                    act.activation(ex, sc, ACT.Exp, scale=scale).then_inc(*e_done.up())
                    for n in range(NB):
                        m = t * NB + n
                        act.wait_ge(*et_done.at(m + 1))
                        if n == 0 and t >= 1:
                            act.wait_ge(*o_done.at(t))
                        act.copy(et[:, n * HB:(n + 1) * HB, :],
                                 bank[0:SC, 4 + m % 2, 0:HB * P].rearrange("p (h q) -> p h q", q=P)
                                 ).then_inc(*et_used.up())
                    if t % QT == QT - 1:
                        act.wait_ge(*ot_done.at(t // QT + 1))
                        act.copy(att_feat[:, 0, (t // QT) * S:(t // QT + 1) * S], bank[:, 7, :]
                                 ).then_inc(*ot_used.up())

            @block.vector
            def _(dve):
                step = steps(dve, step_sig)
                dve.wait_ge(*m_ld.at(16))
                _, dst = mask_src(raw_mask)
                n_m = masks[:, 0:mask_count(mask_bool), :]
                step(dve.tensor_scalar(n_m, dst, 0.0, None, ALU.not_equal))
                dve.tensor_scalar(neg[:, 0:mask_count(mask_bool), :], n_m, 1.0, fill, ALU.subtract, ALU.mult
                                  ).then_inc(*nb_done.up())
                dve.wait_ge(*kq.at(2))
                if bv is not None:
                    dve.tensor_tensor(v_ctx, bank[0:SC, 5, 0:B * P].rearrange("p (b n) -> p b n", b=B),
                                      bv[0:SC, :].unsqueeze(1).broadcast_to([SC, B, P]), ALU.add
                                      ).then_inc(*v_ok.up())
                else:
                    dve.tensor_copy(v_ctx, bank[0:SC, 5, 0:B * P].rearrange("p (b n) -> p b n", b=B)
                                    ).then_inc(*v_ok.up())
                dve.wait_ge(*kq_used.at(1))
                for b in range(B):
                    kb = k_ctx[:, b * SC:(b + 1) * SC]
                    if heads == 1:
                        ins = dve.tensor_copy(kbd[:, b, 0, :], kb)
                    else:
                        ins = dve.tensor_tensor(kbd[:, b, :, :], kb.unsqueeze(1).broadcast_to([P, heads, SC]),
                                                K("headmask").unsqueeze(2).broadcast_to([P, heads, SC]), ALU.mult)
                ins.then_inc(*kbd_done.up())
                for t in range(NT):
                    dve.wait_ge(*s_done.at(t + 1))
                    if t >= 1:
                        dve.wait_ge(*e_done.at(t))
                    src = bank[:, 0:NB, 0:HB * SC].rearrange("p n (h k) -> p n h k", k=SC)
                    mm = m01(t).unsqueeze(1).unsqueeze(1).broadcast_to([P, NB, HB, SC])
                    dve.tensor_tensor(sc.rearrange("p (n h) k -> p n h k", h=HB), src, mm, ALU.mult
                                      ).then_inc(*s_used.up())
                    dve.wait_ge(*mx_ok.at(t + 1))
                    step(dve.tensor_reduce(mx, sc, X_AXIS, ALU.max))
                    dve.tensor_tensor(sc, sc, mx.unsqueeze(2).broadcast_to([P, heads, SC]), ALU.subtract
                                      ).then_inc(*sh_done.up())
                    dve.wait_ge(*e_done.at(t + 1))
                    ins = dve.tensor_reduce(rs, ex, X_AXIS, ALU.add)
                    ins.then_inc(*e_used.up())
                    dve.wait_ge(*e_used.at(t + 1))
                    step(dve.reciprocal(rs, rs))
                    dve.wait_ge(*o_done.at(t + 1))
                    dve.tensor_tensor(o_tok[:, t // QT, t % QT, :].rearrange("p (h d) -> p h d", h=heads),
                                      bank[:, 6, 0:P].rearrange("p (h d) -> p h d", h=heads),
                                      rs.unsqueeze(2).broadcast_to([P, heads, dh]), ALU.mult
                                      ).then_inc(*o_used.up())

            @block.gpsimd
            def _(pool):
                pool.wait_ge(*nb_done.at(1))
                for t in range(NT):
                    pool.wait_ge(*s_used.at(t + 1))
                    pool.tensor_tensor(sc, sc, neg[:, tiles(t), :].unsqueeze(1).broadcast_to([P, heads, SC]), ALU.add
                                       ).then_inc(*mx_ok.up())
        signals.settle()

    def mask_count(kind):
        return {"q": QT, "bq": NT, "b": B}[kind]

    def route_stage(terms, bias, experts, top_k, renormalise, distance=False):
        E, EP = experts, max(experts, 8)
        ns = 8 - top_k
        (l_done, s_ready, x_done, g_done, gt_done, hi_ok, sq_done, kk_done, kk_ok) = (signals(n) for n in (
            "l_done", "s_ready", "x_done", "g_done", "gt_done", "hi_ok", "sq_done", "kk_done", "kk_ok"))
        step_sig = signals("dve_step")
        sq = scratch[:, 0:T]
        with nc.Block() as block:
            @block.tensor
            def _(pe):
                weights_here(pe)
                if distance:
                    pe.wait_ge(*kk_done.at(1))
                    pe.matmul(bank[:, 2, 0:16], ones128, kk_sq, start=True, stop=True).then_inc(*kk_ok.up())
                for t in range(NT):
                    for n, (operand, w) in enumerate(terms):
                        ins = pe.matmul(bank[:, 0, t * 16:t * 16 + E], operand[:, t * P:(t + 1) * P], w,
                                        start=(n == 0), stop=(n == len(terms) - 1))
                ins.then_inc(*l_done.up())
                pe.wait_ge(*g_done.at(1))
                for t in range(NT):
                    ins = pe.transpose(bank[0:16, 4 + t // QT, (t % QT) * P:(t % QT + 1) * P], gates[:, t, :], ident)
                ins.then_inc(*gt_done.up())

            @block.vector
            def _(dve):
                step = steps(dve, step_sig)
                if distance:
                    dve.wait_ge(loads["ld_w"], 16)
                    dve.tensor_tensor(kk_sq, W("l0_keys"), W("l0_keys"), ALU.mult).then_inc(*kk_done.up())
                    for t in range(NT):
                        ins = dve.tensor_tensor_reduce(out=sum_tok[:, t, :], in0=x_tok[:, t, :], in1=x_tok[:, t, :],
                                                       scale=1.0, scalar=0.0, op0=ALU.mult, op1=ALU.add,
                                                       accum_out=small[:, t, 0:1])
                    step(ins)
                    dve.wait_ge(*kk_ok.at(1))
                    step(dve.tensor_tensor(kk_row, bias, bank[:, 2, 0:16], ALU.subtract))
                step(dve.memset(gates[:, :, :], 0.0))
                dve.memset(lg[:, :, 0:EP], -HUGE)
                step(dve.memset(lg[:, :, EP:EP + ns], HUGE))
                step(dve.memset(top_in[:, :, :], HUGE))
                dve.wait_ge(*l_done.at(1))
                logit = bank[:, 0, 0:NT * 16].rearrange("p (t e) -> p t e", e=16)[:, :, 0:E]
                brow = (kk_row if distance else bias)
                if bias is not None:
                    step(dve.tensor_tensor(lg[:, :, 0:E], logit, brow.unsqueeze(1).broadcast_to([P, NT, E]), ALU.add))
                else:
                    step(dve.tensor_copy(lg[:, :, 0:E], logit))
                if distance:
                    step(dve.tensor_tensor(lg[:, :, 0:E], lg[:, :, 0:E], small[:, :, 0:1].broadcast_to([P, NT, E]),
                                           ALU.subtract))
                for t in range(NT):
                    ins = dve.max(top8[:, t, :], lg[:, t, 0:EP])
                step(ins)
                step(dve.tensor_copy(top_in[:, :, 0:top_k], top8[:, :, 0:top_k]))
                for t in range(NT):
                    ins = dve.match_replace(lg_rep[:, t, 0:EP + ns], top_in[:, t, :], lg[:, t, 0:EP + ns], -HUGE)
                step(ins)
                step(dve.tensor_tensor(picked[:, :, 0:E], lg_rep[:, :, 0:E], lg[:, :, 0:E], ALU.not_equal))
                dve.tensor_tensor(lg[:, :, 0:E], lg[:, :, 0:E], top8[:, :, 0:1].broadcast_to([P, NT, E]),
                                  ALU.subtract).then_inc(*s_ready.up())
                dve.wait_ge(*x_done.at(1))
                step(dve.tensor_tensor(picked[:, :, 0:E], picked[:, :, 0:E], lg[:, :, 0:E], ALU.mult))
                step(dve.tensor_reduce(small[:, :, 1], (picked if renormalise else lg)[:, :, 0:E], X_AXIS, ALU.add))
                step(dve.reciprocal(small[:, :, 1], small[:, :, 1]))
                step(dve.tensor_tensor(gates[:, :, 0:E], picked[:, :, 0:E],
                                       small[:, :, 1:2].broadcast_to([P, NT, E]), ALU.mult))
                dve.tensor_reduce(gate_sum[:, :], gates[:, :, 0:E], X_AXIS, ALU.add).then_inc(*g_done.up())
                dve.wait_ge(*hi_ok.at(1))
                dve.tensor_tensor(gate_parts[32:48, :], gate_rows, gate_parts[0:16, :].bitcast(F32),
                                  ALU.subtract)

            @block.scalar
            def _(act):
                act.wait_ge(*s_ready.at(1))
                act.activation(lg[:, :, 0:E], lg[:, :, 0:E], ACT.Exp).then_inc(*x_done.up())
                act.wait_ge(*gt_done.at(1))
                rows16 = bank[0:16, 4:6, :].rearrange("p a n -> p (a n)")
                act.copy(gate_rows, rows16)
                act.copy(gate_parts[0:16, :], rows16).then_inc(*hi_ok.up())
        signals.settle()

    kk_sq = sb("kk_sq", [P, 16])[:, :]
    kk_row = sb("kk_row", [P, 16])[:, :]
    route_w = sb("route_w", [P, 16])
    ones128 = sb("ones128", [P, P])[:, :]

    def expert_stage(source, experts, b1, b2, affine=None):
        NFT = 4
        seq = [(e, hf, f) for e in range(experts) for hf in range(2) for f in range(NFT)]
        N = len(seq)
        LAG = 3
        (up_done, gelu_done, gate_ok, gate_used, h_ready, dn_done, xe_ok, w_used, y_ok) = (signals(n) for n in (
            "up_done", "gelu_done", "gate_ok", "gate_used", "h_ready", "dn_done", "xe_ok", "w_used", "y_ok"))
        g_buf = scratch[:, 0:3 * HF].rearrange("p (s n) -> p s n", n=HF)
        h_buf = scratch[:, 3 * HF:7 * HF].rearrange("p (s n) -> p s n", n=HF)
        first = expert_total[0]
        XE = att_feat[:, 0:2, :]

        def slot(e):
            return (first + e) % NW

        def arrived(eng, e):
            n = first + e
            eng.wait_ge(expert_loaded[n % NW], 16 * (n // NW + 1))

        load_experts(first, experts)
        with nc.Block() as block:
            emit_loads(block, w_used)

            @block.tensor
            def _(pe):
                for i in range(N + LAG):
                    if i < N:
                        e, hf, f = seq[i]
                        if hf == 0 and f == 0:
                            arrived(pe, e)
                            if affine is not None:
                                pe.wait_ge(*xe_ok.at(e + 1))
                        if f == 0:
                            k = e * 2 + hf
                            if k >= 2:
                                pe.wait_ge(*gate_used.at(k - 1))
                            pe.matmul(bank[:, 4 + k % 2, :], sel[0:96, e, :], gate_parts[0:96, hf * HF:(hf + 1) * HF],
                                      start=True, stop=True).then_inc(*gate_ok.up())
                        if i >= 3:
                            pe.wait_ge(*gelu_done.at(i - 2))
                        x = (XE[:, e % 2, :] if affine is not None else source)[:, hf * HF:(hf + 1) * HF]
                        pe.matmul(bank[:, (0, 1, 2)[i % 3], :], wring[:, slot(e), f * P:(f + 1) * P], x, start=True,
                                  stop=True).then_inc(*up_done.up())
                    if i >= LAG:
                        m = i - LAG
                        e, hf, f = seq[m]
                        pe.wait_ge(*h_ready.at(m + 1))
                        ins = pe.matmul(bank[:, 6 + hf, :], wring[:, slot(e), 512 + f * P:512 + (f + 1) * P],
                                        h_buf[:, m % 4, :], start=(e == 0 and f == 0), stop=False,
                                        skip_group_check=True)
                        ins.then_inc(*dn_done.up())
                for hf in range(2):
                    pe.matmul(bank[:, 6 + hf, :], b2, gate_rows[:, hf * HF:(hf + 1) * HF], start=False, stop=True,
                              skip_group_check=True).then_inc(*y_ok.up())

            @block.scalar
            def _(act):
                for i, (e, hf, f) in enumerate(seq):
                    act.wait_ge(*up_done.at(i + 1))
                    if i >= 3:
                        act.wait_ge(*h_ready.at(i - 2))
                    act.activation(g_buf[:, i % 3, :], bank[:, (0, 1, 2)[i % 3], :], ACT.Gelu, bias=C(*b1(e, f))
                                   ).then_inc(*gelu_done.up())
                for hf in range(2):
                    act.wait_ge(*y_ok.at(hf + 1))
                    act.copy(y_feat[:, hf * HF:(hf + 1) * HF], bank[:, 6 + hf, :])

            @block.vector
            def _(dve):
                for i, (e, hf, f) in enumerate(seq):
                    dve.wait_ge(*gelu_done.at(i + 1))
                    k = e * 2 + hf
                    if f == 0:
                        dve.wait_ge(*gate_ok.at(k + 1))
                    if i >= 4:
                        dve.wait_ge(*dn_done.at(i - 3))
                    ins = dve.tensor_tensor(h_buf[:, i % 4, :], g_buf[:, i % 3, :], bank[:, 4 + k % 2, :], ALU.mult)
                    ins.then_inc(*h_ready.up())
                    if f == NFT - 1:
                        dve.wait_ge(*h_ready.at(i + 1))
                        dve.sem_inc(*gate_used.up())

            if affine is not None:
                @block.gpsimd
                def _(pool):
                    for e in range(experts):
                        if e >= 2:
                            pool.wait_ge(*up_done.at((e - 1) * 8))
                        pool.tensor_scalar(XE[:, e % 2, :], source[:, :], affine(e)[0], affine(e)[1], ALU.mult,
                                           ALU.add).then_inc(*xe_ok.up())
        expert_total[0] = first + experts
        signals.settle()

    pending = []

    def load_experts(first, experts):
        pending.extend(range(first, first + experts))

    def emit_loads(block, w_used):
        todo = list(pending)
        pending.clear()
        dn_done = signals("dn_done")
        first = todo[0]

        @block.sync
        def _(sp):
            for n in todo:
                if n - NW >= first:
                    sp.wait_ge(*dn_done.at((n - NW - first + 1) * 8))
                src = l0_experts[n, :, :] if n < 16 else l2_experts[n - 16, :, :]
                sp.dma_start(wring[:, n % NW, :], src).then_inc(expert_loaded[n % NW], 16)

    def gated_stage():
        seq = [(p_, hf) for p_ in range(9) for hf in range(2)]
        (up_done, gelu_done, gate_ok, h_ready, dn_done, y_ok, t_ok) = (signals(n) for n in (
            "up_done", "gelu_done", "gate_ok", "h_ready", "dn_done", "y_ok", "t_ok"))
        g_buf = scratch[:, 0:3 * HF].rearrange("p (s n) -> p s n", n=HF)
        h_buf = scratch[:, 3 * HF:5 * HF].rearrange("p (s n) -> p s n", n=HF)
        t_buf = scratch[:, 5 * HF:7 * HF].rearrange("p (s n) -> p s n", n=HF)
        with nc.Block() as block:
            @block.tensor
            def _(pe):
                for i in range(len(seq) + 1):
                    if i < len(seq):
                        p_, hf = seq[i]
                        x = x_feat[:, hf * HF:(hf + 1) * HF]
                        if i >= 2:
                            pe.wait_ge(*h_ready.at(i - 1))
                        s = i % 2
                        if p_ < 8:
                            wu, wg = (W("l3_w1", p_ * 256 + a * 128, p_ * 256 + a * 128 + 128) for a in range(2))
                        else:
                            wu, wg = W("l3_ws1", 0, 128), W("l3_ws1", 128, 256)
                        pe.matmul(bank[:, 2 * s, :], wu, x, start=True, stop=True)
                        ins = pe.matmul(bank[:, 2 * s + 1, :], wg, x, start=True, stop=True)
                        ins.then_inc(*up_done.up())
                        if p_ < 8:
                            pe.matmul(bank[:, 4 + s, :], sel[0:96, p_, :],
                                      gate_parts[0:96, hf * HF:(hf + 1) * HF], start=True, stop=True
                                      ).then_inc(*gate_ok.up())
                    if i >= 1:
                        p_, hf = seq[i - 1]
                        pe.wait_ge(*h_ready.at(i))
                        w2 = W("l3_w2", p_ * 128, p_ * 128 + 128) if p_ < 8 else W("l3_ws2")
                        ins = pe.matmul(bank[:, 6 + hf, :], w2, h_buf[:, (i - 1) % 2, :], start=(p_ == 0),
                                        stop=(p_ == 8), skip_group_check=True)
                        ins.then_inc(*dn_done.up())

            @block.scalar
            def _(act):
                for i, (p_, hf) in enumerate(seq):
                    act.wait_ge(*up_done.at(i + 1))
                    if i >= 2:
                        act.wait_ge(*h_ready.at(i - 1))
                    act.activation(g_buf[:, i % 2, :], bank[:, 2 * (i % 2) + 1, :], ACT.Silu
                                   ).then_inc(*gelu_done.up())
                for hf in range(2):
                    act.wait_ge(*dn_done.at(17 + hf))
                    act.copy(y_feat[:, hf * HF:(hf + 1) * HF], bank[:, 6 + hf, :])

            @block.vector
            def _(dve):
                for i, (p_, hf) in enumerate(seq):
                    dve.wait_ge(*gelu_done.at(i + 1))
                    if i >= 2:
                        dve.wait_ge(*dn_done.at(i - 1))
                    if p_ < 8:
                        dve.tensor_tensor(t_buf[:, i % 2, :], g_buf[:, i % 2, :], bank[:, 2 * (i % 2), :], ALU.mult
                                          ).then_inc(*t_ok.up())
                        dve.wait_ge(*t_ok.at(i + 1))
                        dve.wait_ge(*gate_ok.at(i + 1))
                        dve.tensor_tensor(h_buf[:, i % 2, :], t_buf[:, i % 2, :], bank[:, 4 + i % 2, :], ALU.mult
                                          ).then_inc(*h_ready.up())
                    else:
                        dve.tensor_tensor(h_buf[:, i % 2, :], g_buf[:, i % 2, :], bank[:, 2 * (i % 2), :], ALU.mult
                                          ).then_inc(*h_ready.up())
        signals.settle()

    def memory_stage():
        TC = (SC - 4) // 4 + 1
        conv_ok, moved = signals("conv_ok"), signals("moved")
        with nc.Block() as block:
            @block.tensor
            def _(pe):
                for b in range(B):
                    for r in range(4):
                        lo = b * S + 256 + r
                        ins = pe.matmul(bank[:, 0, b * 32:b * 32 + TC], W("l0_conv", r * P, r * P + P),
                                        x_feat[:, lo:lo + 4 * (TC - 1) + 1:4], start=(r == 0), stop=(r == 3))
                ins.then_inc(*conv_ok.up())

            @block.gpsimd
            def _(pool):
                for b in range(B):
                    o = b * S
                    pool.tensor_copy(y_feat[:, o:o + 256 - TC], x_feat[:, o + TC:o + 256])
                    pool.tensor_copy(y_feat[:, o + 256:o + S - SC], x_feat[:, o + 256 + SC:o + S])
                    pool.tensor_copy(y_feat[:, o + S - SC:o + S], ctx_feat[:, b * SC:(b + 1) * SC])

            @block.scalar
            def _(act):
                act.wait_ge(*conv_ok.at(1))
                for b in range(B):
                    act.activation(y_feat[:, b * S + 256 - TC:b * S + 256], bank[:, 0, b * 32:b * 32 + TC],
                                   ACT.Identity, bias=C("conv_b"))
        signals.settle()

    def ternary_stage():
        w_ld, tq_done, wt_in, wt_done = (signals(n) for n in ("w_ld", "tq_done", "wt_in", "wt_done"))
        v_clear = signals("v_clear")
        step_sig = signals("dve_step")
        MAGIC = 1.5 * 2.0 ** 23
        amax, scl, inv = small[:, :, 0], small[:, :, 1], small[:, :, 2]
        with nc.Block() as block:
            @block.sync
            def _(sp):
                for s in range(4):
                    sp.dma_start(tern_i[32 * s:32 * s + 32, :], packed_in.rearrange("(o i) -> o i", i=P)
                                 ).then_inc(*w_ld.up(16))
                sp.dma_start(weights13[:, 0:W3_N], weights3_in).then_inc(loads["ld_w3"], 16)

            @block.gpsimd
            def _(pool):
                pool.memset(v_aug[:, :, :, :], 0.0).then_inc(*v_clear.up())
                pool.wait_ge(*v_clear.at(1))
                pool.memset(v_aug[:, :, :, DH:DH + 1], 1.0)

            @block.vector
            def _(dve):
                step = steps(dve, step_sig)
                dve.wait_ge(*w_ld.at(64))
                for s in range(4):
                    r = slice(32 * s, 32 * s + 32)
                    ins = dve.tensor_scalar(tern_i[r, :], tern_i[r, :], 2 * s, 3, ALU.logical_shift_right,
                                            ALU.bitwise_and)
                step(ins)
                step(dve.tensor_copy(tern_f[:, :], tern_i[:, :]))
                dve.tensor_scalar(tern_f[:, :], tern_f[:, :], 1.0, R("l1f_scale"), ALU.subtract, ALU.mult
                                  ).then_inc(*wt_in.up())
                step(dve.tensor_reduce(amax, x_tok[:, :, :], X_AXIS, ALU.max, apply_absolute_value=True))
                step(dve.tensor_scalar(amax, amax, 1e-5, None, ALU.max))
                step(dve.reciprocal(scl, amax))
                step(dve.tensor_scalar(scl, scl, 127.0, None, ALU.mult))
                step(dve.reciprocal(inv, scl))
                for t in range(NT):
                    ins = dve.tensor_scalar(sum_tok[:, t, :], x_tok[:, t, :], scl[:, t:t + 1], MAGIC, ALU.mult,
                                            ALU.add)
                step(ins)
                step(dve.tensor_scalar(sum_tok[:, :, :], sum_tok[:, :, :], MAGIC, 127.0, ALU.subtract, ALU.min))
                for t in range(NT):
                    ins = dve.tensor_scalar(sum_tok[:, t, :], sum_tok[:, t, :], -128.0, inv[:, t:t + 1], ALU.max,
                                            ALU.mult)
                    if t % QT == QT - 1:
                        ins.then_inc(*tq_done.up())

            @block.tensor
            def _(pe):
                pe.wait_ge(*wt_in.at(1))
                pe.transpose(bank[:, 0, 0:P], tern_f[:, :], ident).then_inc(*wt_done.up())
                for hf in range(2):
                    pe.wait_ge(*tq_done.at(hf + 1))
                    for q in range(QT):
                        ins = pe.transpose(bank[:, 1 + hf, q * P:(q + 1) * P], sum_tok[:, hf * QT + q, :], ident)
                    ins.then_inc(*wt_done.up())

            @block.scalar
            def _(act):
                act.wait_ge(*wt_done.at(1))
                act.copy(tern_w[:, :], bank[:, 0, 0:P])
                for hf in range(2):
                    act.wait_ge(*wt_done.at(2 + hf))
                    act.copy(y_feat[:, hf * HF:(hf + 1) * HF], bank[:, 1 + hf, :])
        signals.settle()

    tern_i = sb("tern_i", [P, P], I32)
    tern_f = sb("tern_f", [P, P])
    tern_w = sb("tern_w", [P, P])

    def keep_stage():
        with nc.Block() as block:
            @block.gpsimd
            def _(pool):
                pool.tensor_copy(x_keep[:, :, :], x_tok[:, :, :])

    def prepare_stage():
        with nc.Block() as block:
            @block.vector
            def _(dve):
                step = steps(dve, signals("dve_step"))
                dve.wait_ge(loads["ld_w"], 16)
                step(dve.memset(ones128[:, :], 1.0))
                dve.scalar_tensor_tensor(out=route_w[:, :], in0=W("l0_keys"), scalar=2.0, in1=W("l0_rw"),
                                         op0=ALU.mult, op1=ALU.add)

        signals.settle()

    def pair_stage():
        with nc.Block() as block:
            @block.vector
            def _(dve):
                for p_ in range(8):
                    for a in range(2):
                        dve.tensor_scalar(sel[:, p_, a * 64:(a + 1) * 64], ones128[:, 0:64],
                                          K("sel")[:, 2 * p_ + a:2 * p_ + a + 1], None, ALU.mult)

    def widen_stage():
        ready = signals("prep")
        with nc.Block() as block:
            @block.gpsimd
            def _(pool):
                pool.memset(operands[:, :, :], 0.0).then_inc(*ready.up())
                pool.wait_ge(*ready.at(1))
                for b in range(B):
                    pool.memset(wide_k[64:65, b, 0, :], 1.0)
                    pool.memset(wide_k[0:1, b, 1, :], 1.0)
        signals.settle()

    prepare_stage()
    rsD = float(DH) ** -0.5

    norm_stage(target="hat", affine=(C("l0_g"), C("l0_b")))
    project_stage(hat_feat, W("l0_qkv", 0, 128), W("l0_qkv", 128, 256), W("l0_qkv", 256, 384), C("l0_bqkv", 0),
                  C("l0_bqkv", 1), R("l0_bv"))
    attention_stage(rsD, guard=True)
    norm_stage([(att_feat[:, 0, :], W("l0_proj"))], bias=R("l0_bproj"))
    memory_stage()
    norm_stage([(y_feat, ident)])
    route_stage([(x_feat, route_w[:, :])], R("l0_rb"), 16, 4, True, distance=True)
    expert_stage(x_feat, 16, lambda e, f: ("l0_b1", e * 4 + f), W("l0_b2")[0:16, :])
    norm_stage([(y_feat, ident)])

    layer_loads.append("ld_w1")
    widen_stage()
    norm_stage(target="hat", affine=(C("l1_g"), None))
    for p_ in range(8):
        c = slice(p_ * P, (p_ + 1) * P)
        project_stage(hat_feat, W("l1_wq", c.start, c.stop), W("l1_wk", c.start, c.stop),
                      W("l1_wv", c.start, c.stop), None, None, None, K("l1_cos"), K("l1_sin"),
                      bilinear=W("l1_bil", c.start, c.stop), wide=True)
        attention_stage(WH ** -0.5, wide=True, chunk=p_)
    norm_stage([(att_feat[:, p_, :], W("l1_wo", p_ * P, p_ * P + P)) for p_ in range(8)])
    cross_stage("l1x", C("l1x_bq"), C("l1x_bk"), R("l1x_bv"),
                lambda raw: (mask1_in.rearrange("a b (t p) k -> p (a b t) k", p=P), raw[:, 0:QT, :].bitcast(I32)),
                "q", H, rsD, 1e9 / rsD, lambda t: t % QT)
    norm_stage([(att_feat[:, 0, :], W("l1x", 384, 512))], bias=R("l1x_bo"))
    ternary_stage()
    norm_stage([(y_feat, tern_w[:, :])], bias=R("l1f_bias"))

    project_stage(x_feat, W("l2_attn", 0, 128), W("l2_attn", 128, 256), W("l2_attn", 256, 384), None, None, None,
                  K("l2_cos"), K("l2_sin"))
    attention_stage(rsD, causal=True)
    norm_stage([(att_feat[:, 0, :], W("l2_attn", 384, 512))])
    cross_stage("l2x", None, None, None,
                lambda raw: (mask2_in.rearrange("a b (t p) k -> p (a b t) k", p=P), raw[:, :, :].bitcast(I32)),
                "bq", H, D ** -0.5, 1e20, lambda t: t)
    norm_stage([(att_feat[:, 0, :], W("l2x", 384, 512))], bias=R("l2x_bo"))
    keep_stage()
    for l in range(4):
        norm_stage(target="hat")
        route_stage([(x_feat, W("l2_rw", 4 * l, 4 * l + 4))], R("l2_rb", 4 * l, 4 * l + 4), 4, 2, True)
        expert_stage(hat_feat, 4, lambda e, f, l=l: ("l2_b1", l * 16 + e * 4 + f), W("l2_b2", l * P, l * P + P)[0:16, :],
                     affine=lambda e, l=l: (C("l2_g", l * 4 + e), C("l2_b", l * 4 + e)))
        norm_stage([(y_feat, ident)], residual_scale=gate_sum, norm=(l == 3), plus=x_keep if l == 3 else None)

    layer_loads.append("ld_w3")
    project_stage(x_feat, W("l3_qkv", 0, 128), W("l3_qkv", 128, 256), W("l3_qkv", 256, 384), C("l3_bqkv", 0),
                  C("l3_bqkv", 1), R("l3_bv"), K("l3_cos").broadcast_to([P, HF]), K("l3_sin").broadcast_to([P, HF]))
    attention_stage(rsD)
    norm_stage([(att_feat[:, 0, :], W("l3_fc"))], bias=R("l3_bfc"))
    cross_stage("l3x", C("l3x_bq"), C("l3x_bk"), R("l3x_bv"),
                lambda raw: (mask3_in.rearrange("b k -> (b k)").partition_broadcast(P),
                             raw[:, 0, :].bitcast(U8)[:, 0:B * SC]),
                "b", 1, D ** -0.5, 1e9 * D ** 0.5, lambda t: t // QT)
    norm_stage([(att_feat[:, 0, :], W("l3x", 384, 512))], bias=R("l3x_bo"))
    route_stage([(x_feat, W("l3_wg"))], None, 16, 2, False)
    pair_stage()
    gated_stage()
    norm_stage([(y_feat, ident)], store=True)
    ctx.close()



def pack(parts, values, shape):
    out = np.zeros(shape, np.float32)
    at = 0
    for name, n in parts:
        v = values[name]
        out[:v.shape[0], at:at + n] = v
        at += n
    return out


def kernel(**inputs):
    import concourse.bacc as bacc
    from concourse.bass_utils import run_bass_kernel_spmd as run

    a = {n: np.asarray(v) for n, v in inputs.items()}

    def chunks(w):
        return w.reshape(-1, P, w.shape[-1]).transpose(1, 0, 2).reshape(P, -1)

    bil = np.zeros((P, 8, P), np.float32)
    for p_ in range(8):
        bil[0:64, p_, 0:64] = a["L1_attn_W_bilinear"][2 * p_]
        bil[64:128, p_, 64:128] = a["L1_attn_W_bilinear"][2 * p_ + 1]
    w1 = a["L3_ffn_W1"].reshape(8, 2, P, 2, 64).transpose(2, 0, 3, 1, 4).reshape(P, -1)
    b2 = np.zeros((P, 4, P), np.float32)
    b2[0:4] = a["L2_ffn_b2"].transpose(1, 0, 2)
    weights = {
        "l0_qkv": a["L0_attn_W_qkv"], "l0_proj": a["L0_attn_W_proj"], "l0_conv": chunks(a["L0_xattn_conv_w"].reshape(512, P)),
        "l0_keys": a["L0_ffn_keys"].T, "l0_rw": a["L0_ffn_rw"].T, "l0_b2": a["L0_ffn_b2"],
        "l1_wq": a["L1_attn_Wq"], "l1_wk": a["L1_attn_Wkv"][:, :1024], "l1_wv": a["L1_attn_Wkv"][:, 1024:],
        "l1_bil": bil.reshape(P, -1), "l1_wo": chunks(a["L1_attn_Wo"]),
        "l1x": np.concatenate([a[f"L1_xattn_W{n}"].T for n in "qkvo"], 1),
        "l2_attn": np.concatenate([a[f"L2_attn_{n}w"] for n in "qkvo"], 1),
        "l2x": np.concatenate([a[f"L2_xattn_W{n}"].T for n in "qkvo"], 1),
        "l2_rw": a["L2_ffn_router_w"].transpose(1, 0, 2).reshape(P, 16), "l2_b2": b2.reshape(P, -1),
        "l3_qkv": a["L3_attn_w_qkv"], "l3_fc": a["L3_attn_w_fc"],
        "l3x": np.concatenate([a[f"L3_xattn_W{n}"] for n in "qkvo"], 1),
        "l3_wg": a["L3_ffn_Wg"].T, "l3_w1": w1, "l3_w2": chunks(a["L3_ffn_W2"].reshape(1024, P)),
        "l3_ws1": a["L3_ffn_Ws1"], "l3_ws2": a["L3_ffn_Ws2"],
    }
    cols = {
        "l0_g": a["L0_attn_ln_gamma"], "l0_b": a["L0_attn_ln_beta"], "l0_bqkv": a["L0_attn_b_qkv"],
        "conv_b": a["L0_xattn_conv_b"], "l0_b1": a["L0_ffn_b1"], "l1_g": a["L1_attn_gamma"],
        "l1x_bq": a["L1_xattn_bq"], "l1x_bk": a["L1_xattn_bk"], "l2_g": a["L2_ffn_ln_g"], "l2_b": a["L2_ffn_ln_b"],
        "l2_b1": a["L2_ffn_b1"], "l3_bqkv": a["L3_attn_b_qkv"], "l3x_bq": a["L3_xattn_bq"],
        "l3x_bk": a["L3_xattn_bk"],
    }
    cols = {n: v.reshape(-1, P).T for n, v in cols.items()}
    rows = {
        "l0_bv": a["L0_attn_b_qkv"][256:], "l0_bproj": a["L0_attn_b_proj"], "l0_rb": a["L0_ffn_rb"],
        "l1x_bv": a["L1_xattn_bv"], "l1x_bo": a["L1_xattn_bo"], "l1f_bias": a["L1_ffn_bias"],
        "l1f_scale": a["L1_ffn_weight_scale"], "l2x_bo": a["L2_xattn_bo"], "l2_rb": a["L2_ffn_router_b"].reshape(-1),
        "l3_bv": a["L3_attn_b_qkv"][256:], "l3_bfc": a["L3_attn_b_fc"], "l3x_bv": a["L3_xattn_bv"],
        "l3x_bo": a["L3_xattn_bo"],
    }
    w2_0 = a["L0_ffn_w2"].transpose(0, 2, 1).reshape(16, 4, P, P).transpose(0, 2, 1, 3).reshape(16, P, 512)
    w2_2 = a["L2_ffn_w2"].reshape(16, 4, P, P).transpose(0, 2, 1, 3).reshape(16, P, 512)
    arrays = {
        "x": a["x"], "context": a["ctx_1024"], "mask1": a["mask_1x1xSxS2_if1"], "mask2": a["mask_Bx1xSxS2_ik1"],
        "mask3": a["mask_BxS2_bk0"], "packed": a["L1_ffn_packed_weight"],
        "constants": shape_constants(), "weights": pack(WEIGHTS, weights, (P, W_N)),
        "weights1": pack(WEIGHTS_1, weights, (P, W1_N)), "weights3": pack(WEIGHTS_3, weights, (P, W3_N)),
        "cols": pack(COLS, cols, (P, C_N)), "rows": np.concatenate([rows[n] for n, _ in ROWS]),
        "experts0": np.concatenate([a["L0_ffn_w1"].transpose(0, 2, 1), w2_0], 2),
        "experts2": np.concatenate([a["L2_ffn_w1"].reshape(16, P, 512), w2_2], 2),
    }
    nc = bacc.Bacc("TRN2", target_bir_lowering=False, num_devices=1)
    arrays = {f"in_{n}": np.ascontiguousarray(v) for n, v in arrays.items()}
    args = [nc.dram_tensor(n, v.shape, mybir.dt.from_np(v.dtype), kind="ExternalInput").ap()
            for n, v in arrays.items()]
    out = nc.dram_tensor("out_x", (B, S, D), F32, kind="ExternalOutput").ap()
    build(nc, *args, out)
    return run(nc, [arrays], core_ids=[0]).results[0]["out_x"]
```

```python
from contextlib import ExitStack

import concourse.bass as bass
from concourse import mybir
import numpy as np

F32 = mybir.dt.float32
F32R = mybir.dt.float32r
BF16 = mybir.dt.bfloat16
I32 = mybir.dt.int32
U8 = mybir.dt.uint8
ACT = mybir.ActivationFunctionType
ALU = mybir.AluOpType
X_AXIS = mybir.AxisListType.X

P = 128
B, S, D = 2, 512, 128
T = B * S
NT = T // P
QT = S // P
SC = 77
H, DH = 16, 8
WH = 64
HF = 512
EPS = 1e-5
HUGE = 3.0e38


WEIGHTS = [
    ("l0_qkv", 384), ("l0_proj", 128), ("l0_conv", 512), ("l0_keys", 16), ("l0_rw", 16), ("l0_b2", 128),
    ("l1x", 512), ("l2_attn", 512), ("l2x", 512), ("l2_rw", 16), ("l2_b2", 512), ("l3x", 512),
]
WEIGHTS_1 = [
    ("l1_wq", 1024), ("l1_wk", 1024), ("l1_wv", 1024), ("l1_bil", 1024), ("l1_wo", 1024),
]
WEIGHTS_3 = [
    ("l3_qkv", 384), ("l3_fc", 128), ("l3_wg", 16), ("l3_w1", 2048), ("l3_w2", 1024),
    ("l3_ws1", 256), ("l3_ws2", 128),
]
COLS = [
    ("l0_g", 1), ("l0_b", 1), ("l0_bqkv", 3), ("conv_b", 1), ("l0_b1", 64), ("l1_g", 1), ("l1x_bq", 1),
    ("l1x_bk", 1), ("l2_g", 16), ("l2_b", 16), ("l2_b1", 64), ("l3_bqkv", 3), ("l3x_bq", 1), ("l3x_bk", 1),
]
ROWS = [
    ("l0_bv", 128), ("l0_bproj", 128), ("l0_rb", 16), ("l1x_bv", 128), ("l1x_bo", 128), ("l1f_bias", 128),
    ("l1f_scale", 1), ("l2x_bo", 128), ("l2_rb", 16), ("l3_bv", 128), ("l3_bfc", 128), ("l3x_bv", 128),
    ("l3x_bo", 128),
]
CONSTS = [
    ("ident", 128), ("rot", 128), ("headmask", 16), ("sel", 16), ("marks", 4), ("stack", 4), ("causal_s", 128),
    ("causal_st", 128), ("l1_cos", 512), ("l1_sin", 512), ("l2_cos", 512), ("l2_sin", 512), ("l3_cos", 1),
    ("l3_sin", 1),
]


def offsets(parts):
    at, out = 0, {}
    for name, n in parts:
        out[name] = (at, n)
        at += n
    return out, at


W_AT, W_N = offsets(WEIGHTS)
W1_AT, W1_N = offsets(WEIGHTS_1)
W3_AT, W3_N = offsets(WEIGHTS_3)
C_AT, C_N = offsets(COLS)
R_AT, R_N = offsets(ROWS)
K_AT, K_N = offsets(CONSTS)

CAUSAL = -1.0e10


def shape_constants():
    k = np.zeros((P, K_N), np.float32)

    def put(name, a):
        at, n = K_AT[name]
        k[:, at:at + n] = a

    put("ident", np.eye(P))
    rot = np.zeros((P, P))
    for i in range(0, P, 2):
        rot[i + 1, i] = -1.0
        rot[i, i + 1] = 1.0
    put("rot", rot)
    feature = np.arange(P)
    put("headmask", feature[:, None] // DH == np.arange(H)[None, :])
    row = np.arange(P)[:, None]
    put("sel", (row == np.arange(16)) | (row == 32 + np.arange(16)))
    put("marks", (row == 96 + np.arange(4)) | (row == 100 + np.arange(4)))
    put("stack", (row % 32 // DH == np.arange(4)) & (row < 96))
    token = np.arange(P)
    put("causal_s", np.where(token[None, :] > token[:, None], CAUSAL * np.sqrt(DH), 0.0))
    put("causal_st", np.where(token[:, None] > token[None, :], CAUSAL * np.sqrt(DH), 0.0))
    pos = np.arange(S, dtype=np.float32)
    theta = (1.0 / np.float32(10000.0) ** (np.arange(0, WH, 2, dtype=np.float32) / np.float32(WH))).astype(np.float32)
    freq = (pos[:, None] * theta[None, :]).astype(np.float32)
    emb = np.concatenate([freq, freq], -1).T
    put("l1_cos", np.tile(np.cos(emb), (2, 1)))
    put("l1_sin", np.tile(np.sin(emb), (2, 1)))
    inv = (1.0 / np.float32(10000.0) ** (np.arange(0, DH, 2, dtype=np.float32) / np.float32(DH))).astype(np.float32)
    f2 = np.repeat((pos[:, None] * inv[None, :]).astype(np.float32).T, 2, axis=0)
    put("l2_cos", np.tile(np.cos(f2), (H, 1)))
    put("l2_sin", np.tile(np.sin(f2), (H, 1)))
    f3 = np.repeat(np.arange(H, dtype=np.float32)[:, None] * inv[None, :], 2, axis=1).reshape(P, 1)
    put("l3_cos", np.cos(f3))
    put("l3_sin", np.sin(f3))
    return k


class Signal:

    def __init__(self, nc, name):
        self.sem = nc.alloc_semaphore(name)
        self.base = 0
        self.total = 0

    def up(self, n=1):
        self.total += n
        return self.sem, n

    def at(self, n):
        return self.sem, self.base + n


class Signals:
    def __init__(self, nc):
        self.nc, self.by_name = nc, {}

    def __call__(self, name):
        if name not in self.by_name:
            self.by_name[name] = Signal(self.nc, name)
        return self.by_name[name]

    def settle(self):
        for s in self.by_name.values():
            s.base = s.total


def build(nc, x_in, ctx_in, mask1_in, mask2_in, mask3_in, packed_in, const_in, weights_in, weights1_in, weights3_in, cols_in,
          rows_in,           l0_experts, l2_experts, out):
    ctx = ExitStack()

    def sb(name, shape, dt=F32):
        return ctx.enter_context(nc.sbuf_tensor(name, shape, dt))

    signals = Signals(nc)
    bank = ctx.enter_context(nc.psum_tensor("bank", [P, 8, HF], F32))

    consts = sb("consts", [P, K_N])
    weights = sb("weights", [P, W_N])
    weights13 = sb("weights13", [P, max(W1_N, W3_N)])
    cols = sb("cols", [P, C_N])
    rows = sb("rows", [P, R_N])

    def K(name):
        at, n = K_AT[name]
        return consts[:, at:at + n]

    def W(name, a=0, b=None):
        table, tile = (W_AT, weights) if name in W_AT else (W1_AT if name in W1_AT else W3_AT, weights13)
        at, n = table[name]
        return tile[:, at + a:at + (n if b is None else b)]

    def C(name, i=0):
        at, _ = C_AT[name]
        return cols[:, at + i:at + i + 1]

    def R(name, a=0, b=None):
        at, n = R_AT[name]
        return rows[:, at + a:at + (n if b is None else b)]

    ident = K("ident")
    x_tok = sb("x_tok", [P, NT, D])
    x_feat = sb("x_feat", [P, T])
    hat_feat = sb("hat_feat", [P, T])
    y_feat = sb("y_feat", [P, T])
    stats = sb("stats", [P, NT, 6])
    moments = sb("moments", [P, NT, 2])
    rstd = sb("rstd", [P, NT])
    ctx_tok = sb("ctx_tok", [P, B, D])
    ctx_feat = sb("ctx_feat", [P, B * SC])
    identb = sb("identb", [P, P], BF16)
    causal_s = sb("causal_s", [P, P], BF16)
    causal_st = sb("causal_st", [P, P], BF16)
    ones32 = sb("ones32", [P, 32])
    q_feat = sb("q_feat", [P, T])
    k_feat = sb("k_feat", [P, T])
    operands = sb("operands", [P, 4, T])
    parts = {n: operands[:, i, :].bitcast(F32R) for i, n in enumerate(("q_hi", "q_lo", "k_hi", "k_lo"))}
    rot_tmp = y_feat
    res_tok = operands[:, 0, :].rearrange("p (t d) -> p t d", d=D)
    sum_tok = k_feat[:, :].rearrange("p (t d) -> p t d", d=D)
    KS = sb("KS", [P, 2, 4, HF], F32R)
    QM = sb("QM", [P, 2, HF], F32R)
    v_aug = sb("v_aug", [P, NT, H, 32])
    v_wide = v_aug[:, :, :, :].rearrange("p a b c -> p (a b c)")[:, 0:2 * T].rearrange(
        "p (s t n) -> p s t n", s=2, t=NT)
    probs = sb("probs", [P, 2, 4, HF])
    neg_max = sb("neg_max", [P, QT, 4])
    max_parts = sb("max_parts", [P, QT, 8], F32R)
    max_wide = sb("max_wide", [P, QT, P])
    o_feat = sb("o_feat", [P, HF])
    o_sums = sb("o_sums", [P, HF])
    o_tok = sb("o_tok", [P, B, QT, P])
    rsum = sb("rsum", [P, QT, 4])
    att_feat = sb("att_feat", [P, 8, T])
    NW = 4
    wring = probs[:, :, :, :].rearrange("p a b n -> p (a b n)").rearrange("p (w n) -> p w n", w=NW)
    sel = sb("sel", [P, 16, P], F32R)
    gate_parts = sb("gate_parts", [P, T], F32R)
    gate_rows = q_feat[0:16, :]

    def wide_q(slot, j):
        if slot == 0:
            return sel[:, :, :].rearrange("p a n -> p (a n)")[:, j * T:(j + 1) * T].rearrange("p (x n) -> p x n", x=2)
        return QM[:, :, :] if j == 0 else gate_parts[:, :].rearrange("p (x n) -> p x n", x=2)
    gates = sb("gates", [P, NT, 16])
    gate_sum = sb("gate_sum", [P, NT])

    flat = att_feat[:, :, :].rearrange("p a n -> p (a n)")
    scratch = flat[:, 2 * T:2 * T + 7 * HF]
    x_keep = att_feat[:, 7, :].rearrange("p (t d) -> p t d", d=D)
    zeros = o_sums
    lg = sb("lg", [P, NT, 24])
    lg_rep = sb("lg_rep", [P, NT, 24])
    top8 = sb("top8", [P, NT, 8])
    top_in = sb("top_in", [P, NT, 8])
    picked = sb("picked", [P, NT, 16])
    small = sb("small", [P, NT, 4])

    loads = {n: nc.alloc_semaphore(n) for n in ("ld_const", "ld_x", "ld_w", "ld_w1", "ld_w3", "ld_ctx")}
    expert_loaded = [nc.alloc_semaphore(f"expert_loaded{i}") for i in range(NW)]
    expert_total = [0]

    done_q = signals("dve_step")

    def steps(eng, sig):
        def step(ins):
            ins.then_inc(*sig.up())
            eng.wait_ge(sig.sem, sig.total)
        return step

    def constant_rows(dve):
        for j in range(4):
            for s in range(2):
                dve.tensor_scalar(KS[96:128, s, j, :], zeros[96:128, :], K("marks")[96:128, j:j + 1], None, ALU.add)
        for e in range(16):
            dve.tensor_scalar(sel[:, e, :], zeros[:, 0:P], K("sel")[:, e:e + 1], None, ALU.add)

    with nc.Block() as block:
        t_done, init_done = signals("t_done"), signals("init_done")

        @block.sync
        def _(sp):
            sp.dma_start(consts[:, :], const_in).then_inc(loads["ld_const"], 16)
            sp.dma_start(x_tok[:, :, :], x_in.rearrange("b (t p) d -> p (b t) d", p=P)).then_inc(loads["ld_x"], 16)
            sp.dma_start(cols[:, :], cols_in).then_inc(loads["ld_const"], 16)
            sp.dma_start(rows[:, :], rows_in.partition_broadcast(P)).then_inc(loads["ld_const"], 16)
            sp.dma_start(ctx_tok[0:SC, :, :], ctx_in.rearrange("b s d -> s b d")).then_inc(loads["ld_ctx"], 16)
            sp.dma_start(weights[:, :], weights_in).then_inc(loads["ld_w"], 16)
            sp.dma_start(weights13[:, 0:W1_N], weights1_in).then_inc(loads["ld_w1"], 16)

        @block.gpsimd
        def _(pool):
            pool.memset(KS[:, :, :, :].bitcast(F32), 0.0).then_inc(*init_done.up())
            pool.memset(QM[:, :, :].bitcast(F32), 0.0)
            pool.memset(v_aug[:, :, :, :], 0.0).then_inc(*init_done.up())
            pool.memset(max_wide[:, :, :], 0.0)
            pool.memset(ones32[:, :], 1.0)
            pool.memset(gate_parts[:, :].bitcast(F32), 0.0)
            pool.memset(zeros[:, :], 0.0).then_inc(*init_done.up())
            pool.wait_ge(*init_done.at(3))
            pool.memset(v_aug[:, :, :, DH:DH + 1], 1.0)

        @block.vector
        def _(dve):
            dve.wait_ge(loads["ld_const"], 48)
            dve.tensor_copy(identb[:, :], ident)
            dve.tensor_copy(causal_s[:, :], K("causal_s"))
            dve.tensor_copy(causal_st[:, :], K("causal_st"))
            dve.wait_ge(*init_done.at(3))
            constant_rows(dve)

        @block.tensor
        def _(pe):
            pe.wait_ge(loads["ld_const"], 48)
            pe.wait_ge(loads["ld_x"], 16)
            for hf in range(2):
                for q in range(QT):
                    ins = pe.transpose(bank[:, hf, q * P:(q + 1) * P], x_tok[:, hf * QT + q, :], ident)
                ins.then_inc(*t_done.up())
            pe.wait_ge(loads["ld_ctx"], 16)
            for b in range(B):
                ins = pe.transpose(bank[:, 2, b * SC:(b + 1) * SC], ctx_tok[0:SC, b, :], ident[0:SC, 0:SC])
            ins.then_inc(*t_done.up())

        @block.scalar
        def _(act):
            for hf in range(2):
                act.wait_ge(*t_done.at(hf + 1))
                act.copy(x_feat[:, hf * HF:(hf + 1) * HF], bank[:, hf, :])
            act.wait_ge(*t_done.at(3))
            act.copy(ctx_feat[:, :], bank[:, 2, 0:B * SC])
    signals.settle()

    def weights_here(pe):
        pe.wait_ge(loads["ld_w"], 16)
        for name in layer_loads:
            pe.wait_ge(loads[name], 16)

    layer_loads = []

    def norm_stage(terms=None, bias=None, residual_scale=None, norm=True, target="x", affine=None, store=False,
                   plus=None):
        y_done, res_done, std_in, std_out, tok_done, t_done = (
            signals(n) for n in ("y_done", "res_done", "std_in", "std_out", "tok_done", "t_done"))
        step_sig = signals("dve_step")
        dest = x_tok if target == "x" else sum_tok
        feat = x_feat if target == "x" else hat_feat
        stored = signals("stored")
        with nc.Block() as block:
            if terms is not None:
                @block.gpsimd
                def _(pool):
                    if bias is not None:
                        for hf in range(2):
                            half = slice(hf * QT, (hf + 1) * QT)
                            pool.tensor_tensor(res_tok[:, half, :], x_tok[:, half, :],
                                               bias.unsqueeze(1).broadcast_to([P, QT, D]), ALU.add
                                               ).then_inc(*res_done.up())

            @block.tensor
            def _(pe):
                weights_here(pe)
                if terms is not None:
                    for hf in range(2):
                        for q in range(QT):
                            t = hf * QT + q
                            for n, (operand, w) in enumerate(terms):
                                ins = pe.matmul(bank[:, hf, q * P:(q + 1) * P], operand[:, t * P:(t + 1) * P], w,
                                                start=(n == 0), stop=(n == len(terms) - 1))
                        ins.then_inc(*y_done.up())
                for hf in range(2):
                    pe.wait_ge(*tok_done.at(hf + 1))
                    for q in range(QT):
                        t = hf * QT + q
                        ins = pe.transpose(bank[:, 2 + hf, q * P:(q + 1) * P], dest[:, t, :], ident)
                    ins.then_inc(*t_done.up())

            @block.vector
            def _(dve):
                step = steps(dve, step_sig)
                for hf in range(2):
                    half = slice(hf * QT, (hf + 1) * QT)
                    y = bank[:, hf, :].rearrange("p (q d) -> p q d", d=D)
                    if terms is not None:
                        dve.wait_ge(*y_done.at(hf + 1))
                        into = sum_tok if norm else x_tok
                        if residual_scale is not None:
                            for q in range(QT):
                                ins = dve.scalar_tensor_tensor(out=into[:, hf * QT + q, :],
                                                               in0=x_tok[:, hf * QT + q, :],
                                                               scalar=residual_scale[:, hf * QT + q:hf * QT + q + 1],
                                                               in1=y[:, q, :], op0=ALU.mult, op1=ALU.add)
                        else:
                            if bias is not None:
                                dve.wait_ge(*res_done.at(hf + 1))
                            ins = dve.tensor_tensor(into[:, half, :], y,
                                                    (res_tok if bias is not None else x_tok)[:, half, :], ALU.add)
                        if not norm:
                            ins.then_inc(*tok_done.up())
                            continue
                        step(ins)
                        if plus is not None:
                            step(dve.tensor_tensor(into[:, half, :], into[:, half, :], plus[:, half, :], ALU.add))
                    source = sum_tok if terms is not None else x_tok
                    for q in range(QT):
                        ins = dve.bn_stats(stats[:, hf * QT + q, :], source[:, hf * QT + q, :])
                    step(ins)
                    for q in range(QT):
                        ins = dve.bn_aggr(moments[:, hf * QT + q, :], stats[:, hf * QT + q, :])
                    step(ins)
                    dve.tensor_scalar(rstd[:, half], moments[:, half, 1], EPS, None, ALU.add
                                      ).then_inc(*std_in.up())
                    dve.wait_ge(*std_out.at(hf + 1))
                    step(dve.reciprocal(rstd[:, half], rstd[:, half]))
                    for q in range(QT):
                        t = hf * QT + q
                        ins = dve.tensor_scalar(dest[:, t, :], source[:, t, :], moments[:, t, 0:1], rstd[:, t:t + 1],
                                                ALU.subtract, ALU.mult)
                    ins.then_inc(*tok_done.up())

            @block.scalar
            def _(act):
                if norm:
                    for hf in range(2):
                        act.wait_ge(*std_in.at(hf + 1))
                        act.activation(rstd[:, hf * QT:(hf + 1) * QT], rstd[:, hf * QT:(hf + 1) * QT],
                                       ACT.Sqrt).then_inc(*std_out.up())
                for hf in range(2):
                    act.wait_ge(*t_done.at(hf + 1))
                    o = feat[:, hf * HF:(hf + 1) * HF]
                    if affine is not None and affine[1] is not None:
                        act.activation(o, bank[:, 2 + hf, :], ACT.Identity, bias=affine[1], scale=affine[0])
                    elif affine is not None:
                        act.activation(o, bank[:, 2 + hf, :], ACT.Copy, scale=affine[0])
                    else:
                        act.copy(o, bank[:, 2 + hf, :])

            if store:
                @block.sync
                def _(sp):
                    view = out.rearrange("b (t p) d -> p (b t) d", p=P)
                    for hf in range(2):
                        sp.wait_ge(*tok_done.at(hf + 1))
                        half = slice(hf * QT, (hf + 1) * QT)
                        sp.dma_start(view[:, half, :], x_tok[:, half, :]).then_inc(*stored.up(16))
                    sp.wait_ge(*stored.at(32))
        signals.settle()

    def project_stage(source, wq, wk, wv, bq, bk, bv, cos=None, sin=None, bilinear=None, wide=False):
        proj, proj_used, raw, v_done, rotated, rot_used = (
            signals(n) for n in ("proj", "proj_used", "raw", "v_done", "rotated", "rot_used"))
        final, hi_done, bil_in = signals("final"), signals("hi_done"), signals("bil_in")
        step_sig = signals("dve_step")
        rotary = cos is not None
        ready = {}
        items = [(n, hf) for n in range(2) for hf in range(2)]
        feats = (q_feat, k_feat)

        with nc.Block() as block:
            @block.tensor
            def _(pe):
                weights_here(pe)
                for i, (n, hf) in enumerate(items):
                    pe.matmul(bank[:, i, :], (wq, wk)[n], source[:, hf * HF:(hf + 1) * HF], start=True,
                              stop=True).then_inc(*proj.up())
                for t in range(NT):
                    ins = pe.matmul(bank[:, 6 + t // QT, (t % QT) * P:(t % QT + 1) * P], source[:, t * P:(t + 1) * P],
                                    wv, start=True, stop=True)
                    if t % QT == QT - 1:
                        ins.then_inc(*v_done.up())
                if rotary:
                    for i, (n, hf) in enumerate(items):
                        pe.wait_ge(*raw.at(i + 1))
                        if i >= 2:
                            pe.wait_ge(*rot_used.at(i - 1))
                        pe.matmul(bank[:, 4 + i % 2, :], K("rot"), feats[n][:, hf * HF:(hf + 1) * HF], start=True,
                                  stop=True).then_inc(*rotated.up())
                if bilinear is not None:
                    for hf in range(2):
                        pe.wait_ge(*rot_used.at(3 + hf))
                        pe.matmul(bank[:, hf, :], bilinear, k_feat[:, hf * HF:(hf + 1) * HF], start=True,
                                  stop=True).then_inc(*bil_in.up())

            @block.scalar
            def _(act):
                for i, (n, hf) in enumerate(items):
                    act.wait_ge(*proj.at(i + 1))
                    bias = (bq, bk)[n]
                    o = feats[n][:, hf * HF:(hf + 1) * HF]
                    if bias is not None:
                        ins = act.activation(o, bank[:, i, :], ACT.Identity, bias=bias)
                    else:
                        ins = act.copy(o, bank[:, i, :])
                    ins.then_inc(*raw.up())
                if wide:
                    for hf in range(2):
                        act.wait_ge(*rot_used.at(1 + hf))
                        for a, r in ((0, 0), (1, 64)):
                            act.copy(wide_q[r:r + 64, hf, a, :], q_feat[r:r + 64, hf * HF:(hf + 1) * HF])
                    for hf in range(2):
                        act.wait_ge(*bil_in.at(1 + hf))
                        for a, r in ((0, 0), (1, 64)):
                            act.copy(wide_k[r:r + 64, hf, a, :], bank[r:r + 64, hf, :])
                else:
                    for i, (n, hf) in enumerate(items):
                        act.wait_ge(*(rot_used if rotary else raw).at(i + 1))
                        hi = parts[("q_hi", "k_hi")[n]]
                        act.copy(hi[:, hf * HF:(hf + 1) * HF], feats[n][:, hf * HF:(hf + 1) * HF]
                                 ).then_inc(*hi_done.up())

            @block.vector
            def _(dve):
                step = steps(dve, step_sig)
                for hf in range(2):
                    dve.wait_ge(*v_done.at(hf + 1))
                    half = slice(hf * QT, (hf + 1) * QT)
                    v = bank[:, 6 + hf, :]
                    if wide:
                        dve.tensor_copy(v_wide[:, half, :], v.rearrange("p (t n) -> p t n", n=P))
                        continue
                    for q in range(QT):
                        o = v_aug[:, hf * QT + q, :, 0:DH]
                        vq = v[:, q * P:(q + 1) * P].rearrange("p (h d) -> p h d", d=DH)
                        if bv is not None:
                            dve.tensor_tensor(o, vq, bv.rearrange("p (h d) -> p h d", d=DH), ALU.add)
                        else:
                            dve.tensor_copy(o, vq)
                if rotary:
                    for i, (n, hf) in enumerate(items):
                        f = feats[n][:, hf * HF:(hf + 1) * HF]
                        tmp = rot_tmp[:, hf * HF:(hf + 1) * HF]
                        dve.wait_ge(*rotated.at(i + 1))
                        dve.tensor_tensor(tmp, bank[:, 4 + i % 2, :], sin, ALU.mult)
                        step(dve.tensor_tensor(f, f, cos, ALU.mult))
                        dve.tensor_tensor(f, f, tmp, ALU.add).then_inc(*rot_used.up())
                if not wide:
                    for i, (n, hf) in enumerate(items):
                        dve.wait_ge(*hi_done.at(i + 1))
                        sl = slice(hf * HF, (hf + 1) * HF)
                        dve.tensor_tensor(parts[("q_lo", "k_lo")[n]][:, sl], feats[n][:, sl],
                                          parts[("q_hi", "k_hi")[n]][:, sl].bitcast(F32), ALU.subtract)

            if wide:
                @block.gpsimd
                def _(pool):
                    for hf in range(2):
                        pool.memset(wide_q[64:65, hf, 0, :], 0.0)
                        pool.memset(wide_q[0:1, hf, 1, :], 0.0)
        signals.settle()

    def wide_stage():
        units = [(p_, b) for p_ in range(8) for b in range(B)]
        NU, NG = len(units), 2 * QT
        MX, ST, PVB, SUMS, MISC, PJ = (0, 1), (2, 3), 4, 5, 6, 7
        Q, RQ, KK, RK, V, BIL = range(6)
        PIECE_AT = {0: Q, 1: RQ, 2: KK, 3: RK, 4: V, 5: BIL}
        MAXIMA_AT = {3: (0, 1), 4: (2, 3), 5: (4, 5), 6: (6, 7)}
        (proj_done, proj_read, cos_done, rot_done, hi_done, lo_done, m_clear, mx_done, mx_used, mp_done, mt_done,
         m_ready, st_done, exp_done, pv_done, res_copied, att_done) = (signals(n) for n in (
             "proj_done", "proj_read", "cos_done", "rot_done", "hi_done", "lo_done", "m_clear", "mx_done", "mx_used",
             "mp_done", "mt_done", "m_ready", "st_done", "exp_done", "pv_done", "res_copied", "att_done"))
        op_loaded = [[signals(f"op_loaded{s}{j}") for j in range(2)] for s in range(2)]
        step_sig = signals("dve_step")
        part_buf = operands[:, :, :].rearrange("p n t -> p (n t)").rearrange("p (s n t) -> p s n t", s=2, n=4)
        cos_buf = o_tok[:, :, :, :].rearrange("p b q d -> p (b q d)").rearrange("p (n t) -> p n t", n=2)
        rot_buf = rot_tmp[:, :].rearrange("p (n t) -> p n t", n=2)

        def slot(u):
            return u % 2

        def raw(u, n):
            return (q_feat, k_feat)[n][:, slot(u) * HF:(slot(u) + 1) * HF]

        def part(u, n, low):
            return part_buf[:, slot(u), 2 * n + low, :]

        def q_tile(u, j, ab):
            return wide_q(slot(u), j)[:, ab, :]

        def k_tile(u, j, ab):
            return KS[:, slot(u), 2 * j + ab, :]

        def values_of(u):
            return v_wide[:, (u // 2) % 2, :, :]

        with nc.Block() as block:
            @block.sync
            def _(sp):
                for u in range(NU):
                    sp.wait_ge(*lo_done.at(2 * u + 2))
                    if u >= 2:
                        sp.wait_ge(*st_done.at((u - 1) * NG))
                    for j in range(2):
                        own, other = slice(64 * j, 64 * j + 64), slice(64 - 64 * j, 128 - 64 * j)
                        q_hi, q_lo, k_hi, k_lo = (part(u, n, low)[own, :] for n in range(2) for low in range(2))
                        moves = [(q_tile(u, j, 0)[own, :], q_hi), (q_tile(u, j, 1)[own, :], q_hi),
                                 (q_tile(u, j, 0)[other, :], q_lo),
                                 (k_tile(u, j, 0)[own, :], k_hi), (k_tile(u, j, 0)[other, :], k_hi),
                                 (k_tile(u, j, 1)[own, :], k_lo)]
                        for to, src in moves:
                            sp.dma_start(to.bitcast(F32), src).then_inc(*op_loaded[slot(u)][j].up(16))

            @block.tensor
            def _(pe):
                weights_here(pe)

                def project(u, piece):
                    p_, b = units[u]
                    c = slice(p_ * P, (p_ + 1) * P)
                    x = hat_feat[:, b * S:(b + 1) * S]
                    if 6 * u + piece:
                        pe.wait_ge(*proj_read.at(6 * u + piece))
                    if piece == BIL:
                        pe.wait_ge(*rot_done.at(2 * u + 2))
                    if piece == V:
                        for q in range(QT):
                            ins = pe.matmul(bank[:, PJ, q * P:(q + 1) * P], x[:, q * P:(q + 1) * P],
                                            W("l1_wv", c.start, c.stop), start=True, stop=True)
                    else:
                        w, operand = {Q: (W("l1_wq", c.start, c.stop), x), KK: (W("l1_wk", c.start, c.stop), x),
                                      RQ: (K("rot"), raw(u, 0)), RK: (K("rot"), raw(u, 1)),
                                      BIL: (W("l1_bil", c.start, c.stop), raw(u, 1))}[piece]
                        ins = pe.matmul(bank[:, PJ, :], w, operand, start=True, stop=True)
                    ins.then_inc(*proj_done.up())

                def maxima(u, i):
                    j, q = divmod(i, QT)
                    n = u * NG + i
                    if q == 0:
                        pe.wait_ge(*op_loaded[slot(u)][j].at(96 * (u // 2 + 1)))
                    if i == 0:
                        pe.wait_ge(*m_clear.at(u + 1))
                    if n >= 2:
                        pe.wait_ge(*mx_used.at(n - 1))
                    for ab in range(2):
                        ins = pe.matmul(bank[:, MX[n % 2], :], q_tile(u, j, ab)[:, q * P:(q + 1) * P],
                                        k_tile(u, j, ab), start=(ab == 0), stop=(ab == 1))
                    ins.then_inc(*mx_done.up())

                def turn_maxima(u):
                    pe.wait_ge(*mp_done.at(u + 1))
                    for q in range(QT):
                        ins = pe.transpose(bank[:, MISC, q * P:(q + 1) * P], max_wide[:, q, :], ident)
                    ins.then_inc(*mt_done.up())

                def scores(u, n):
                    kt, j = divmod(n, 2)
                    m = u * NG + n
                    if n == 0:
                        pe.wait_ge(*m_ready.at(u + 1))
                    if m >= 2:
                        pe.wait_ge(*exp_done.at(m - 1))
                    for ab in range(2):
                        ins = pe.matmul(bank[:, ST[m % 2], :], k_tile(u, j, ab)[:, kt * P:(kt + 1) * P],
                                        q_tile(u, j, ab), start=(ab == 0), stop=(ab == 1))
                    ins.then_inc(*st_done.up())

                def values(u, kt):
                    p_, b = units[u]
                    pe.wait_ge(*exp_done.at(u * NG + 2 * kt + 2))
                    if kt == 0 and u >= 1:
                        pe.wait_ge(*res_copied.at(u))
                    for to, operand in ((PVB, values_of(u)[:, b * QT + kt, :]), (SUMS, ones128)):
                        for j in range(2):
                            r = slice(64 * j, 64 * j + 64)
                            ins = pe.matmul(bank[r, to, :], operand[:, r], probs[:, kt % 2, j, :],
                                            start=(kt == 0), stop=(kt == QT - 1))
                    ins.then_inc(*pv_done.up())

                for u in range(2):
                    for piece in range(6):
                        project(u, piece)
                for i in range(NG):
                    maxima(0, i)
                turn_maxima(0)
                for u in range(NU):
                    for n in range(NG):
                        scores(u, n)
                        if u + 1 < NU:
                            for i in MAXIMA_AT.get(n, ()):
                                maxima(u + 1, i)
                        if n in PIECE_AT and u + 2 < NU:
                            project(u + 2, PIECE_AT[n])
                        if n % 2 == 1 and u * QT + n // 2 >= 1:
                            values(*divmod(u * QT + n // 2 - 1, QT))
                        if n == NG - 1 and u + 1 < NU:
                            turn_maxima(u + 1)
                values(NU - 1, QT - 1)

            @block.scalar
            def _(act):
                def copy_piece(u, piece):
                    p_, b = units[u]
                    act.wait_ge(*proj_done.at(6 * u + piece + 1))
                    if piece == V:
                        act.copy(values_of(u)[:, b * QT:(b + 1) * QT, :],
                                 bank[:, PJ, :].rearrange("p (t n) -> p t n", n=P)).then_inc(*proj_read.up())
                    else:
                        act.copy(raw(u, 0 if piece == Q else 1), bank[:, PJ, :]).then_inc(*proj_read.up())

                def high(u, n):
                    if n == 0:
                        act.wait_ge(*rot_done.at(2 * u + 1))
                        act.copy(part(u, 0, 0).bitcast(F32R), raw(u, 0)).then_inc(*hi_done.up())
                    else:
                        act.wait_ge(*proj_done.at(6 * u + BIL + 1))
                        act.copy(part(u, 1, 0).bitcast(F32R), bank[:, PJ, :]).then_inc(*hi_done.up())

                def maxima_rows(u):
                    act.wait_ge(*mt_done.at(u + 1))
                    act.copy(q_tile(u, 0, 1)[64:66, :], bank[64:66, MISC, :])
                    act.copy(q_tile(u, 1, 1)[0:2, :], bank[0:2, MISC, :]).then_inc(*m_ready.up())

                def exponentials(u, n):
                    kt, j = divmod(n, 2)
                    m = u * NG + n
                    act.wait_ge(*st_done.at(m + 1))
                    if j == 0 and u * QT + kt >= 2:
                        act.wait_ge(*pv_done.at(u * QT + kt - 1))
                    act.activation(probs[:, kt % 2, j, :], bank[:, ST[m % 2], :], ACT.Exp, scale=WH ** -0.5
                                   ).then_inc(*exp_done.up())

                def copy_result(u):
                    act.wait_ge(*pv_done.at((u + 1) * QT))
                    if u >= 1:
                        act.wait_ge(*att_done.at(u))
                    act.copy(o_sums[:, :], bank[:, SUMS, :])
                    act.copy(o_feat[:, :], bank[:, PVB, :]).then_inc(*res_copied.up())

                for u in range(2):
                    copy_piece(u, Q)
                    copy_piece(u, KK)
                    high(u, 0)
                    copy_piece(u, V)
                    high(u, 1)
                maxima_rows(0)
                for u in range(NU):
                    for n in range(NG):
                        exponentials(u, n)
                        if u + 2 < NU:
                            if n in PIECE_AT and PIECE_AT[n] in (Q, KK, V):
                                copy_piece(u + 2, PIECE_AT[n])
                            if n == 3:
                                high(u + 2, 0)
                            if n == 5:
                                high(u + 2, 1)
                        if n == 1 and u >= 1:
                            copy_result(u - 1)
                        if n == NG - 1 and u + 1 < NU:
                            maxima_rows(u + 1)
                copy_result(NU - 1)

            @block.vector
            def _(dve):
                step = steps(dve, step_sig)

                def rotate(u, n):
                    dve.wait_ge(*proj_done.at(6 * u + (RQ, RK)[n] + 1))
                    ins = dve.tensor_tensor(rot_buf[:, n, :], bank[:, PJ, :], K("l1_sin"), ALU.mult)
                    ins.then_inc(*proj_read.up())
                    dve.wait_ge(*proj_read.at(6 * u + (RQ, RK)[n] + 1))
                    dve.wait_ge(*cos_done.at(2 * u + n + 1))
                    dve.tensor_tensor(raw(u, n), cos_buf[:, n, :], rot_buf[:, n, :], ALU.add).then_inc(*rot_done.up())

                def low(u, n):
                    dve.wait_ge(*hi_done.at(2 * u + n + 1))
                    if n == 0:
                        dve.tensor_tensor(part(u, 0, 1).bitcast(F32R), raw(u, 0), part(u, 0, 0), ALU.subtract
                                          ).then_inc(*lo_done.up())
                    else:
                        dve.tensor_tensor(part(u, 1, 1).bitcast(F32R), bank[:, PJ, :], part(u, 1, 0), ALU.subtract
                                          ).then_inc(*lo_done.up())
                        dve.wait_ge(*lo_done.at(2 * u + 2))
                        dve.sem_inc(*proj_read.up())

                def reduce_maxima(u, i):
                    j, q = divmod(i, QT)
                    n = u * NG + i
                    dve.wait_ge(*mx_done.at(n + 1))
                    dve.tensor_reduce(neg_max[:, q, 1 - j:2 - j], bank[:, MX[n % 2], :], X_AXIS, ALU.max,
                                      negate=True).then_inc(*mx_used.up())

                def split_maxima(u):
                    dve.wait_ge(*mx_used.at((u + 1) * NG))
                    if u >= 1:
                        dve.wait_ge(*mt_done.at(u))
                    hi, lo = max_wide[:, :, 0:65:64], max_wide[:, :, 1:66:64]
                    step(dve.tensor_copy(hi.bitcast(F32R), neg_max[:, :, 0:2]))
                    dve.tensor_tensor(lo.bitcast(F32R), neg_max[:, :, 0:2], hi, ALU.subtract
                                      ).then_inc(*mp_done.up())

                def invert(u, q):
                    if q == 0:
                        dve.wait_ge(*res_copied.at(u + 1))
                    sl = o_sums[:, q * P:(q + 1) * P]
                    ins = dve.reciprocal(sl, sl)
                    if q == QT - 1:
                        step(ins)

                def normalise(u):
                    p_, b = units[u]
                    dve.tensor_tensor(att_feat[:, p_, b * S:(b + 1) * S], o_feat[:, :], o_sums[:, :], ALU.mult
                                      ).then_inc(*att_done.up())

                for u in range(2):
                    rotate(u, 0)
                    rotate(u, 1)
                    low(u, 0)
                    low(u, 1)
                for i in range(NG):
                    reduce_maxima(0, i)
                split_maxima(0)
                for u in range(NU):
                    for n in range(NG):
                        if u + 1 < NU:
                            for i in MAXIMA_AT.get(n, ()):
                                reduce_maxima(u + 1, i)
                            if n == 6:
                                split_maxima(u + 1)
                        if u + 2 < NU:
                            if n in (1, 3):
                                rotate(u + 2, n // 2)
                            if n == 3:
                                low(u + 2, 0)
                            if n == 5:
                                low(u + 2, 1)
                        if u >= 1 and n in (2, 3, 4):
                            for q in {2: (0, 1), 3: (2,), 4: (3,)}[n]:
                                invert(u - 1, q)
                            if n == 4:
                                normalise(u - 1)
                for q in range(QT):
                    invert(NU - 1, q)
                normalise(NU - 1)

            @block.gpsimd
            def _(pool):
                step = steps(pool, signals("pool_step"))
                for s in range(2):
                    for j in range(2):
                        other = slice(64 - 64 * j, 128 - 64 * j)
                        step(pool.memset(wide_q(s, j)[other, 1, :].bitcast(F32), 0.0))
                        step(pool.memset(KS[other, s, 2 * j + 1, :].bitcast(F32), 1.0))
                    pool.sem_inc(*m_clear.up())
                for u in range(NU):
                    for n in range(2):
                        pool.wait_ge(*proj_read.at(6 * u + (Q, KK)[n] + 1))
                        if u >= 1:
                            pool.wait_ge(*rot_done.at(2 * u + n - 1))
                        pool.tensor_tensor(cos_buf[:, n, :], raw(u, n), K("l1_cos"), ALU.mult).then_inc(*cos_done.up())
                    if u >= 2:
                        pool.wait_ge(*st_done.at((u - 1) * NG))
                        pool.wait_ge(*cos_done.at(2 * u + 2))
                        step(pool.memset(q_tile(u, 0, 1)[64:66, :].bitcast(F32), 0.0))
                        step(pool.memset(q_tile(u, 1, 1)[0:2, :].bitcast(F32), 0.0))
                        pool.sem_inc(*m_clear.up())
        signals.settle()

    def attention_stage(scale, causal=False, wide=False, guard=False, chunk=0):
        NJ = 2 if wide else 4
        units = [(b, 0) for b in range(B)] if wide else [(b, g) for g in range(4) for b in range(B)]
        NU = len(units)
        MX_BANKS = [0, 1] if wide else [0, 1, 2]
        ST_BANKS = [2, 3] if wide else [3, 4, 5]
        NX, NS = len(MX_BANKS), len(ST_BANKS)
        NG = QT * NJ
        PVB, MISC, SUMS, SUMT = 6, 7, 5, 4
        LEAD = 1 if wide else 3
        TURN = NG - LEAD
        START = 0 if wide else 1
        COPY, RESULT, FLUSH = (1, 3, 5) if wide else (2, 5, 9)

        def maxima_of(n):
            a, w = n - START, TURN - START
            return range(a * NG // w, (a + 1) * NG // w) if 0 <= a < w else range(0)

        (mx_done, mx_used, mp_done, mt_done, m_ready, st_done, exp_done, pv_done, o_ready, ot_done, on_done,
         fl_done, fl_used, built, first_built) = (signals(n) for n in (
             "mx_done", "mx_used", "mp_done", "mt_done", "m_ready", "st_done", "exp_done", "pv_done", "o_ready",
             "ot_done", "on_done", "fl_done", "fl_used", "built", "first_built"))
        NB_ = 3
        base_loaded = [signals(f"base_loaded{i}") for i in range(NB_)]
        step_sig = signals("dve_step")

        def key_op(u, j):
            return wide_k[:, u, j, :] if wide else KS[:, u % 2, j, :]

        def query_op(u, j):
            return wide_q[:, u, j, :] if wide else QM[:, u % 2, :]

        def q_base(g):
            return att_feat[:, 1 + g % NB_, :]

        def k_base(g):
            return att_feat[:, 1 + NB_ + g % NB_, :]

        def flush_of(u):
            return wide or units[u][1] == 3

        NFL = NU if wide else B

        with nc.Block() as block:
            if not wide:
                @block.sync
                def _(sp):
                    for g in range(4):
                        if g >= NB_:
                            sp.wait_ge(*built.at(3 * B * (g - NB_ + 1)))
                            sp.wait_ge(*first_built.at(2 * B * (g - NB_ + 1)))
                        for base, names in ((q_base(g), ("q_hi", "q_lo", "q_hi")), (k_base(g), ("k_hi", "k_hi", "k_lo"))):
                            for blk, name in enumerate(names):
                                sp.dma_start(base[32 * blk:32 * blk + 32, :],
                                             parts[name][32 * g:32 * g + 32, :].bitcast(F32)
                                             ).then_inc(*base_loaded[g % NB_].up(16))

                @block.gpsimd
                def _(pool):
                    for u, (b, g) in enumerate(units):
                        s, tok = u % 2, slice(b * S, (b + 1) * S)
                        if b == 0:
                            pool.wait_ge(*base_loaded[g % NB_].at(96 * (g // NB_ + 1)))
                        if u >= 2:
                            pool.wait_ge(*st_done.at((u - 1) * NG))
                        for j in range(1, 4):
                            pool.tensor_scalar(KS[0:96, s, j, :], k_base(g)[0:96, tok], K("stack")[0:96, j:j + 1],
                                               None, ALU.mult).then_inc(*built.up())

            @block.tensor
            def _(pe):
                def max_step(u, i):
                    j, q = divmod(i, QT)
                    n = u * NJ * QT + i
                    if q == 0 and not wide:
                        if j == 0:
                            pe.wait_ge(*first_built.at(2 * u + 2))
                        else:
                            pe.wait_ge(*built.at(3 * u + j))
                    if n >= NX:
                        pe.wait_ge(*mx_used.at(n - NX + 1))
                    keys = (q + 1) * P if causal else S
                    kr = slice(0, P) if wide else slice(0, 96)
                    ins = pe.matmul(bank[:, MX_BANKS[n % NX], 0:keys], query_op(u, j)[kr, q * P:(q + 1) * P],
                                    key_op(u, j)[kr, 0:keys], start=True, stop=True)
                    if causal:
                        ins = pe.matmul(bank[:, MX_BANKS[n % NX], q * P:(q + 1) * P], identb[:, :], causal_s[:, :], start=False,
                                        stop=True, skip_group_check=True)
                    ins.then_inc(*mx_done.up())

                def misc_free(pe, units_done):
                    if units_done > 0:
                        pe.wait_ge(*on_done.at(units_done))
                    nf = sum(flush_of(v) for v in range(units_done))
                    if nf:
                        pe.wait_ge(*fl_used.at(nf))

                def turn_maxima(u):
                    pe.wait_ge(*mp_done.at(u + 1))
                    misc_free(pe, u - 1)
                    for q in range(QT):
                        if wide:
                            ins = pe.transpose(bank[:, MISC, q * P:(q + 1) * P], max_wide[:, q, :], ident)
                        else:
                            ins = pe.transpose(bank[0:8, MISC, q * P:(q + 1) * P], max_parts[:, q, :].bitcast(F32),
                                               ident)
                    ins.then_inc(*mt_done.up())

                def scores(u, n):
                    kt, j = divmod(n, NJ)
                    m = u * NG + n
                    if n == 0:
                        pe.wait_ge(*m_ready.at(u + 1))
                    if m >= NS:
                        pe.wait_ge(*exp_done.at(m - NS + 1))
                    lo = kt * P if causal else 0
                    st = bank[:, ST_BANKS[m % NS], :]
                    ins = pe.matmul(st[:, lo:S], key_op(u, j)[:, kt * P:(kt + 1) * P], query_op(u, j)[:, lo:S],
                                    start=True, stop=True)
                    if causal:
                        ins = pe.matmul(st[:, lo:lo + P], identb[:, :], causal_st[:, :], start=False, stop=True,
                                        skip_group_check=True)
                    ins.then_inc(*st_done.up())

                def values(u, kt):
                    b, g = units[u]
                    pe.wait_ge(*exp_done.at(u * NG + (kt + 1) * NJ))
                    if kt == 0 and u >= 1:
                        pe.wait_ge(*o_ready.at(u))
                    lo = kt * P if causal else 0
                    for j in range(NJ):
                        p = probs[:, kt % 2, j, lo:S]
                        if wide:
                            pe.matmul(bank[64 * j:64 * j + 64, PVB, lo:S], v_wide[:, b * QT + kt, 64 * j:64 * j + 64],
                                      p, start=(kt == 0), stop=(kt == QT - 1))
                        else:
                            ins = pe.matmul(bank[32 * j:32 * j + 32, PVB, lo:S],
                                            v_aug[:, b * QT + kt, 4 * g + j, :], p, start=(kt == 0),
                                            stop=(kt == QT - 1))
                    if wide:
                        for j in range(NJ):
                            ins = pe.matmul(bank[32 * j:32 * j + 32, SUMS, :], ones32[:, :], probs[:, kt % 2, j, :],
                                            start=(kt == 0), stop=(kt == QT - 1))
                    ins.then_inc(*pv_done.up())

                def turn_result(u):
                    pe.wait_ge(*o_ready.at(u + 1))
                    if u + 1 < NU:
                        pe.wait_ge(*m_ready.at(u + 2))
                    misc_free(pe, u)
                    for q in range(QT):
                        ins = pe.transpose(bank[:, MISC, q * P:(q + 1) * P], o_feat[:, q * P:(q + 1) * P], ident)
                    if wide:
                        for q in range(QT):
                            ins = pe.transpose(bank[:, SUMT, q * 64:(q + 1) * 64], o_sums[0:64, q * P:(q + 1) * P],
                                               ident[0:64, 0:64])
                    ins.then_inc(*ot_done.up())

                def flush(u):
                    b = units[u][0]
                    pe.wait_ge(*on_done.at(u + 1))
                    for q in range(QT):
                        ins = pe.transpose(bank[:, MISC, q * P:(q + 1) * P], o_tok[:, b, q, :], ident)
                    ins.then_inc(*fl_done.up())

                for i in range(NG):
                    max_step(0, i)
                turn_maxima(0)
                for u in range(NU):
                    for n in range(NG):
                        scores(u, n)
                        if u + 1 < NU:
                            for i in maxima_of(n):
                                max_step(u + 1, i)
                        if n % NJ == 1 and u * QT + n // NJ >= 1:
                            values(*divmod(u * QT + n // NJ - 1, QT))
                        if n == RESULT and u >= 1:
                            turn_result(u - 1)
                        if n == FLUSH and u >= 1 and flush_of(u - 1):
                            flush(u - 1)
                        if n == TURN and u + 1 < NU:
                            turn_maxima(u + 1)
                values(NU - 1, QT - 1)
                turn_result(NU - 1)
                flush(NU - 1)

            @block.vector
            def _(dve):
                step = steps(dve, step_sig)

                def reduce_step(u, i):
                    j, q = divmod(i, QT)
                    n = u * NJ * QT + i
                    keys = (q + 1) * P if causal else S
                    dve.wait_ge(*mx_done.at(n + 1))
                    if wide:
                        o = max_wide[:, q, (64, 0)[j]:(64, 0)[j] + 1]
                        if i == 0 and u >= 1:
                            dve.wait_ge(*mt_done.at(u))
                    else:
                        o = neg_max[:, q, j:j + 1]
                    ins = dve.tensor_reduce(o, bank[:, MX_BANKS[n % NX], 0:keys], X_AXIS, ALU.max, negate=True)
                    ins.then_inc(*mx_used.up())
                    return ins

                def split_maxima(u):
                    if wide:
                        dve.wait_ge(*mx_used.at((u + 1) * NJ * QT))
                        dve.sem_inc(*mp_done.up())
                        return
                    dve.wait_ge(*mx_used.at((u + 1) * NJ * QT))
                    if u >= 1:
                        dve.wait_ge(*mt_done.at(u))
                    step(dve.tensor_copy(max_parts[:, :, 0:4], neg_max[:, :, :]))
                    dve.tensor_tensor(max_parts[:, :, 4:8], neg_max[:, :, :], max_parts[:, :, 0:4].bitcast(F32),
                                      ALU.subtract).then_inc(*mp_done.up())

                def normalise(u):
                    b, g = units[u]
                    dve.wait_ge(*ot_done.at(u + 1))
                    if wide:
                        o = bank[:, MISC, :].rearrange("p (q j d) -> p q j d", q=QT, j=2)
                        r = bank[:, SUMT, 0:4 * 64].rearrange("p (q j d) -> p q j d", q=QT, j=2)[:, :, :, 0]
                        dest = o_tok[:, b, :, :].rearrange("p q (j d) -> p q j d", j=2)
                        width = WH
                    else:
                        o = bank[:, MISC, :].rearrange("p (q j d) -> p q j d", q=QT, j=4)
                        r = o[:, :, :, DH]
                        o = o[:, :, :, 0:DH]
                        dest = o_tok[:, b, :, 32 * g:32 * g + 32].rearrange("p q (j d) -> p q j d", j=4)
                        width = DH
                    rs = rsum[:, :, 0:NJ]
                    if guard:
                        step(dve.tensor_scalar(rs, r, 1e-12, None, ALU.max))
                        step(dve.reciprocal(rs, rs))
                    else:
                        step(dve.reciprocal(rs, r))
                    dve.tensor_tensor(dest, o, rs.unsqueeze(3).broadcast_to([P, QT, NJ, width]), ALU.mult
                                      ).then_inc(*on_done.up())

                for i in range(NG):
                    reduce_step(0, i)
                split_maxima(0)
                for u in range(NU):
                    for n in range(NG):
                        if u + 1 < NU:
                            for i in maxima_of(n):
                                reduce_step(u + 1, i)
                        if n == RESULT and u >= 1:
                            normalise(u - 1)
                        if n == TURN - 1 and u + 1 < NU:
                            split_maxima(u + 1)
                normalise(NU - 1)

            @block.scalar
            def _(act):
                def maxima_rows(u):
                    act.wait_ge(*mt_done.at(u + 1))
                    if wide:
                        act.copy(wide_q[64:65, u, 0, :], bank[64:65, MISC, :])
                        act.copy(wide_q[0:1, u, 1, :], bank[0:1, MISC, :]).then_inc(*m_ready.up())
                    else:
                        act.copy(QM[96:104, u % 2, :], bank[0:8, MISC, :]).then_inc(*m_ready.up())

                def build_first(u):
                    b, g = units[u]
                    s, tok = u % 2, slice(b * S, (b + 1) * S)
                    act.wait_ge(*base_loaded[g % NB_].at(96 * (g // NB_ + 1)))
                    if u >= 2:
                        act.wait_ge(*st_done.at((u - 1) * NG))
                    act.copy(QM[0:96, s, :], q_base(g)[0:96, tok]).then_inc(*first_built.up())
                    act.activation(KS[0:96, s, 0, :], k_base(g)[0:96, tok], ACT.Copy, scale=K("stack")[0:96, 0:1]
                                   ).then_inc(*first_built.up())

                def exponentials(u, n):
                    kt, j = divmod(n, NJ)
                    m = u * NG + n
                    act.wait_ge(*st_done.at(m + 1))
                    if j == 0 and u * QT + kt >= 2:
                        act.wait_ge(*pv_done.at(u * QT + kt - 1))
                    lo = kt * P if causal else 0
                    act.activation(probs[:, kt % 2, j, lo:S], bank[:, ST_BANKS[m % NS], lo:S], ACT.Exp, scale=scale).then_inc(*exp_done.up())

                def copy_result(u):
                    act.wait_ge(*pv_done.at((u + 1) * QT))
                    if u >= 1:
                        act.wait_ge(*ot_done.at(u))
                    if wide:
                        act.copy(o_sums[0:64, :], bank[0:64, SUMS, :])
                    act.copy(o_feat[:, :], bank[:, PVB, :]).then_inc(*o_ready.up())

                def flush_copy(u, k):
                    b = units[u][0]
                    act.wait_ge(*fl_done.at(k))
                    act.copy(att_feat[:, chunk, b * S:(b + 1) * S], bank[:, MISC, :]).then_inc(*fl_used.up())

                k = 0
                if not wide:
                    build_first(0)
                maxima_rows(0)
                for u in range(NU):
                    if not wide and u + 1 < NU:
                        build_first(u + 1)
                    for n in range(NG):
                        exponentials(u, n)
                        if n == COPY and u >= 1:
                            copy_result(u - 1)
                        if n == FLUSH and u >= 1 and flush_of(u - 1):
                            k += 1
                            flush_copy(u - 1, k)
                        if n == TURN and u + 1 < NU:
                            maxima_rows(u + 1)
                copy_result(NU - 1)
                flush_copy(NU - 1, k + 1)
        signals.settle()

    def cross_stage(wname, bq, bk, bv, mask_src, mask_bool, heads, scale, fill, mask_tiles):
        wq, wk, wv = (W(wname, 128 * i, 128 * i + 128) for i in range(3))
        dh = P // heads
        halves = 2 if heads > 1 else 1
        G = heads // halves
        HB = min(G, 4)
        NB = G // HB
        N = NT * halves
        KP = 96
        (m_ld, kq, kq_used, kbd_done, q_ready, s_done, s_used, sh_done, filled, e_done, et_done, et_used, o_done,
         o_used, ot_done, ot_used, nb_done, v_ok, cleared) = (signals(n) for n in (
             "m_ld", "kq", "kq_used", "kbd_done", "q_ready", "s_done", "s_used", "sh_done", "filled", "e_done",
             "et_done", "et_used", "o_done", "o_used", "ot_done", "ot_used", "nb_done", "v_ok", "cleared"))
        step_sig = signals("dve_step")
        at = [T]

        def take(n):
            at[0] += n
            return flat[:, at[0] - n:at[0]]

        kbd = take(B * heads * SC).rearrange("p (b h k) -> p b h k", b=B, k=SC)
        v_ctx = take(B * heads * (dh + 1)).rearrange("p (b h d) -> p b h d", b=B, h=heads)
        k_ctx = take(B * SC)
        neg = take(NT * SC).rearrange("p (t k) -> p t k", k=SC)
        masks = take(NT * SC).rearrange("p (t k) -> p t k", k=SC)
        sc_flat = take(4 * max(G, 2) * SC)
        raw_mask = sc_flat[:, 0:NT * SC].rearrange("p (t k) -> p t k", k=SC)
        sc = sc_flat[:, 0:4 * G * SC].rearrange("p (s h k) -> p s h k", s=4, k=SC)
        et = probs[0:KP, :, :, :].rearrange("p a b c -> p (a b c)").rearrange("p (s h q) -> p s h q", s=4, q=P)

        def batch(i):
            return i // halves // QT

        def head(i, g):
            return (i % halves) * G + g

        def last_of_tile(i):
            return i >= 0 and i % halves == halves - 1

        def o_bank(t):
            return bank[:, 6 + t % 2, 0:heads * (dh + 1)].rearrange("p (h d) -> p h d", h=heads)

        def mask_of(table, i):
            return table[:, mask_tiles(i // halves), :]

        with nc.Block() as block:
            @block.sync
            def _(sp):
                n, dst = mask_src(raw_mask)
                sp.dma_start(dst, n).then_inc(*m_ld.up(16))

            @block.tensor
            def _(pe):
                pe.matmul(bank[:, 4, 0:B * SC], wk, ctx_feat[:, :], start=True, stop=True).then_inc(*kq.up())
                for b in range(B):
                    ins = pe.matmul(bank[0:SC, 5, b * P:(b + 1) * P], ctx_feat[:, b * SC:(b + 1) * SC], wv, start=True,
                                    stop=True)
                ins.then_inc(*kq.up())
                for hf in range(2):
                    pe.matmul(bank[:, 6 + hf, :], wq, x_feat[:, hf * HF:(hf + 1) * HF], start=True, stop=True
                              ).then_inc(*kq.up())
                pe.wait_ge(*q_ready.at(2))
                pe.wait_ge(*kbd_done.at(1))
                pe.wait_ge(*v_ok.at(1))

                def scores(i):
                    if i >= 2:
                        pe.wait_ge(*s_used.at(i - 1))
                    t = i // halves
                    for n in range(NB):
                        h = head(i, n * HB)
                        ins = pe.matmul(bank[:, 2 * (i % 2) + n, 0:HB * SC], q_feat[:, t * P:(t + 1) * P],
                                        kbd[:, batch(i), h:h + HB, :], start=True, stop=True)
                    ins.then_inc(*s_done.up())

                def turn(i):
                    pe.wait_ge(*e_done.at(i + 1))
                    for n in range(NB):
                        m = i * NB + n
                        if m >= 2:
                            pe.wait_ge(*et_used.at(m - 1))
                        for h in range(HB):
                            ins = pe.transpose(bank[0:SC, 4 + m % 2, h * P:(h + 1) * P], sc[:, i % 4, n * HB + h, :],
                                               ident)
                        ins.then_inc(*et_done.up())

                def values(i):
                    t = i // halves
                    pe.wait_ge(*et_used.at((i + 1) * NB))
                    if i % halves == 0:
                        if t >= 2:
                            pe.wait_ge(*o_used.at(t - 1))
                        if t == QT + 1:
                            pe.wait_ge(*ot_used.at(1))
                    for g in range(G):
                        h = head(i, g)
                        ins = pe.matmul(o_bank(t)[:, h, :], et[:, i % 4, g, :], v_ctx[0:KP, batch(i), h, :], start=True,
                                        stop=True)
                    ins.then_inc(*o_done.up())

                def turn_result(b):
                    pe.wait_ge(*o_used.at(QT * (b + 1)))
                    for q in range(QT):
                        ins = pe.transpose(bank[:, 7, q * P:(q + 1) * P], o_tok[:, b, q, :], ident)
                    ins.then_inc(*ot_done.up())

                for k in range(N + 5):
                    if k < N:
                        scores(k)
                    if 0 <= k - 2 < N:
                        turn(k - 2)
                    if k - 4 in (N // 2 - 1, N - 1):
                        turn_result(batch(k - 4))
                    if 0 <= k - 3 < N:
                        values(k - 3)

            @block.scalar
            def _(act):
                act.wait_ge(*kq.at(1))
                if bk is not None:
                    act.activation(k_ctx, bank[:, 4, 0:B * SC], ACT.Identity, bias=bk).then_inc(*kq_used.up())
                else:
                    act.copy(k_ctx, bank[:, 4, 0:B * SC]).then_inc(*kq_used.up())
                for hf in range(2):
                    act.wait_ge(*kq.at(3 + hf))
                    o = q_feat[:, hf * HF:(hf + 1) * HF]
                    if bq is not None:
                        act.activation(o, bank[:, 6 + hf, :], ACT.Identity, bias=bq).then_inc(*q_ready.up())
                    else:
                        act.copy(o, bank[:, 6 + hf, :]).then_inc(*q_ready.up())
                act.wait_ge(*cleared.at(1))
                for k in range(N + 5):
                    if 0 <= k - 1 < N:
                        i = k - 1
                        act.wait_ge(*sh_done.at(i + 1))
                        act.activation(sc[:, i % 4, :, :], sc[:, i % 4, :, :], ACT.Exp, scale=scale
                                       ).then_inc(*e_done.up())
                    if 0 <= k - 2 < N:
                        i = k - 2
                        if i >= 4:
                            act.wait_ge(*o_done.at(i - 3))
                        for n in range(NB):
                            m = i * NB + n
                            act.wait_ge(*et_done.at(m + 1))
                            act.copy(et[0:SC, i % 4, n * HB:(n + 1) * HB, :],
                                     bank[0:SC, 4 + m % 2, 0:HB * P].rearrange("p (h q) -> p h q", q=P)
                                     ).then_inc(*et_used.up())
                    if k - 4 in (N // 2 - 1, N - 1):
                        b = batch(k - 4)
                        act.wait_ge(*ot_done.at(b + 1))
                        act.copy(att_feat[:, 0, b * S:(b + 1) * S], bank[:, 7, :]).then_inc(*ot_used.up())

            @block.vector
            def _(dve):
                step = steps(dve, step_sig)
                dve.wait_ge(*kq.at(2))
                dve.wait_ge(*cleared.at(1))
                v_in = bank[0:SC, 5, 0:B * P].rearrange("p (b h d) -> p b h d", b=B, h=heads)
                for b in range(B):
                    o = v_ctx[0:SC, b, :, 0:dh]
                    if bv is not None:
                        dve.tensor_tensor(o, v_in[:, b, :, :], bv[0:SC, :].rearrange("p (h d) -> p h d", h=heads), ALU.add)
                    else:
                        dve.tensor_copy(o, v_in[:, b, :, :])
                dve.memset(v_ctx[0:SC, :, :, dh:dh + 1], 1.0).then_inc(*v_ok.up())
                dve.wait_ge(*kq_used.at(1))
                for b in range(B):
                    kb = k_ctx[:, b * SC:(b + 1) * SC]
                    if heads == 1:
                        ins = dve.tensor_copy(kbd[:, b, 0, :], kb)
                    else:
                        ins = dve.tensor_tensor(kbd[:, b, :, :], kb.unsqueeze(1).broadcast_to([P, heads, SC]),
                                                K("headmask").unsqueeze(2).broadcast_to([P, heads, SC]), ALU.mult)
                ins.then_inc(*kbd_done.up())
                dve.wait_ge(*m_ld.at(16))
                _, dst = mask_src(raw_mask)
                n_m = masks[:, 0:mask_count(mask_bool), :]
                step(dve.tensor_scalar(n_m, dst, 0.0, None, ALU.not_equal))
                step(dve.tensor_scalar(neg[:, 0:mask_count(mask_bool), :], n_m, 1.0, fill, ALU.subtract, ALU.mult))
                dve.sem_inc(*nb_done.up())

                def keep_unmasked(i):
                    dve.wait_ge(*s_done.at(i + 1))
                    if i >= 4:
                        dve.wait_ge(*et_done.at((i - 3) * NB))
                    src = bank[:, 2 * (i % 2):2 * (i % 2) + NB, 0:HB * SC].rearrange("p n (h k) -> p n h k", k=SC)
                    mm = mask_of(masks, i).unsqueeze(1).unsqueeze(1).broadcast_to([P, NB, HB, SC])
                    dve.tensor_tensor(sc[:, i % 4, :, :].rearrange("p (n h) k -> p n h k", h=HB), src, mm, ALU.mult
                                      ).then_inc(*s_used.up())

                def less_maxima(i):
                    x, mx = sc[:, i % 4, :, :], picked[:, i % 4, 0:G]
                    dve.wait_ge(*filled.at(i + 1))
                    step(dve.tensor_reduce(mx, x, X_AXIS, ALU.max))
                    dve.tensor_tensor(x, x, mx.unsqueeze(2).broadcast_to([P, G, SC]), ALU.subtract
                                      ).then_inc(*sh_done.up())

                def normalise(i):
                    t = i // halves
                    rs = picked[:, 4 + t % 2, 0:heads]
                    dve.wait_ge(*o_done.at(i + 1))
                    step(dve.reciprocal(rs, o_bank(t)[:, :, dh]))
                    dve.tensor_tensor(o_tok[:, t // QT, t % QT, :].rearrange("p (h d) -> p h d", h=heads),
                                      o_bank(t)[:, :, 0:dh], rs.unsqueeze(2).broadcast_to([P, heads, dh]), ALU.mult
                                      ).then_inc(*o_used.up())

                for k in range(N + 5):
                    if k < N:
                        keep_unmasked(k)
                    if 0 <= k - 1 < N:
                        less_maxima(k - 1)
                    if last_of_tile(k - 3) and k - 3 < N:
                        normalise(k - 3)

            @block.gpsimd
            def _(pool):
                step = steps(pool, signals("pool_step"))
                step(pool.memset(v_ctx[64:KP, :, :, :], 0.0))
                step(pool.memset(et[64:KP, :, :, :], 0.0))
                pool.sem_inc(*cleared.up())
                pool.wait_ge(*nb_done.at(1))
                for i in range(N):
                    pool.wait_ge(*s_used.at(i + 1))
                    pool.tensor_tensor(sc[:, i % 4, :, :], sc[:, i % 4, :, :],
                                       mask_of(neg, i).unsqueeze(1).broadcast_to([P, G, SC]), ALU.add
                                       ).then_inc(*filled.up())
        signals.settle()

    def mask_count(kind):
        return {"q": QT, "bq": NT, "b": B}[kind]

    def route_stage(terms, bias, experts, top_k, renormalise, distance=False):
        E, EP = experts, max(experts, 8)
        ns = 8 - top_k
        (l_done, s_ready, x_done, g_done, gt_done, hi_ok, sq_done, kk_done, kk_ok) = (signals(n) for n in (
            "l_done", "s_ready", "x_done", "g_done", "gt_done", "hi_ok", "sq_done", "kk_done", "kk_ok"))
        step_sig = signals("dve_step")
        sq = scratch[:, 0:T]
        with nc.Block() as block:
            @block.tensor
            def _(pe):
                weights_here(pe)
                if distance:
                    pe.wait_ge(*kk_done.at(1))
                    pe.matmul(bank[:, 2, 0:16], ones128, kk_sq, start=True, stop=True).then_inc(*kk_ok.up())
                for t in range(NT):
                    for n, (operand, w) in enumerate(terms):
                        ins = pe.matmul(bank[:, 0, t * 16:t * 16 + E], operand[:, t * P:(t + 1) * P], w,
                                        start=(n == 0), stop=(n == len(terms) - 1))
                ins.then_inc(*l_done.up())
                pe.wait_ge(*g_done.at(1))
                for t in range(NT):
                    ins = pe.transpose(bank[0:16, 4 + t // QT, (t % QT) * P:(t % QT + 1) * P], gates[:, t, :], ident)
                ins.then_inc(*gt_done.up())

            @block.vector
            def _(dve):
                step = steps(dve, step_sig)
                if distance:
                    dve.wait_ge(loads["ld_w"], 16)
                    dve.tensor_tensor(kk_sq, W("l0_keys"), W("l0_keys"), ALU.mult).then_inc(*kk_done.up())
                    for t in range(NT):
                        ins = dve.tensor_tensor_reduce(out=sum_tok[:, t, :], in0=x_tok[:, t, :], in1=x_tok[:, t, :],
                                                       scale=1.0, scalar=0.0, op0=ALU.mult, op1=ALU.add,
                                                       accum_out=small[:, t, 0:1])
                    step(ins)
                    dve.wait_ge(*kk_ok.at(1))
                    step(dve.tensor_tensor(kk_row, bias, bank[:, 2, 0:16], ALU.subtract))
                step(dve.memset(gates[:, :, :], 0.0))
                dve.memset(lg[:, :, 0:EP], -HUGE)
                step(dve.memset(lg[:, :, EP:EP + ns], HUGE))
                step(dve.memset(top_in[:, :, :], HUGE))
                dve.wait_ge(*l_done.at(1))
                logit = bank[:, 0, 0:NT * 16].rearrange("p (t e) -> p t e", e=16)[:, :, 0:E]
                brow = (kk_row if distance else bias)
                if bias is not None:
                    step(dve.tensor_tensor(lg[:, :, 0:E], logit, brow.unsqueeze(1).broadcast_to([P, NT, E]), ALU.add))
                else:
                    step(dve.tensor_copy(lg[:, :, 0:E], logit))
                if distance:
                    step(dve.tensor_tensor(lg[:, :, 0:E], lg[:, :, 0:E], small[:, :, 0:1].broadcast_to([P, NT, E]),
                                           ALU.subtract))
                for t in range(NT):
                    ins = dve.max(top8[:, t, :], lg[:, t, 0:EP])
                step(ins)
                step(dve.tensor_copy(top_in[:, :, 0:top_k], top8[:, :, 0:top_k]))
                for t in range(NT):
                    ins = dve.match_replace(lg_rep[:, t, 0:EP + ns], top_in[:, t, :], lg[:, t, 0:EP + ns], -HUGE)
                step(ins)
                step(dve.tensor_tensor(picked[:, :, 0:E], lg_rep[:, :, 0:E], lg[:, :, 0:E], ALU.not_equal))
                dve.tensor_tensor(lg[:, :, 0:E], lg[:, :, 0:E], top8[:, :, 0:1].broadcast_to([P, NT, E]),
                                  ALU.subtract).then_inc(*s_ready.up())
                dve.wait_ge(*x_done.at(1))
                step(dve.tensor_tensor(picked[:, :, 0:E], picked[:, :, 0:E], lg[:, :, 0:E], ALU.mult))
                step(dve.tensor_reduce(small[:, :, 1], (picked if renormalise else lg)[:, :, 0:E], X_AXIS, ALU.add))
                step(dve.reciprocal(small[:, :, 1], small[:, :, 1]))
                step(dve.tensor_tensor(gates[:, :, 0:E], picked[:, :, 0:E],
                                       small[:, :, 1:2].broadcast_to([P, NT, E]), ALU.mult))
                dve.tensor_reduce(gate_sum[:, :], gates[:, :, 0:E], X_AXIS, ALU.add).then_inc(*g_done.up())
                dve.wait_ge(*hi_ok.at(1))
                dve.tensor_tensor(gate_parts[32:48, :], gate_rows, gate_parts[0:16, :].bitcast(F32),
                                  ALU.subtract)

            @block.scalar
            def _(act):
                act.wait_ge(*s_ready.at(1))
                act.activation(lg[:, :, 0:E], lg[:, :, 0:E], ACT.Exp).then_inc(*x_done.up())
                act.wait_ge(*gt_done.at(1))
                rows16 = bank[0:16, 4:6, :].rearrange("p a n -> p (a n)")
                act.copy(gate_rows, rows16)
                act.copy(gate_parts[0:16, :], rows16).then_inc(*hi_ok.up())
        signals.settle()

    kk_sq = sb("kk_sq", [P, 16])[:, :]
    kk_row = sb("kk_row", [P, 16])[:, :]
    route_w = sb("route_w", [P, 16])
    ones128 = sb("ones128", [P, P])[:, :]

    def expert_stage(source, experts, b1, b2, affine=None):
        NFT = 4
        seq = [(e, hf, f) for e in range(experts) for hf in range(2) for f in range(NFT)]
        N = len(seq)
        LAG = 3
        (up_done, gelu_done, gate_ok, gate_used, h_ready, dn_done, xe_ok, w_used, y_ok) = (signals(n) for n in (
            "up_done", "gelu_done", "gate_ok", "gate_used", "h_ready", "dn_done", "xe_ok", "w_used", "y_ok"))
        g_buf = scratch[:, 0:3 * HF].rearrange("p (s n) -> p s n", n=HF)
        h_buf = scratch[:, 3 * HF:7 * HF].rearrange("p (s n) -> p s n", n=HF)
        first = expert_total[0]
        XE = att_feat[:, 0:2, :]

        def slot(e):
            return (first + e) % NW

        def arrived(eng, e):
            n = first + e
            eng.wait_ge(expert_loaded[n % NW], 16 * (n // NW + 1))

        load_experts(first, experts)
        with nc.Block() as block:
            emit_loads(block, w_used)

            @block.tensor
            def _(pe):
                for i in range(N + LAG):
                    if i < N:
                        e, hf, f = seq[i]
                        if hf == 0 and f == 0:
                            arrived(pe, e)
                            if affine is not None:
                                pe.wait_ge(*xe_ok.at(e + 1))
                        if f == 0:
                            k = e * 2 + hf
                            if k >= 2:
                                pe.wait_ge(*gate_used.at(k - 1))
                            pe.matmul(bank[:, 4 + k % 2, :], sel[0:96, e, :], gate_parts[0:96, hf * HF:(hf + 1) * HF],
                                      start=True, stop=True).then_inc(*gate_ok.up())
                        if i >= 3:
                            pe.wait_ge(*gelu_done.at(i - 2))
                        x = (XE[:, e % 2, :] if affine is not None else source)[:, hf * HF:(hf + 1) * HF]
                        pe.matmul(bank[:, (0, 1, 2)[i % 3], :], wring[:, slot(e), f * P:(f + 1) * P], x, start=True,
                                  stop=True).then_inc(*up_done.up())
                    if i >= LAG:
                        m = i - LAG
                        e, hf, f = seq[m]
                        pe.wait_ge(*h_ready.at(m + 1))
                        ins = pe.matmul(bank[:, 6 + hf, :], wring[:, slot(e), 512 + f * P:512 + (f + 1) * P],
                                        h_buf[:, m % 4, :], start=(e == 0 and f == 0), stop=False,
                                        skip_group_check=True)
                        ins.then_inc(*dn_done.up())
                for hf in range(2):
                    pe.matmul(bank[:, 6 + hf, :], b2, gate_rows[:, hf * HF:(hf + 1) * HF], start=False, stop=True,
                              skip_group_check=True).then_inc(*y_ok.up())

            @block.scalar
            def _(act):
                for i, (e, hf, f) in enumerate(seq):
                    act.wait_ge(*up_done.at(i + 1))
                    if i >= 3:
                        act.wait_ge(*h_ready.at(i - 2))
                    act.activation(g_buf[:, i % 3, :], bank[:, (0, 1, 2)[i % 3], :], ACT.Gelu, bias=C(*b1(e, f))
                                   ).then_inc(*gelu_done.up())
                for hf in range(2):
                    act.wait_ge(*y_ok.at(hf + 1))
                    act.copy(y_feat[:, hf * HF:(hf + 1) * HF], bank[:, 6 + hf, :])

            @block.vector
            def _(dve):
                for i, (e, hf, f) in enumerate(seq):
                    dve.wait_ge(*gelu_done.at(i + 1))
                    k = e * 2 + hf
                    if f == 0:
                        dve.wait_ge(*gate_ok.at(k + 1))
                    if i >= 4:
                        dve.wait_ge(*dn_done.at(i - 3))
                    ins = dve.tensor_tensor(h_buf[:, i % 4, :], g_buf[:, i % 3, :], bank[:, 4 + k % 2, :], ALU.mult)
                    ins.then_inc(*h_ready.up())
                    if f == NFT - 1:
                        dve.wait_ge(*h_ready.at(i + 1))
                        dve.sem_inc(*gate_used.up())

            if affine is not None:
                @block.gpsimd
                def _(pool):
                    for e in range(experts):
                        if e >= 2:
                            pool.wait_ge(*up_done.at((e - 1) * 8))
                        pool.tensor_scalar(XE[:, e % 2, :], source[:, :], affine(e)[0], affine(e)[1], ALU.mult,
                                           ALU.add).then_inc(*xe_ok.up())
        expert_total[0] = first + experts
        signals.settle()

    pending = []

    def load_experts(first, experts):
        pending.extend(range(first, first + experts))

    def emit_loads(block, w_used):
        todo = list(pending)
        pending.clear()
        dn_done = signals("dn_done")
        first = todo[0]

        @block.sync
        def _(sp):
            for n in todo:
                if n - NW >= first:
                    sp.wait_ge(*dn_done.at((n - NW - first + 1) * 8))
                src = l0_experts[n, :, :] if n < 16 else l2_experts[n - 16, :, :]
                sp.dma_start(wring[:, n % NW, :], src).then_inc(expert_loaded[n % NW], 16)

    def gated_stage():
        seq = [(p_, hf) for p_ in range(9) for hf in range(2)]
        (up_done, gelu_done, gate_ok, h_ready, dn_done, y_ok, t_ok) = (signals(n) for n in (
            "up_done", "gelu_done", "gate_ok", "h_ready", "dn_done", "y_ok", "t_ok"))
        g_buf = scratch[:, 0:3 * HF].rearrange("p (s n) -> p s n", n=HF)
        h_buf = scratch[:, 3 * HF:5 * HF].rearrange("p (s n) -> p s n", n=HF)
        t_buf = scratch[:, 5 * HF:7 * HF].rearrange("p (s n) -> p s n", n=HF)
        with nc.Block() as block:
            @block.tensor
            def _(pe):
                for i in range(len(seq) + 1):
                    if i < len(seq):
                        p_, hf = seq[i]
                        x = x_feat[:, hf * HF:(hf + 1) * HF]
                        if i >= 2:
                            pe.wait_ge(*h_ready.at(i - 1))
                        s = i % 2
                        if p_ < 8:
                            wu, wg = (W("l3_w1", p_ * 256 + a * 128, p_ * 256 + a * 128 + 128) for a in range(2))
                        else:
                            wu, wg = W("l3_ws1", 0, 128), W("l3_ws1", 128, 256)
                        pe.matmul(bank[:, 2 * s, :], wu, x, start=True, stop=True)
                        ins = pe.matmul(bank[:, 2 * s + 1, :], wg, x, start=True, stop=True)
                        ins.then_inc(*up_done.up())
                        if p_ < 8:
                            pe.matmul(bank[:, 4 + s, :], sel[0:96, p_, :],
                                      gate_parts[0:96, hf * HF:(hf + 1) * HF], start=True, stop=True
                                      ).then_inc(*gate_ok.up())
                    if i >= 1:
                        p_, hf = seq[i - 1]
                        pe.wait_ge(*h_ready.at(i))
                        w2 = W("l3_w2", p_ * 128, p_ * 128 + 128) if p_ < 8 else W("l3_ws2")
                        ins = pe.matmul(bank[:, 6 + hf, :], w2, h_buf[:, (i - 1) % 2, :], start=(p_ == 0),
                                        stop=(p_ == 8), skip_group_check=True)
                        ins.then_inc(*dn_done.up())

            @block.scalar
            def _(act):
                for i, (p_, hf) in enumerate(seq):
                    act.wait_ge(*up_done.at(i + 1))
                    if i >= 2:
                        act.wait_ge(*h_ready.at(i - 1))
                    act.activation(g_buf[:, i % 2, :], bank[:, 2 * (i % 2) + 1, :], ACT.Silu
                                   ).then_inc(*gelu_done.up())
                for hf in range(2):
                    act.wait_ge(*dn_done.at(17 + hf))
                    act.copy(y_feat[:, hf * HF:(hf + 1) * HF], bank[:, 6 + hf, :])

            @block.vector
            def _(dve):
                for i, (p_, hf) in enumerate(seq):
                    dve.wait_ge(*gelu_done.at(i + 1))
                    if i >= 2:
                        dve.wait_ge(*dn_done.at(i - 1))
                    if p_ < 8:
                        dve.tensor_tensor(t_buf[:, i % 2, :], g_buf[:, i % 2, :], bank[:, 2 * (i % 2), :], ALU.mult
                                          ).then_inc(*t_ok.up())
                        dve.wait_ge(*t_ok.at(i + 1))
                        dve.wait_ge(*gate_ok.at(i + 1))
                        dve.tensor_tensor(h_buf[:, i % 2, :], t_buf[:, i % 2, :], bank[:, 4 + i % 2, :], ALU.mult
                                          ).then_inc(*h_ready.up())
                    else:
                        dve.tensor_tensor(h_buf[:, i % 2, :], g_buf[:, i % 2, :], bank[:, 2 * (i % 2), :], ALU.mult
                                          ).then_inc(*h_ready.up())
        signals.settle()

    def memory_stage():
        TC = (SC - 4) // 4 + 1
        conv_ok, moved = signals("conv_ok"), signals("moved")
        with nc.Block() as block:
            @block.tensor
            def _(pe):
                for b in range(B):
                    for r in range(4):
                        lo = b * S + 256 + r
                        ins = pe.matmul(bank[:, 0, b * 32:b * 32 + TC], W("l0_conv", r * P, r * P + P),
                                        x_feat[:, lo:lo + 4 * (TC - 1) + 1:4], start=(r == 0), stop=(r == 3))
                ins.then_inc(*conv_ok.up())

            @block.gpsimd
            def _(pool):
                for b in range(B):
                    o = b * S
                    pool.tensor_copy(y_feat[:, o:o + 256 - TC], x_feat[:, o + TC:o + 256])
                    pool.tensor_copy(y_feat[:, o + 256:o + S - SC], x_feat[:, o + 256 + SC:o + S])
                    pool.tensor_copy(y_feat[:, o + S - SC:o + S], ctx_feat[:, b * SC:(b + 1) * SC])

            @block.scalar
            def _(act):
                act.wait_ge(*conv_ok.at(1))
                for b in range(B):
                    act.activation(y_feat[:, b * S + 256 - TC:b * S + 256], bank[:, 0, b * 32:b * 32 + TC],
                                   ACT.Identity, bias=C("conv_b"))
        signals.settle()

    def ternary_stage():
        w_ld, tq_done, wt_in, wt_done = (signals(n) for n in ("w_ld", "tq_done", "wt_in", "wt_done"))
        v_clear = signals("v_clear")
        step_sig = signals("dve_step")
        MAGIC = 1.5 * 2.0 ** 23
        amax, scl, inv = small[:, :, 0], small[:, :, 1], small[:, :, 2]
        with nc.Block() as block:
            @block.sync
            def _(sp):
                for s in range(4):
                    sp.dma_start(tern_i[32 * s:32 * s + 32, :], packed_in.rearrange("(o i) -> o i", i=P)
                                 ).then_inc(*w_ld.up(16))
                sp.dma_start(weights13[:, 0:W3_N], weights3_in).then_inc(loads["ld_w3"], 16)

            @block.gpsimd
            def _(pool):
                pool.memset(zeros[:, :], 0.0).then_inc(*v_clear.up())
                pool.memset(QM[:, :, :].bitcast(F32), 0.0)
                pool.memset(gate_parts[:, :].bitcast(F32), 0.0)
                pool.memset(v_aug[:, :, :, :], 0.0).then_inc(*v_clear.up())
                pool.wait_ge(*v_clear.at(2))
                pool.memset(v_aug[:, :, :, DH:DH + 1], 1.0)

            @block.vector
            def _(dve):
                step = steps(dve, step_sig)
                dve.wait_ge(*w_ld.at(64))
                for s in range(4):
                    r = slice(32 * s, 32 * s + 32)
                    ins = dve.tensor_scalar(tern_i[r, :], tern_i[r, :], 2 * s, 3, ALU.logical_shift_right,
                                            ALU.bitwise_and)
                step(ins)
                step(dve.tensor_copy(tern_f[:, :], tern_i[:, :]))
                dve.tensor_scalar(tern_f[:, :], tern_f[:, :], 1.0, R("l1f_scale"), ALU.subtract, ALU.mult
                                  ).then_inc(*wt_in.up())
                step(dve.tensor_reduce(amax, x_tok[:, :, :], X_AXIS, ALU.max, apply_absolute_value=True))
                step(dve.tensor_scalar(amax, amax, 1e-5, None, ALU.max))
                step(dve.reciprocal(scl, amax))
                step(dve.tensor_scalar(scl, scl, 127.0, None, ALU.mult))
                step(dve.reciprocal(inv, scl))
                for t in range(NT):
                    ins = dve.tensor_scalar(sum_tok[:, t, :], x_tok[:, t, :], scl[:, t:t + 1], MAGIC, ALU.mult,
                                            ALU.add)
                step(ins)
                step(dve.tensor_scalar(sum_tok[:, :, :], sum_tok[:, :, :], MAGIC, 127.0, ALU.subtract, ALU.min))
                for t in range(NT):
                    ins = dve.tensor_scalar(sum_tok[:, t, :], sum_tok[:, t, :], -128.0, inv[:, t:t + 1], ALU.max,
                                            ALU.mult)
                    if t % QT == QT - 1:
                        ins.then_inc(*tq_done.up())
                dve.wait_ge(*v_clear.at(1))
                constant_rows(dve)

            @block.tensor
            def _(pe):
                pe.wait_ge(*wt_in.at(1))
                pe.transpose(bank[:, 0, 0:P], tern_f[:, :], ident).then_inc(*wt_done.up())
                for hf in range(2):
                    pe.wait_ge(*tq_done.at(hf + 1))
                    for q in range(QT):
                        ins = pe.transpose(bank[:, 1 + hf, q * P:(q + 1) * P], sum_tok[:, hf * QT + q, :], ident)
                    ins.then_inc(*wt_done.up())

            @block.scalar
            def _(act):
                act.wait_ge(*wt_done.at(1))
                act.copy(tern_w[:, :], bank[:, 0, 0:P])
                for hf in range(2):
                    act.wait_ge(*wt_done.at(2 + hf))
                    act.copy(y_feat[:, hf * HF:(hf + 1) * HF], bank[:, 1 + hf, :])
        signals.settle()

    tern_i = sb("tern_i", [P, P], I32)
    tern_f = sb("tern_f", [P, P])
    tern_w = sb("tern_w", [P, P])

    def keep_stage():
        with nc.Block() as block:
            @block.gpsimd
            def _(pool):
                pool.tensor_copy(x_keep[:, :, :], x_tok[:, :, :])

    def prepare_stage():
        with nc.Block() as block:
            @block.vector
            def _(dve):
                step = steps(dve, signals("dve_step"))
                dve.wait_ge(loads["ld_w"], 16)
                step(dve.memset(ones128[:, :], 1.0))
                dve.scalar_tensor_tensor(out=route_w[:, :], in0=W("l0_keys"), scalar=2.0, in1=W("l0_rw"),
                                         op0=ALU.mult, op1=ALU.add)

        signals.settle()

    def pair_stage():
        with nc.Block() as block:
            @block.vector
            def _(dve):
                for p_ in range(8):
                    for a in range(2):
                        dve.tensor_scalar(sel[:, p_, a * 64:(a + 1) * 64], ones128[:, 0:64],
                                          K("sel")[:, 2 * p_ + a:2 * p_ + a + 1], None, ALU.mult)

    prepare_stage()
    rsD = float(DH) ** -0.5

    norm_stage(target="hat", affine=(C("l0_g"), C("l0_b")))
    project_stage(hat_feat, W("l0_qkv", 0, 128), W("l0_qkv", 128, 256), W("l0_qkv", 256, 384), C("l0_bqkv", 0),
                  C("l0_bqkv", 1), R("l0_bv"))
    attention_stage(rsD, guard=True)
    norm_stage([(att_feat[:, 0, :], W("l0_proj"))], bias=R("l0_bproj"))
    memory_stage()
    norm_stage([(y_feat, ident)])
    route_stage([(x_feat, route_w[:, :])], R("l0_rb"), 16, 4, True, distance=True)
    expert_stage(x_feat, 16, lambda e, f: ("l0_b1", e * 4 + f), W("l0_b2")[0:16, :])
    norm_stage([(y_feat, ident)])

    layer_loads.append("ld_w1")
    norm_stage(target="hat", affine=(C("l1_g"), None))
    wide_stage()
    norm_stage([(att_feat[:, p_, :], W("l1_wo", p_ * P, p_ * P + P)) for p_ in range(8)])
    cross_stage("l1x", C("l1x_bq"), C("l1x_bk"), R("l1x_bv"),
                lambda raw: (mask1_in.rearrange("a b (t p) k -> p (a b t) k", p=P), raw[:, 0:QT, :].bitcast(I32)),
                "q", H, rsD, 1e9 / rsD, lambda t: t % QT)
    norm_stage([(att_feat[:, 0, :], W("l1x", 384, 512))], bias=R("l1x_bo"))
    ternary_stage()
    norm_stage([(y_feat, tern_w[:, :])], bias=R("l1f_bias"))

    project_stage(x_feat, W("l2_attn", 0, 128), W("l2_attn", 128, 256), W("l2_attn", 256, 384), None, None, None,
                  K("l2_cos"), K("l2_sin"))
    attention_stage(rsD, causal=True)
    norm_stage([(att_feat[:, 0, :], W("l2_attn", 384, 512))])
    cross_stage("l2x", None, None, None,
                lambda raw: (mask2_in.rearrange("a b (t p) k -> p (a b t) k", p=P), raw[:, :, :].bitcast(I32)),
                "bq", H, D ** -0.5, 1e20, lambda t: t)
    norm_stage([(att_feat[:, 0, :], W("l2x", 384, 512))], bias=R("l2x_bo"))
    keep_stage()
    for l in range(4):
        norm_stage(target="hat")
        route_stage([(x_feat, W("l2_rw", 4 * l, 4 * l + 4))], R("l2_rb", 4 * l, 4 * l + 4), 4, 2, True)
        expert_stage(hat_feat, 4, lambda e, f, l=l: ("l2_b1", l * 16 + e * 4 + f), W("l2_b2", l * P, l * P + P)[0:16, :],
                     affine=lambda e, l=l: (C("l2_g", l * 4 + e), C("l2_b", l * 4 + e)))
        norm_stage([(y_feat, ident)], residual_scale=gate_sum, norm=(l == 3), plus=x_keep if l == 3 else None)

    layer_loads.append("ld_w3")
    project_stage(x_feat, W("l3_qkv", 0, 128), W("l3_qkv", 128, 256), W("l3_qkv", 256, 384), C("l3_bqkv", 0),
                  C("l3_bqkv", 1), R("l3_bv"), K("l3_cos").broadcast_to([P, HF]), K("l3_sin").broadcast_to([P, HF]))
    attention_stage(rsD)
    norm_stage([(att_feat[:, 0, :], W("l3_fc"))], bias=R("l3_bfc"))
    cross_stage("l3x", C("l3x_bq"), C("l3x_bk"), R("l3x_bv"),
                lambda raw: (mask3_in.rearrange("b k -> (b k)").partition_broadcast(P),
                             raw[:, 0, :].bitcast(U8)[:, 0:B * SC]),
                "b", 1, D ** -0.5, 1e9 * D ** 0.5, lambda t: t // QT)
    norm_stage([(att_feat[:, 0, :], W("l3x", 384, 512))], bias=R("l3x_bo"))
    route_stage([(x_feat, W("l3_wg"))], None, 16, 2, False)
    pair_stage()
    gated_stage()
    norm_stage([(y_feat, ident)], store=True)
    ctx.close()



def pack(parts, values, shape):
    out = np.zeros(shape, np.float32)
    at = 0
    for name, n in parts:
        v = values[name]
        out[:v.shape[0], at:at + n] = v
        at += n
    return out


def kernel(**inputs):
    import concourse.bacc as bacc
    from concourse.bass_utils import run_bass_kernel_spmd as run

    a = {n: np.asarray(v) for n, v in inputs.items()}

    def chunks(w):
        return w.reshape(-1, P, w.shape[-1]).transpose(1, 0, 2).reshape(P, -1)

    bil = np.zeros((P, 8, P), np.float32)
    for p_ in range(8):
        bil[0:64, p_, 0:64] = a["L1_attn_W_bilinear"][2 * p_]
        bil[64:128, p_, 64:128] = a["L1_attn_W_bilinear"][2 * p_ + 1]
    w1 = a["L3_ffn_W1"].reshape(8, 2, P, 2, 64).transpose(2, 0, 3, 1, 4).reshape(P, -1)
    b2 = np.zeros((P, 4, P), np.float32)
    b2[0:4] = a["L2_ffn_b2"].transpose(1, 0, 2)
    weights = {
        "l0_qkv": a["L0_attn_W_qkv"], "l0_proj": a["L0_attn_W_proj"], "l0_conv": chunks(a["L0_xattn_conv_w"].reshape(512, P)),
        "l0_keys": a["L0_ffn_keys"].T, "l0_rw": a["L0_ffn_rw"].T, "l0_b2": a["L0_ffn_b2"],
        "l1_wq": a["L1_attn_Wq"], "l1_wk": a["L1_attn_Wkv"][:, :1024], "l1_wv": a["L1_attn_Wkv"][:, 1024:],
        "l1_bil": bil.reshape(P, -1), "l1_wo": chunks(a["L1_attn_Wo"]),
        "l1x": np.concatenate([a[f"L1_xattn_W{n}"].T for n in "qkvo"], 1),
        "l2_attn": np.concatenate([a[f"L2_attn_{n}w"] for n in "qkvo"], 1),
        "l2x": np.concatenate([a[f"L2_xattn_W{n}"].T for n in "qkvo"], 1),
        "l2_rw": a["L2_ffn_router_w"].transpose(1, 0, 2).reshape(P, 16), "l2_b2": b2.reshape(P, -1),
        "l3_qkv": a["L3_attn_w_qkv"], "l3_fc": a["L3_attn_w_fc"],
        "l3x": np.concatenate([a[f"L3_xattn_W{n}"] for n in "qkvo"], 1),
        "l3_wg": a["L3_ffn_Wg"].T, "l3_w1": w1, "l3_w2": chunks(a["L3_ffn_W2"].reshape(1024, P)),
        "l3_ws1": a["L3_ffn_Ws1"], "l3_ws2": a["L3_ffn_Ws2"],
    }
    cols = {
        "l0_g": a["L0_attn_ln_gamma"], "l0_b": a["L0_attn_ln_beta"], "l0_bqkv": a["L0_attn_b_qkv"],
        "conv_b": a["L0_xattn_conv_b"], "l0_b1": a["L0_ffn_b1"], "l1_g": a["L1_attn_gamma"],
        "l1x_bq": a["L1_xattn_bq"], "l1x_bk": a["L1_xattn_bk"], "l2_g": a["L2_ffn_ln_g"], "l2_b": a["L2_ffn_ln_b"],
        "l2_b1": a["L2_ffn_b1"], "l3_bqkv": a["L3_attn_b_qkv"], "l3x_bq": a["L3_xattn_bq"],
        "l3x_bk": a["L3_xattn_bk"],
    }
    cols = {n: v.reshape(-1, P).T for n, v in cols.items()}
    rows = {
        "l0_bv": a["L0_attn_b_qkv"][256:], "l0_bproj": a["L0_attn_b_proj"], "l0_rb": a["L0_ffn_rb"],
        "l1x_bv": a["L1_xattn_bv"], "l1x_bo": a["L1_xattn_bo"], "l1f_bias": a["L1_ffn_bias"],
        "l1f_scale": a["L1_ffn_weight_scale"], "l2x_bo": a["L2_xattn_bo"], "l2_rb": a["L2_ffn_router_b"].reshape(-1),
        "l3_bv": a["L3_attn_b_qkv"][256:], "l3_bfc": a["L3_attn_b_fc"], "l3x_bv": a["L3_xattn_bv"],
        "l3x_bo": a["L3_xattn_bo"],
    }
    w2_0 = a["L0_ffn_w2"].transpose(0, 2, 1).reshape(16, 4, P, P).transpose(0, 2, 1, 3).reshape(16, P, 512)
    w2_2 = a["L2_ffn_w2"].reshape(16, 4, P, P).transpose(0, 2, 1, 3).reshape(16, P, 512)
    arrays = {
        "x": a["x"], "context": a["ctx_1024"], "mask1": a["mask_1x1xSxS2_if1"], "mask2": a["mask_Bx1xSxS2_ik1"],
        "mask3": a["mask_BxS2_bk0"], "packed": a["L1_ffn_packed_weight"],
        "constants": shape_constants(), "weights": pack(WEIGHTS, weights, (P, W_N)),
        "weights1": pack(WEIGHTS_1, weights, (P, W1_N)), "weights3": pack(WEIGHTS_3, weights, (P, W3_N)),
        "cols": pack(COLS, cols, (P, C_N)), "rows": np.concatenate([rows[n] for n, _ in ROWS]),
        "experts0": np.concatenate([a["L0_ffn_w1"].transpose(0, 2, 1), w2_0], 2),
        "experts2": np.concatenate([a["L2_ffn_w1"].reshape(16, P, 512), w2_2], 2),
    }
    nc = bacc.Bacc("TRN2", target_bir_lowering=False, num_devices=1)
    arrays = {f"in_{n}": np.ascontiguousarray(v) for n, v in arrays.items()}
    args = [nc.dram_tensor(n, v.shape, mybir.dt.from_np(v.dtype), kind="ExternalInput").ap()
            for n, v in arrays.items()]
    out = nc.dram_tensor("out_x", (B, S, D), F32, kind="ExternalOutput").ap()
    build(nc, *args, out)
    return run(nc, [arrays], core_ids=[0]).results[0]["out_x"]
```

```python
from contextlib import ExitStack

import concourse.bass as bass
from concourse import mybir
import numpy as np

F32 = mybir.dt.float32
F32R = mybir.dt.float32r
BF16 = mybir.dt.bfloat16
I32 = mybir.dt.int32
U8 = mybir.dt.uint8
ACT = mybir.ActivationFunctionType
ALU = mybir.AluOpType
X_AXIS = mybir.AxisListType.X

P = 128
B, S, D = 2, 512, 128
T = B * S
NT = T // P
QT = S // P
SC = 77
H, DH = 16, 8
WH = 64
HF = 512
EPS = 1e-5
HUGE = 3.0e38


WEIGHTS = [
    ("l0_qkv", 384), ("l0_proj", 128), ("l0_conv", 512), ("l0_keys", 16), ("l0_rw", 16), ("l0_b2", 128),
    ("l1x", 512), ("l2_attn", 512), ("l2x", 512), ("l2_rw", 16), ("l2_b2", 512), ("l3x", 512),
]
WEIGHTS_1 = [
    ("l1_wq", 1024), ("l1_wk", 1024), ("l1_wv", 1024), ("l1_bil", 1024), ("l1_wo", 1024),
]
WEIGHTS_3 = [
    ("l3_qkv", 384), ("l3_fc", 128), ("l3_wg", 16), ("l3_w1", 2048), ("l3_w2", 1024),
    ("l3_ws1", 256), ("l3_ws2", 128),
]
COLS = [
    ("l0_g", 1), ("l0_b", 1), ("l0_bqkv", 3), ("conv_b", 1), ("l0_b1", 64), ("l1_g", 1), ("l1x_bq", 1),
    ("l1x_bk", 1), ("l2_g", 16), ("l2_b", 16), ("l2_b1", 64), ("l3_bqkv", 3), ("l3x_bq", 1), ("l3x_bk", 1),
]
ROWS = [
    ("l0_bv", 128), ("l0_bproj", 128), ("l0_rb", 16), ("l1x_bv", 128), ("l1x_bo", 128), ("l1f_bias", 128),
    ("l1f_scale", 1), ("l2x_bo", 128), ("l2_rb", 16), ("l3_bv", 128), ("l3_bfc", 128), ("l3x_bv", 128),
    ("l3x_bo", 128),
]
CONSTS = [
    ("ident", 128), ("rot", 128), ("headmask", 16), ("sel", 16), ("marks", 4), ("stack", 4), ("causal_s", 128),
    ("causal_st", 128), ("l1_cos", 512), ("l1_sin", 512), ("l2_cos", 512), ("l2_sin", 512), ("l3_cos", 1),
    ("l3_sin", 1),
]


def offsets(parts):
    at, out = 0, {}
    for name, n in parts:
        out[name] = (at, n)
        at += n
    return out, at


W_AT, W_N = offsets(WEIGHTS)
W1_AT, W1_N = offsets(WEIGHTS_1)
W3_AT, W3_N = offsets(WEIGHTS_3)
C_AT, C_N = offsets(COLS)
R_AT, R_N = offsets(ROWS)
K_AT, K_N = offsets(CONSTS)

CAUSAL = -1.0e10


def shape_constants():
    k = np.zeros((P, K_N), np.float32)

    def put(name, a):
        at, n = K_AT[name]
        k[:, at:at + n] = a

    put("ident", np.eye(P))
    rot = np.zeros((P, P))
    for i in range(0, P, 2):
        rot[i + 1, i] = -1.0
        rot[i, i + 1] = 1.0
    put("rot", rot)
    feature = np.arange(P)
    put("headmask", feature[:, None] // DH == np.arange(H)[None, :])
    row = np.arange(P)[:, None]
    put("sel", (row == np.arange(16)) | (row == 32 + np.arange(16)))
    put("marks", (row == 96 + np.arange(4)) | (row == 100 + np.arange(4)))
    put("stack", (row % 32 // DH == np.arange(4)) & (row < 96))
    token = np.arange(P)
    put("causal_s", np.where(token[None, :] > token[:, None], CAUSAL * np.sqrt(DH), 0.0))
    put("causal_st", np.where(token[:, None] > token[None, :], CAUSAL * np.sqrt(DH), 0.0))
    pos = np.arange(S, dtype=np.float32)
    theta = (1.0 / np.float32(10000.0) ** (np.arange(0, WH, 2, dtype=np.float32) / np.float32(WH))).astype(np.float32)
    freq = (pos[:, None] * theta[None, :]).astype(np.float32)
    emb = np.concatenate([freq, freq], -1).T
    put("l1_cos", np.tile(np.cos(emb), (2, 1)))
    put("l1_sin", np.tile(np.sin(emb), (2, 1)))
    inv = (1.0 / np.float32(10000.0) ** (np.arange(0, DH, 2, dtype=np.float32) / np.float32(DH))).astype(np.float32)
    f2 = np.repeat((pos[:, None] * inv[None, :]).astype(np.float32).T, 2, axis=0)
    put("l2_cos", np.tile(np.cos(f2), (H, 1)))
    put("l2_sin", np.tile(np.sin(f2), (H, 1)))
    f3 = np.repeat(np.arange(H, dtype=np.float32)[:, None] * inv[None, :], 2, axis=1).reshape(P, 1)
    put("l3_cos", np.cos(f3))
    put("l3_sin", np.sin(f3))
    return k


class Signal:

    def __init__(self, nc, name):
        self.sem = nc.alloc_semaphore(name)
        self.base = 0
        self.total = 0

    def up(self, n=1):
        self.total += n
        return self.sem, n

    def at(self, n):
        return self.sem, self.base + n


    def absolute(self, n):
        return self.sem, n


class Signals:
    def __init__(self, nc):
        self.nc, self.by_name = nc, {}

    def __call__(self, name):
        if name not in self.by_name:
            self.by_name[name] = Signal(self.nc, name)
        return self.by_name[name]

    def settle(self):
        for s in self.by_name.values():
            s.base = s.total


def build(nc, x_in, ctx_in, mask1_in, mask2_in, mask3_in, packed_in, const_in, weights_in, weights1_in, weights3_in, cols_in,
          rows_in,           l0_experts, l2_experts, out):
    ctx = ExitStack()

    def sb(name, shape, dt=F32):
        return ctx.enter_context(nc.sbuf_tensor(name, shape, dt))

    signals = Signals(nc)
    bank = ctx.enter_context(nc.psum_tensor("bank", [P, 8, HF], F32))

    consts = sb("consts", [P, K_N])
    weights = sb("weights", [P, W_N])
    weights13 = sb("weights13", [P, max(W1_N, W3_N)])
    cols = sb("cols", [P, C_N])
    rows = sb("rows", [P, R_N])

    def K(name):
        at, n = K_AT[name]
        return consts[:, at:at + n]

    def W(name, a=0, b=None):
        table, tile = (W_AT, weights) if name in W_AT else (W1_AT if name in W1_AT else W3_AT, weights13)
        at, n = table[name]
        return tile[:, at + a:at + (n if b is None else b)]

    def C(name, i=0):
        at, _ = C_AT[name]
        return cols[:, at + i:at + i + 1]

    def R(name, a=0, b=None):
        at, n = R_AT[name]
        return rows[:, at + a:at + (n if b is None else b)]

    ident = K("ident")
    warm = sb("warm", [P, 2])
    x_tok = sb("x_tok", [P, NT, D])
    x_feat = sb("x_feat", [P, T])
    hat_feat = sb("hat_feat", [P, T])
    y_feat = sb("y_feat", [P, T])
    stats = sb("stats", [P, NT, 6])
    moments = sb("moments", [P, NT, 2])
    rstd = sb("rstd", [P, NT])
    ctx_tok = sb("ctx_tok", [P, B, D])
    ctx_feat = sb("ctx_feat", [P, B * SC])
    identb = sb("identb", [P, P], BF16)
    causal_s = sb("causal_s", [P, P], BF16)
    causal_st = sb("causal_st", [P, P], BF16)
    q_feat = sb("q_feat", [P, T])
    k_feat = sb("k_feat", [P, T])
    operands = sb("operands", [P, 4, T])
    parts = {n: operands[:, i, :].bitcast(F32R) for i, n in enumerate(("q_hi", "q_lo", "k_hi", "k_lo"))}
    rot_tmp = y_feat
    res_tok = hat_feat[:, :].rearrange("p (t d) -> p t d", d=D)
    sum_tok = k_feat[:, :].rearrange("p (t d) -> p t d", d=D)
    KS = sb("KS", [P, 2, 4, HF], F32R)
    QM = sb("QM", [P, 2, HF], F32R)
    v_aug = sb("v_aug", [P, NT, H, 32])
    v_wide = v_aug[:, :, :, :].rearrange("p a b c -> p (a b c)")[:, 0:2 * T].rearrange(
        "p (s t n) -> p s t n", s=2, t=NT)
    probs = sb("probs", [P, 2, 4, HF])
    neg_max = sb("neg_max", [P, QT, 4])
    max_parts = sb("max_parts", [P, QT, 8], F32R)
    max_wide = sb("max_wide", [P, QT, 66])
    o_feat = sb("o_feat", [P, HF])
    o_sums = sb("o_sums", [P, HF])
    o_tok = sb("o_tok", [P, B, QT, P])
    rsum = sb("rsum", [P, QT, 4])
    att_feat = sb("att_feat", [P, 8, T])
    NW = 4
    wring = probs[:, :, :, :].rearrange("p a b n -> p (a b n)").rearrange("p (w n) -> p w n", w=NW)
    sel = sb("sel", [P, 16, P], F32R)
    gate_parts = sb("gate_parts", [P, T], F32R)
    gate_rows = q_feat[0:16, :]
    x_hi = QM[:, :, :].rearrange("p s n -> p (s n)")
    x_lo = sb("x_lo", [P, T], F32R)
    bias_buf = sb("bias_buf", [P, 2, 4])

    def wide_q(slot, j):
        if slot == 0:
            return sel[:, :, :].rearrange("p a n -> p (a n)")[:, j * T:(j + 1) * T].rearrange("p (x n) -> p x n", x=2)
        return QM[:, :, :] if j == 0 else gate_parts[:, :].rearrange("p (x n) -> p x n", x=2)
    gates = sb("gates", [P, NT, 16])
    gate_sum = sb("gate_sum", [P, NT])

    flat = att_feat[:, :, :].rearrange("p a n -> p (a n)")
    scratch = flat[:, 2 * T:2 * T + 7 * HF]
    scaled = o_feat[:, :]
    x_keep = att_feat[:, 7, :].rearrange("p (t d) -> p t d", d=D)
    zeros = o_sums
    lg = sb("lg", [P, NT, 24])
    lg_rep = sb("lg_rep", [P, NT, 24])
    top8 = sb("top8", [P, NT, 8])
    top_in = sb("top_in", [P, NT, 8])
    picked = sb("picked", [P, NT, 16])
    small = sb("small", [P, NT, 4])

    loads = {n: nc.alloc_semaphore(n) for n in ("ld_const", "ld_x", "ld_w", "ld_w1", "ld_w3", "ld_ctx")}


    def steps(eng, sig):
        def step(ins):
            ins.then_inc(*sig.up())
            eng.wait_ge(sig.sem, sig.total)
        return step

    def marked_rows(eng):
        for j in range(4):
            for s in range(2):
                eng.tensor_scalar(KS[96:128, s, j, :], zeros[96:128, :], K("marks")[96:128, j:j + 1], None, ALU.add)

    def constant_rows(dve):
        marked_rows(dve)
        for e in range(16):
            dve.tensor_scalar(sel[:, e, :], zeros[:, 0:P], K("sel")[:, e:e + 1], None, ALU.add)

    with nc.Block() as block:
        t_done, init_done = signals("t_done"), signals("init_done")

        @block.sync
        def _(sp):
            sp.dma_start(consts[:, :], const_in).then_inc(loads["ld_const"], 16)
            sp.dma_start(x_tok[:, :, :], x_in.rearrange("b (t p) d -> p (b t) d", p=P)).then_inc(loads["ld_x"], 16)
            sp.dma_start(cols[:, :], cols_in).then_inc(loads["ld_const"], 16)
            sp.dma_start(rows[:, :], rows_in.partition_broadcast(P)).then_inc(loads["ld_const"], 16)
            sp.dma_start(ctx_tok[0:SC, :, :], ctx_in.rearrange("b s d -> s b d")).then_inc(loads["ld_ctx"], 16)
            sp.dma_start(weights[:, :], weights_in).then_inc(loads["ld_w"], 16)
            sp.dma_start(weights13[:, 0:W1_N], weights1_in).then_inc(loads["ld_w1"], 16)

        @block.gpsimd
        def _(pool):
            pool.memset(KS[:, :, :, :].bitcast(F32), 0.0).then_inc(*init_done.up())
            pool.memset(QM[:, :, :].bitcast(F32), 0.0)
            pool.memset(v_aug[:, :, :, :], 0.0).then_inc(*init_done.up())
            pool.memset(max_wide[:, :, :], 0.0)
            pool.memset(warm[:, :], 1.0)
            pool.memset(gate_parts[:, :].bitcast(F32), 0.0)
            pool.memset(zeros[:, :], 0.0).then_inc(*init_done.up())
            pool.wait_ge(*init_done.at(3))
            pool.memset(v_aug[:, :, :, DH:DH + 1], 1.0)

        @block.vector
        def _(dve):
            dve.wait_ge(loads["ld_const"], 48)
            dve.tensor_copy(identb[:, :], ident)
            dve.tensor_copy(causal_s[:, :], K("causal_s"))
            dve.tensor_copy(causal_st[:, :], K("causal_st"))
            dve.wait_ge(*init_done.at(3))
            constant_rows(dve)

        @block.tensor
        def _(pe):
            pe.wait_ge(loads["ld_const"], 48)
            pe.wait_ge(loads["ld_x"], 16)
            for hf in range(2):
                for q in range(QT):
                    ins = pe.transpose(bank[:, hf, q * P:(q + 1) * P], x_tok[:, hf * QT + q, :], ident)
                ins.then_inc(*t_done.up())
            pe.wait_ge(loads["ld_ctx"], 16)
            for b in range(B):
                ins = pe.transpose(bank[:, 2, b * SC:(b + 1) * SC], ctx_tok[0:SC, b, :], ident[0:SC, 0:SC])
            ins.then_inc(*t_done.up())

        @block.scalar
        def _(act):
            for hf in range(2):
                act.wait_ge(*t_done.at(hf + 1))
                act.copy(x_feat[:, hf * HF:(hf + 1) * HF], bank[:, hf, :])
            act.wait_ge(*t_done.at(3))
            act.copy(ctx_feat[:, :], bank[:, 2, 0:B * SC])
    signals.settle()

    def preload(act, function):
        act.activation(warm[:, 1:2], warm[:, 0:1], function)

    def weights_here(pe):
        pe.wait_ge(loads["ld_w"], 16)
        for name in layer_loads:
            pe.wait_ge(loads[name], 16)

    layer_loads = []

    def norm_stage(terms=None, bias=None, residual_scale=None, norm=True, hat=None, store=False, plus=None,
                   keep=False):
        y_done, res_done, std_in, std_out, x_done, xt_done, hat_done, hat_turned, stored, xt_used = (
            signals(n) for n in ("y_done", "res_done", "std_in", "std_out", "x_done", "xt_done", "hat_done",
                                 "hat_turned", "stored", "xt_used"))
        step_sig = signals("dve_step")
        x_norm = terms is not None and norm
        HV = [slice(hf * QT, (hf + 1) * QT) for hf in range(2)]
        hat_std = 2 if x_norm else 0

        with nc.Block() as block:
            if bias is not None or keep:
                @block.gpsimd
                def _(pool):
                    for hf in range(2 if bias is not None else 0):
                        pool.tensor_tensor(res_tok[:, HV[hf], :], x_tok[:, HV[hf], :],
                                           bias.unsqueeze(1).broadcast_to([P, QT, D]), ALU.add
                                           ).then_inc(*res_done.up())
                    for hf in range(2 if keep else 0):
                        pool.wait_ge(*x_done.at(hf + 1))
                        pool.tensor_copy(x_keep[:, HV[hf], :], x_tok[:, HV[hf], :])

            @block.tensor
            def _(pe):
                weights_here(pe)
                if terms is not None:
                    for hf in range(2):
                        for q in range(QT):
                            t = hf * QT + q
                            for n, (operand, w) in enumerate(terms):
                                to, tile = bank[:, hf, q * P:(q + 1) * P], operand[:, t * P:(t + 1) * P]
                                if w is None:
                                    ins = pe.transpose(to, tile, ident)
                                else:
                                    ins = pe.matmul(to, tile, w, start=(n == 0), stop=(n == len(terms) - 1))
                        ins.then_inc(*y_done.up())
                    for hf in range(2 if not store else 0):
                        pe.wait_ge(*x_done.at(hf + 1))
                        for q in range(QT):
                            ins = pe.transpose(bank[:, 2 + hf, q * P:(q + 1) * P], x_tok[:, hf * QT + q, :], ident)
                        ins.then_inc(*xt_done.up())
                for hf in range(2 if hat is not None else 0):
                    pe.wait_ge(*hat_done.at(hf + 1))
                    for q in range(QT):
                        ins = pe.transpose(bank[:, 4 + hf, q * P:(q + 1) * P], sum_tok[:, hf * QT + q, :], ident)
                    ins.then_inc(*hat_turned.up())

            @block.vector
            def _(dve):
                step = steps(dve, step_sig)

                def layer_norm(source, dest, hf, n):
                    for t in range(hf * QT, (hf + 1) * QT):
                        ins = dve.bn_stats(stats[:, t, :], source[:, t, :])
                    step(ins)
                    for t in range(hf * QT, (hf + 1) * QT):
                        ins = dve.bn_aggr(moments[:, t, :], stats[:, t, :])
                    step(ins)
                    dve.tensor_scalar(rstd[:, HV[hf]], moments[:, HV[hf], 1], EPS, None, ALU.add
                                      ).then_inc(*std_in.up())
                    dve.wait_ge(*std_out.at(n + 1))
                    step(dve.reciprocal(rstd[:, HV[hf]], rstd[:, HV[hf]]))
                    for t in range(hf * QT, (hf + 1) * QT):
                        ins = dve.tensor_scalar(dest[:, t, :], source[:, t, :], moments[:, t, 0:1], rstd[:, t:t + 1],
                                                ALU.subtract, ALU.mult)
                    return ins

                for hf in range(2 if terms is not None else 0):
                    half = HV[hf]
                    y = bank[:, hf, :].rearrange("p (q d) -> p q d", d=D)
                    dve.wait_ge(*y_done.at(hf + 1))
                    into = sum_tok if norm else x_tok
                    if residual_scale is not None:
                        for q in range(QT):
                            t = hf * QT + q
                            ins = dve.scalar_tensor_tensor(out=into[:, t, :], in0=x_tok[:, t, :],
                                                           scalar=residual_scale[:, t:t + 1], in1=y[:, q, :],
                                                           op0=ALU.mult, op1=ALU.add)
                    else:
                        if bias is not None:
                            dve.wait_ge(*res_done.at(hf + 1))
                        ins = dve.tensor_tensor(into[:, half, :], y, (res_tok if bias is not None else x_tok)[:, half, :],
                                                ALU.add)
                    if norm:
                        step(ins)
                        if plus is not None:
                            step(dve.tensor_tensor(into[:, half, :], into[:, half, :], plus[:, half, :], ALU.add))
                        ins = layer_norm(sum_tok, x_tok, hf, hf)
                    ins.then_inc(*x_done.up())
                for hf in range(2 if hat is not None else 0):
                    if terms is not None:
                        dve.wait_ge(*x_done.at(hf + 1))
                    layer_norm(x_tok, sum_tok, hf, hat_std + hf).then_inc(*hat_done.up())

            @block.scalar
            def _(act):
                def root(hf, n):
                    act.wait_ge(*std_in.at(n + 1))
                    act.activation(rstd[:, HV[hf]], rstd[:, HV[hf]], ACT.Sqrt).then_inc(*std_out.up())

                def copy_x(hf):
                    act.wait_ge(*xt_done.at(hf + 1))
                    act.copy(x_feat[:, hf * HF:(hf + 1) * HF], bank[:, 2 + hf, :])

                def copy_hat(hf):
                    act.wait_ge(*hat_turned.at(hf + 1))
                    o = hat_feat[:, hf * HF:(hf + 1) * HF]
                    scale, shift = hat
                    if shift is not None:
                        act.activation(o, bank[:, 4 + hf, :], ACT.Identity, bias=shift, scale=scale)
                    elif scale is not None:
                        act.activation(o, bank[:, 4 + hf, :], ACT.Copy, scale=scale)
                    else:
                        act.copy(o, bank[:, 4 + hf, :])

                preload(act, ACT.Sqrt)
                for hf in range(2 if x_norm else 0):
                    root(hf, hf)
                if hat is None and not store:
                    preload(act, ACT.Exp)
                for hf in range(2):
                    if terms is not None and not store:
                        copy_x(hf)
                    if hat is not None:
                        root(hf, hat_std + hf)
                if hat is not None:
                    preload(act, ACT.Exp)
                    for hf in range(2):
                        copy_hat(hf)

            if store:
                @block.sync
                def _(sp):
                    view = out.rearrange("b (t p) d -> p (b t) d", p=P)
                    for hf in range(2):
                        sp.wait_ge(*x_done.at(hf + 1))
                        sp.dma_start(view[:, HV[hf], :], x_tok[:, HV[hf], :]).then_inc(*stored.up(16))
                    sp.wait_ge(*stored.at(32))
        signals.settle()

    def project_stage(source, wq, wk, wv, bq, bk, bv, cos=None, sin=None, restore=False):
        proj, raw, v_done, rotated, rot_used, hi_done = (
            signals(n) for n in ("proj", "raw", "v_done", "rotated", "rot_used", "hi_done"))
        step_sig = signals("dve_step")
        rotary = cos is not None
        items = [(n, hf) for n in range(2) for hf in range(2)]
        feats = (q_feat, k_feat)

        with nc.Block() as block:
            @block.tensor
            def _(pe):
                weights_here(pe)
                for i, (n, hf) in enumerate(items):
                    pe.matmul(bank[:, i, :], (wq, wk)[n], source[:, hf * HF:(hf + 1) * HF], start=True,
                              stop=True).then_inc(*proj.up())
                for t in range(NT):
                    ins = pe.matmul(bank[:, 6 + t // QT, (t % QT) * P:(t % QT + 1) * P], source[:, t * P:(t + 1) * P],
                                    wv, start=True, stop=True)
                    if t % QT == QT - 1:
                        ins.then_inc(*v_done.up())
                if rotary:
                    for i, (n, hf) in enumerate(items):
                        pe.wait_ge(*raw.at(i + 1))
                        if i >= 2:
                            pe.wait_ge(*rot_used.at(i - 1))
                        pe.matmul(bank[:, 4 + i % 2, :], K("rot"), feats[n][:, hf * HF:(hf + 1) * HF], start=True,
                                  stop=True).then_inc(*rotated.up())

            @block.scalar
            def _(act):
                for i, (n, hf) in enumerate(items):
                    act.wait_ge(*proj.at(i + 1))
                    bias = (bq, bk)[n]
                    o = feats[n][:, hf * HF:(hf + 1) * HF]
                    if bias is not None:
                        ins = act.activation(o, bank[:, i, :], ACT.Identity, bias=bias)
                    else:
                        ins = act.copy(o, bank[:, i, :])
                    ins.then_inc(*raw.up())
                for i, (n, hf) in enumerate(items):
                    act.wait_ge(*(rot_used if rotary else raw).at(i + 1))
                    hi = parts[("q_hi", "k_hi")[n]]
                    act.copy(hi[:, hf * HF:(hf + 1) * HF], feats[n][:, hf * HF:(hf + 1) * HF]
                             ).then_inc(*hi_done.up())

            @block.vector
            def _(dve):
                step = steps(dve, step_sig)
                for hf in range(2):
                    dve.wait_ge(*v_done.at(hf + 1))
                    half = slice(hf * QT, (hf + 1) * QT)
                    v = bank[:, 6 + hf, :]
                    for q in range(QT):
                        o = v_aug[:, hf * QT + q, :, 0:DH]
                        vq = v[:, q * P:(q + 1) * P].rearrange("p (h d) -> p h d", d=DH)
                        if bv is not None:
                            dve.tensor_tensor(o, vq, bv.rearrange("p (h d) -> p h d", d=DH), ALU.add)
                        else:
                            dve.tensor_copy(o, vq)
                if rotary:
                    for i, (n, hf) in enumerate(items):
                        f = feats[n][:, hf * HF:(hf + 1) * HF]
                        tmp = rot_tmp[:, hf * HF:(hf + 1) * HF]
                        dve.wait_ge(*rotated.at(i + 1))
                        dve.tensor_tensor(tmp, bank[:, 4 + i % 2, :], sin, ALU.mult)
                        step(dve.tensor_tensor(f, f, cos, ALU.mult))
                        dve.tensor_tensor(f, f, tmp, ALU.add).then_inc(*rot_used.up())
                for i, (n, hf) in enumerate(items):
                    dve.wait_ge(*hi_done.at(i + 1))
                    sl = slice(hf * HF, (hf + 1) * HF)
                    dve.tensor_tensor(parts[("q_lo", "k_lo")[n]][:, sl], feats[n][:, sl],
                                      parts[("q_hi", "k_hi")[n]][:, sl].bitcast(F32), ALU.subtract)

            if restore:
                @block.gpsimd
                def _(pool):
                    pool.memset(QM[96:128, :, :].bitcast(F32), 0.0)
                    marked_rows(pool)
        signals.settle()

    def wide_stage():
        units = [(p_, b) for p_ in range(8) for b in range(B)]
        NU, NG = len(units), 2 * QT
        MX, ST, PVB, SUMS, MISC, PJ = (0, 1), (2, 3), 4, 5, 6, 7
        Q, RQ, KK, RK, BIL, V = range(6)
        PIECE_AT = {0: Q, 1: RQ, 2: KK, 3: RK, 5: BIL}
        MAXIMA_AT = {3: (0, 1), 4: (2, 3), 5: (4, 5), 6: (6, 7)}
        (proj_done, proj_read, cos_done, rot_done, hi_done, lo_done, m_clear, mx_done, mx_used, mp_done, mt_done,
         m_ready, st_done, exp_done, pv_done, res_copied, att_done, added, sums_done, inverted) = (signals(n) for n in (
             "proj_done", "proj_read", "cos_done", "rot_done", "hi_done", "lo_done", "m_clear", "mx_done", "mx_used",
             "mp_done", "mt_done", "m_ready", "st_done", "exp_done", "pv_done", "res_copied", "att_done", "added",
             "sums_done", "inverted"))
        op_loaded = [[signals(f"op_loaded{s}{j}") for j in range(2)] for s in range(2)]
        step_sig = signals("dve_step")
        part_buf = operands[:, :, :].rearrange("p n t -> p (n t)").rearrange("p (s n t) -> p s n t", s=2, n=4)
        cos_buf = o_tok[:, :, :, :].rearrange("p b q d -> p (b q d)").rearrange("p (n t) -> p n t", n=2)
        rot_buf = rot_tmp[:, :].rearrange("p (n t) -> p n t", n=2)

        def slot(u):
            return u % 2

        def raw(u, n):
            return (q_feat, k_feat)[n][:, slot(u) * HF:(slot(u) + 1) * HF]

        def part(u, n, low):
            return part_buf[:, slot(u), 2 * n + low, :]

        def q_tile(u, j, ab):
            return wide_q(slot(u), j)[:, ab, :]

        def k_tile(u, j, ab):
            return KS[:, slot(u), 2 * j + ab, :]

        sum_buf = v_aug[:, :, :, :].rearrange("p a b c -> p (a b c)")[:, 2 * T:4 * T].rearrange(
            "p (s j n) -> p s j n", s=2, j=2)

        exps = probs[:, :, :, :].rearrange("p a b n -> p (a b n)").rearrange("p (k j n) -> p k j n", k=QT, j=2)

        def values_of(u):
            return v_wide[:, (u // 2) % 2, :, :]

        with nc.Block() as block:
            @block.sync
            def _(sp):
                for u in range(NU):
                    sp.wait_ge(*lo_done.at(2 * u + 2))
                    if u >= 2:
                        sp.wait_ge(*st_done.at((u - 1) * NG))
                    for j in range(2):
                        own, other = slice(64 * j, 64 * j + 64), slice(64 - 64 * j, 128 - 64 * j)
                        q_hi, q_lo, k_hi, k_lo = (part(u, n, low)[own, :] for n in range(2) for low in range(2))
                        moves = [(q_tile(u, j, 0)[own, :], q_hi), (q_tile(u, j, 1)[own, :], q_hi),
                                 (q_tile(u, j, 0)[other, :], q_lo),
                                 (k_tile(u, j, 0)[own, :], k_hi), (k_tile(u, j, 0)[other, :], k_hi),
                                 (k_tile(u, j, 1)[own, :], k_lo)]
                        for to, src in moves:
                            sp.dma_start(to.bitcast(F32), src).then_inc(*op_loaded[slot(u)][j].up(16))

            @block.tensor
            def _(pe):
                weights_here(pe)

                def project(u, piece):
                    p_, b = units[u]
                    c = slice(p_ * P, (p_ + 1) * P)
                    x = hat_feat[:, b * S:(b + 1) * S]
                    if 6 * u + piece:
                        pe.wait_ge(*proj_read.at(6 * u + piece))
                    if piece == BIL:
                        pe.wait_ge(*rot_done.at(2 * u + 2))
                    if piece == V:
                        for q in range(QT):
                            ins = pe.matmul(bank[:, PJ, q * P:(q + 1) * P], x[:, q * P:(q + 1) * P],
                                            W("l1_wv", c.start, c.stop), start=True, stop=True)
                    else:
                        w, operand = {Q: (W("l1_wq", c.start, c.stop), x), KK: (W("l1_wk", c.start, c.stop), x),
                                      RQ: (K("rot"), raw(u, 0)), RK: (K("rot"), raw(u, 1)),
                                      BIL: (W("l1_bil", c.start, c.stop), raw(u, 1))}[piece]
                        ins = pe.matmul(bank[:, PJ, :], w, operand, start=True, stop=True)
                    ins.then_inc(*proj_done.up())

                def maxima(u, i):
                    j, q = divmod(i, QT)
                    n = u * NG + i
                    if q == 0:
                        pe.wait_ge(*op_loaded[slot(u)][j].at(96 * (u // 2 + 1)))
                    if i == 0:
                        pe.wait_ge(*m_clear.at(u + 1))
                    if n >= 2:
                        pe.wait_ge(*mx_used.at(n - 1))
                    for ab in range(2):
                        ins = pe.matmul(bank[:, MX[n % 2], :], q_tile(u, j, ab)[:, q * P:(q + 1) * P],
                                        k_tile(u, j, ab), start=(ab == 0), stop=(ab == 1))
                    ins.then_inc(*mx_done.up())

                def turn_maxima(u):
                    pe.wait_ge(*mp_done.at(u + 1))
                    for q in range(QT):
                        ins = pe.transpose(bank[0:66, MISC, q * P:(q + 1) * P], max_wide[:, q, :], ident)
                    ins.then_inc(*mt_done.up())

                def scores(u, n):
                    kt, j = divmod(n, 2)
                    m = u * NG + n
                    if n == 0:
                        pe.wait_ge(*m_ready.at(u + 1))
                    if m >= 2:
                        pe.wait_ge(*exp_done.at(m - 1))
                    for ab in range(2):
                        ins = pe.matmul(bank[:, ST[m % 2], :], k_tile(u, j, ab)[:, kt * P:(kt + 1) * P],
                                        q_tile(u, j, ab), start=(ab == 0), stop=(ab == 1))
                    ins.then_inc(*st_done.up())

                def values(u, kt):
                    p_, b = units[u]
                    pe.wait_ge(*exp_done.at(u * NG + 2 * kt + 2))
                    if kt == 0 and u >= 1:
                        pe.wait_ge(*res_copied.at(u))
                    for j in range(2):
                        r = slice(64 * j, 64 * j + 64)
                        ins = pe.matmul(bank[r, PVB, :], values_of(u)[:, b * QT + kt, r], exps[:, kt, j, :],
                                        start=(kt == 0), stop=(kt == QT - 1))
                    ins.then_inc(*pv_done.up())

                def sums(u):
                    pe.wait_ge(*added.at((QT - 1) * (u + 1)))
                    if u >= 1:
                        pe.wait_ge(*inverted.at(u))
                    for j in range(2):
                        r = slice(64 * j, 64 * j + 64)
                        ins = pe.matmul(bank[r, SUMS, :], ones128[:, r], sum_buf[:, slot(u), j, :], start=True,
                                        stop=True)
                    ins.then_inc(*sums_done.up())

                for u in range(2):
                    for piece in range(6):
                        project(u, piece)
                for i in range(NG):
                    maxima(0, i)
                turn_maxima(0)
                for u in range(NU):
                    for n in range(NG):
                        scores(u, n)
                        if u + 1 < NU:
                            for i in MAXIMA_AT.get(n, ()):
                                maxima(u + 1, i)
                        if n in PIECE_AT and u + 2 < NU:
                            project(u + 2, PIECE_AT[n])
                        if n % 2 == 1 and u * QT + n // 2 >= 1:
                            values(*divmod(u * QT + n // 2 - 1, QT))
                        if n == 2 and u >= 1:
                            sums(u - 1)
                        if n == NG - 1 and u + 1 < NU:
                            turn_maxima(u + 1)
                            if u + 2 < NU:
                                project(u + 2, V)
                values(NU - 1, QT - 1)
                sums(NU - 1)

            @block.scalar
            def _(act):
                def copy_piece(u, piece):
                    p_, b = units[u]
                    act.wait_ge(*proj_done.at(6 * u + piece + 1))
                    if piece == V:
                        act.copy(values_of(u)[:, b * QT:(b + 1) * QT, :],
                                 bank[:, PJ, :].rearrange("p (t n) -> p t n", n=P)).then_inc(*proj_read.up())
                    else:
                        act.copy(raw(u, 0 if piece == Q else 1), bank[:, PJ, :]).then_inc(*proj_read.up())

                def high(u, n):
                    if n == 0:
                        act.wait_ge(*rot_done.at(2 * u + 1))
                        act.copy(part(u, 0, 0).bitcast(F32R), raw(u, 0)).then_inc(*hi_done.up())
                    else:
                        act.wait_ge(*proj_done.at(6 * u + BIL + 1))
                        act.copy(part(u, 1, 0).bitcast(F32R), bank[:, PJ, :]).then_inc(*hi_done.up())

                def maxima_rows(u):
                    act.wait_ge(*mt_done.at(u + 1))
                    act.copy(q_tile(u, 0, 1)[64:66, :], bank[64:66, MISC, :])
                    act.copy(q_tile(u, 1, 1)[0:2, :], bank[0:2, MISC, :]).then_inc(*m_ready.up())

                def exponentials(u, n):
                    kt, j = divmod(n, 2)
                    m = u * NG + n
                    act.wait_ge(*st_done.at(m + 1))
                    if j == 0 and u >= 1:
                        act.wait_ge(*pv_done.at((u - 1) * QT + kt + 1))
                        act.wait_ge(*added.at((QT - 1) * (u - 1) + max(kt, 1)))
                    act.activation(exps[:, kt, j, :], bank[:, ST[m % 2], :], ACT.Exp, scale=WH ** -0.5
                                   ).then_inc(*exp_done.up())

                def copy_result(u):
                    act.wait_ge(*pv_done.at((u + 1) * QT))
                    if u >= 1:
                        act.wait_ge(*att_done.at(u))
                    act.copy(o_feat[:, :], bank[:, PVB, :]).then_inc(*res_copied.up())

                for u in range(2):
                    copy_piece(u, Q)
                    copy_piece(u, KK)
                    high(u, 0)
                    high(u, 1)
                    copy_piece(u, V)
                maxima_rows(0)
                for u in range(NU):
                    for n in range(NG):
                        exponentials(u, n)
                        if u + 2 < NU:
                            if n in PIECE_AT and PIECE_AT[n] in (Q, KK):
                                copy_piece(u + 2, PIECE_AT[n])
                            if n == 3:
                                high(u + 2, 0)
                            if n == 5:
                                high(u + 2, 1)
                        if n == 1 and u >= 1:
                            copy_result(u - 1)
                        if n == NG - 1 and u + 1 < NU:
                            maxima_rows(u + 1)
                            if u + 2 < NU:
                                copy_piece(u + 2, V)
                copy_result(NU - 1)

            @block.vector
            def _(dve):
                step = steps(dve, step_sig)

                def cosines(u, n):
                    dve.wait_ge(*proj_read.at(6 * u + (Q, KK)[n] + 1))
                    if u >= 1:
                        dve.wait_ge(*rot_done.at(2 * u + n - 1))
                    dve.tensor_tensor(cos_buf[:, n, :], raw(u, n), K("l1_cos"), ALU.mult).then_inc(*cos_done.up())

                def rotate(u, n):
                    dve.wait_ge(*proj_done.at(6 * u + (RQ, RK)[n] + 1))
                    ins = dve.tensor_tensor(rot_buf[:, n, :], bank[:, PJ, :], K("l1_sin"), ALU.mult)
                    ins.then_inc(*proj_read.up())
                    dve.wait_ge(*proj_read.at(6 * u + (RQ, RK)[n] + 1))
                    dve.wait_ge(*cos_done.at(2 * u + n + 1))
                    dve.tensor_tensor(raw(u, n), cos_buf[:, n, :], rot_buf[:, n, :], ALU.add).then_inc(*rot_done.up())

                def low(u, n):
                    dve.wait_ge(*hi_done.at(2 * u + n + 1))
                    if n == 0:
                        dve.tensor_tensor(part(u, 0, 1).bitcast(F32R), raw(u, 0), part(u, 0, 0), ALU.subtract
                                          ).then_inc(*lo_done.up())
                    else:
                        dve.tensor_tensor(part(u, 1, 1).bitcast(F32R), bank[:, PJ, :], part(u, 1, 0), ALU.subtract
                                          ).then_inc(*lo_done.up())
                        dve.wait_ge(*lo_done.at(2 * u + 2))
                        dve.sem_inc(*proj_read.up())

                def reduce_maxima(u, i):
                    j, q = divmod(i, QT)
                    n = u * NG + i
                    dve.wait_ge(*mx_done.at(n + 1))
                    dve.tensor_reduce(neg_max[:, q, 1 - j:2 - j], bank[:, MX[n % 2], :], X_AXIS, ALU.max,
                                      negate=True).then_inc(*mx_used.up())

                def split_maxima(u):
                    dve.wait_ge(*mx_used.at((u + 1) * NG))
                    if u >= 1:
                        dve.wait_ge(*mt_done.at(u))
                    hi, lo = max_wide[:, :, 0:65:64], max_wide[:, :, 1:66:64]
                    step(dve.tensor_copy(hi.bitcast(F32R), neg_max[:, :, 0:2]))
                    dve.tensor_tensor(lo.bitcast(F32R), neg_max[:, :, 0:2], hi, ALU.subtract
                                      ).then_inc(*mp_done.up())

                def invert(u, q):
                    if q == 0:
                        dve.wait_ge(*sums_done.at(u + 1))
                        if u >= 1:
                            dve.wait_ge(*att_done.at(u))
                    ins = dve.reciprocal(o_sums[:, q * P:(q + 1) * P], bank[:, SUMS, q * P:(q + 1) * P])
                    if q == QT - 1:
                        ins.then_inc(*inverted.up())

                def normalise(u):
                    p_, b = units[u]
                    dve.wait_ge(*inverted.at(u + 1))
                    dve.wait_ge(*res_copied.at(u + 1))
                    dve.tensor_tensor(att_feat[:, p_, b * S:(b + 1) * S], o_feat[:, :], o_sums[:, :], ALU.mult
                                      ).then_inc(*att_done.up())

                for u in range(2):
                    cosines(u, 0)
                    rotate(u, 0)
                    cosines(u, 1)
                    rotate(u, 1)
                    low(u, 0)
                    low(u, 1)
                for i in range(NG):
                    reduce_maxima(0, i)
                split_maxima(0)
                for u in range(NU):
                    for n in range(NG):
                        if u + 1 < NU:
                            for i in MAXIMA_AT.get(n, ()):
                                reduce_maxima(u + 1, i)
                            if n == 6:
                                split_maxima(u + 1)
                        if u + 2 < NU:
                            if n in (0, 2):
                                cosines(u + 2, n // 2)
                            if n in (1, 3):
                                rotate(u + 2, n // 2)
                            if n == 3:
                                low(u + 2, 0)
                            if n == 5:
                                low(u + 2, 1)
                        if u >= 1 and n >= 3:
                            if n < 7:
                                invert(u - 1, n - 3)
                            else:
                                normalise(u - 1)
                for q in range(QT):
                    invert(NU - 1, q)
                normalise(NU - 1)

            @block.gpsimd
            def _(pool):
                step = steps(pool, signals("pool_step"))
                for s in range(2):
                    for j in range(2):
                        other = slice(64 - 64 * j, 128 - 64 * j)
                        step(pool.memset(wide_q(s, j)[other, 1, :].bitcast(F32), 0.0))
                        step(pool.memset(KS[other, s, 2 * j + 1, :].bitcast(F32), 1.0))
                    pool.sem_inc(*m_clear.up())

                def add_up(u, kt):
                    pool.wait_ge(*exp_done.at(u * NG + 2 * kt + 2))
                    if kt == 1 and u >= 2:
                        pool.wait_ge(*sums_done.at(u - 1))
                    if kt > 1:
                        pool.wait_ge(*added.at((QT - 1) * u + kt - 1))
                    pool.tensor_tensor(sum_buf[:, slot(u), :, :], exps[:, 0, :, :] if kt == 1 else
                                       sum_buf[:, slot(u), :, :], exps[:, kt, :, :], ALU.add
                                       ).then_inc(*added.up())

                def clear_maxima(u):
                    pool.wait_ge(*st_done.at((u - 1) * NG))
                    pool.wait_ge(*added.at((QT - 1) * (u - 1)))
                    step(pool.memset(q_tile(u, 0, 1)[64:66, :].bitcast(F32), 0.0))
                    step(pool.memset(q_tile(u, 1, 1)[0:2, :].bitcast(F32), 0.0))
                    pool.sem_inc(*m_clear.up())

                for u in range(NU):
                    for kt in range(1, QT):
                        add_up(u, kt)
                    if u + 2 < NU:
                        clear_maxima(u + 2)
        signals.settle()

    def attention_stage(scale, causal=False, guard=False):
        NJ = 4
        units = [(b, g) for g in range(4) for b in range(B)]
        NU = len(units)
        MX_BANKS = [0, 1, 2]
        ST_BANKS = [3, 4, 5]
        NX, NS = len(MX_BANKS), len(ST_BANKS)
        NG = QT * NJ
        PVB, MISC = 6, 7
        LEAD = 3
        TURN = NG - LEAD
        START = 1
        COPY, RESULT, FLUSH = 2, 5, 9

        def maxima_of(n):
            a, w = n - START, TURN - START
            return range(a * NG // w, (a + 1) * NG // w) if 0 <= a < w else range(0)

        (mx_done, mx_used, mp_done, mt_done, m_ready, st_done, exp_done, pv_done, o_ready, ot_done, on_done,
         fl_done, fl_used, built, first_built) = (signals(n) for n in (
             "mx_done", "mx_used", "mp_done", "mt_done", "m_ready", "st_done", "exp_done", "pv_done", "o_ready",
             "ot_done", "on_done", "fl_done", "fl_used", "built", "first_built"))
        GROUPS_AT_ONCE = 3
        base_loaded = [signals(f"base_loaded{i}") for i in range(GROUPS_AT_ONCE)]
        step_sig = signals("dve_step")

        def key_op(u, j):
            return KS[:, u % 2, j, :]

        def query_op(u, j):
            return QM[:, u % 2, :]

        def q_base(g):
            return att_feat[:, 1 + g % GROUPS_AT_ONCE, :]

        def k_base(g):
            return att_feat[:, 1 + GROUPS_AT_ONCE + g % GROUPS_AT_ONCE, :]

        def flush_of(u):
            return units[u][1] == 3

        with nc.Block() as block:
            @block.sync
            def _(sp):
                for g in range(4):
                    if g >= GROUPS_AT_ONCE:
                        sp.wait_ge(*built.at(3 * B * (g - GROUPS_AT_ONCE + 1)))
                        sp.wait_ge(*first_built.at(2 * B * (g - GROUPS_AT_ONCE + 1)))
                    for base, names in ((q_base(g), ("q_hi", "q_lo", "q_hi")), (k_base(g), ("k_hi", "k_hi", "k_lo"))):
                        for blk, name in enumerate(names):
                            sp.dma_start(base[32 * blk:32 * blk + 32, :],
                                         parts[name][32 * g:32 * g + 32, :].bitcast(F32)
                                         ).then_inc(*base_loaded[g % GROUPS_AT_ONCE].up(16))

            @block.gpsimd
            def _(pool):
                for u, (b, g) in enumerate(units):
                    s, tok = u % 2, slice(b * S, (b + 1) * S)
                    if b == 0:
                        pool.wait_ge(*base_loaded[g % GROUPS_AT_ONCE].at(96 * (g // GROUPS_AT_ONCE + 1)))
                    if u >= 2:
                        pool.wait_ge(*st_done.at((u - 1) * NG))
                    for j in range(1, 4):
                        pool.tensor_scalar(KS[0:96, s, j, :], k_base(g)[0:96, tok], K("stack")[0:96, j:j + 1],
                                           None, ALU.mult).then_inc(*built.up())

            @block.tensor
            def _(pe):
                def max_step(u, i):
                    j, q = divmod(i, QT)
                    n = u * NJ * QT + i
                    if q == 0:
                        if j == 0:
                            pe.wait_ge(*first_built.at(2 * u + 2))
                        else:
                            pe.wait_ge(*built.at(3 * u + j))
                    if n >= NX:
                        pe.wait_ge(*mx_used.at(n - NX + 1))
                    keys = (q + 1) * P if causal else S
                    kr = slice(0, 96)
                    ins = pe.matmul(bank[:, MX_BANKS[n % NX], 0:keys], query_op(u, j)[kr, q * P:(q + 1) * P],
                                    key_op(u, j)[kr, 0:keys], start=True, stop=True)
                    if causal:
                        ins = pe.matmul(bank[:, MX_BANKS[n % NX], q * P:(q + 1) * P], identb[:, :], causal_s[:, :], start=False,
                                        stop=True, skip_group_check=True)
                    ins.then_inc(*mx_done.up())

                def misc_free(pe, units_done):
                    if units_done > 0:
                        pe.wait_ge(*on_done.at(units_done))
                    nf = sum(flush_of(v) for v in range(units_done))
                    if nf:
                        pe.wait_ge(*fl_used.at(nf))

                def turn_maxima(u):
                    pe.wait_ge(*mp_done.at(u + 1))
                    misc_free(pe, u - 1)
                    for q in range(QT):
                        ins = pe.transpose(bank[0:8, MISC, q * P:(q + 1) * P], max_parts[:, q, :].bitcast(F32), ident)
                    ins.then_inc(*mt_done.up())

                def scores(u, n):
                    kt, j = divmod(n, NJ)
                    m = u * NG + n
                    if n == 0:
                        pe.wait_ge(*m_ready.at(u + 1))
                    if m >= NS:
                        pe.wait_ge(*exp_done.at(m - NS + 1))
                    lo = kt * P if causal else 0
                    st = bank[:, ST_BANKS[m % NS], :]
                    ins = pe.matmul(st[:, lo:S], key_op(u, j)[:, kt * P:(kt + 1) * P], query_op(u, j)[:, lo:S],
                                    start=True, stop=True)
                    if causal:
                        ins = pe.matmul(st[:, lo:lo + P], identb[:, :], causal_st[:, :], start=False, stop=True,
                                        skip_group_check=True)
                    ins.then_inc(*st_done.up())

                def values(u, kt):
                    b, g = units[u]
                    pe.wait_ge(*exp_done.at(u * NG + (kt + 1) * NJ))
                    if kt == 0 and u >= 1:
                        pe.wait_ge(*o_ready.at(u))
                    lo = kt * P if causal else 0
                    for j in range(NJ):
                        p = probs[:, kt % 2, j, lo:S]
                        ins = pe.matmul(bank[32 * j:32 * j + 32, PVB, lo:S], v_aug[:, b * QT + kt, 4 * g + j, :], p,
                                        start=(kt == 0), stop=(kt == QT - 1))
                    ins.then_inc(*pv_done.up())

                def turn_result(u):
                    pe.wait_ge(*o_ready.at(u + 1))
                    if u + 1 < NU:
                        pe.wait_ge(*m_ready.at(u + 2))
                    misc_free(pe, u)
                    for q in range(QT):
                        ins = pe.transpose(bank[:, MISC, q * P:(q + 1) * P], o_feat[:, q * P:(q + 1) * P], ident)
                    ins.then_inc(*ot_done.up())

                def flush(u):
                    b = units[u][0]
                    pe.wait_ge(*on_done.at(u + 1))
                    for q in range(QT):
                        ins = pe.transpose(bank[:, MISC, q * P:(q + 1) * P], o_tok[:, b, q, :], ident)
                    ins.then_inc(*fl_done.up())

                for i in range(NG):
                    max_step(0, i)
                turn_maxima(0)
                for u in range(NU):
                    for n in range(NG):
                        scores(u, n)
                        if u + 1 < NU:
                            for i in maxima_of(n):
                                max_step(u + 1, i)
                        if n % NJ == 1 and u * QT + n // NJ >= 1:
                            values(*divmod(u * QT + n // NJ - 1, QT))
                        if n == RESULT and u >= 1:
                            turn_result(u - 1)
                        if n == FLUSH and u >= 1 and flush_of(u - 1):
                            flush(u - 1)
                        if n == TURN and u + 1 < NU:
                            turn_maxima(u + 1)
                values(NU - 1, QT - 1)
                turn_result(NU - 1)
                flush(NU - 1)

            @block.vector
            def _(dve):
                step = steps(dve, step_sig)

                def reduce_step(u, i):
                    j, q = divmod(i, QT)
                    n = u * NJ * QT + i
                    keys = (q + 1) * P if causal else S
                    dve.wait_ge(*mx_done.at(n + 1))
                    o = neg_max[:, q, j:j + 1]
                    ins = dve.tensor_reduce(o, bank[:, MX_BANKS[n % NX], 0:keys], X_AXIS, ALU.max, negate=True)
                    ins.then_inc(*mx_used.up())
                    return ins

                def split_maxima(u):
                    dve.wait_ge(*mx_used.at((u + 1) * NJ * QT))
                    if u >= 1:
                        dve.wait_ge(*mt_done.at(u))
                    step(dve.tensor_copy(max_parts[:, :, 0:4], neg_max[:, :, :]))
                    dve.tensor_tensor(max_parts[:, :, 4:8], neg_max[:, :, :], max_parts[:, :, 0:4].bitcast(F32),
                                      ALU.subtract).then_inc(*mp_done.up())

                def normalise(u):
                    b, g = units[u]
                    dve.wait_ge(*ot_done.at(u + 1))
                    ot = bank[:, MISC, :].rearrange("p (q j d) -> p q j d", q=QT, j=4)
                    o, r = ot[:, :, :, 0:DH], ot[:, :, :, DH]
                    dest = o_tok[:, b, :, 32 * g:32 * g + 32].rearrange("p q (j d) -> p q j d", j=4)
                    rs = rsum[:, :, 0:NJ]
                    if guard:
                        step(dve.tensor_scalar(rs, r, 1e-12, None, ALU.max))
                        step(dve.reciprocal(rs, rs))
                    else:
                        step(dve.reciprocal(rs, r))
                    dve.tensor_tensor(dest, o, rs.unsqueeze(3).broadcast_to([P, QT, NJ, DH]), ALU.mult
                                      ).then_inc(*on_done.up())

                for i in range(NG):
                    reduce_step(0, i)
                split_maxima(0)
                for u in range(NU):
                    for n in range(NG):
                        if u + 1 < NU:
                            for i in maxima_of(n):
                                reduce_step(u + 1, i)
                        if n == RESULT and u >= 1:
                            normalise(u - 1)
                        if n == TURN - 1 and u + 1 < NU:
                            split_maxima(u + 1)
                normalise(NU - 1)

            @block.scalar
            def _(act):
                def maxima_rows(u):
                    act.wait_ge(*mt_done.at(u + 1))
                    act.copy(QM[96:104, u % 2, :], bank[0:8, MISC, :]).then_inc(*m_ready.up())

                def build_first(u):
                    b, g = units[u]
                    s, tok = u % 2, slice(b * S, (b + 1) * S)
                    act.wait_ge(*base_loaded[g % GROUPS_AT_ONCE].at(96 * (g // GROUPS_AT_ONCE + 1)))
                    if u >= 2:
                        act.wait_ge(*st_done.at((u - 1) * NG))
                    act.copy(QM[0:96, s, :], q_base(g)[0:96, tok]).then_inc(*first_built.up())
                    act.activation(KS[0:96, s, 0, :], k_base(g)[0:96, tok], ACT.Copy, scale=K("stack")[0:96, 0:1]
                                   ).then_inc(*first_built.up())

                def exponentials(u, n):
                    kt, j = divmod(n, NJ)
                    m = u * NG + n
                    act.wait_ge(*st_done.at(m + 1))
                    if j == 0 and u * QT + kt >= 2:
                        act.wait_ge(*pv_done.at(u * QT + kt - 1))
                    lo = kt * P if causal else 0
                    act.activation(probs[:, kt % 2, j, lo:S], bank[:, ST_BANKS[m % NS], lo:S], ACT.Exp, scale=scale).then_inc(*exp_done.up())

                def copy_result(u):
                    act.wait_ge(*pv_done.at((u + 1) * QT))
                    if u >= 1:
                        act.wait_ge(*ot_done.at(u))
                    act.copy(o_feat[:, :], bank[:, PVB, :]).then_inc(*o_ready.up())

                def flush_copy(u, k):
                    b = units[u][0]
                    act.wait_ge(*fl_done.at(k))
                    act.copy(att_feat[:, 0, b * S:(b + 1) * S], bank[:, MISC, :]).then_inc(*fl_used.up())

                k = 0
                build_first(0)
                maxima_rows(0)
                for u in range(NU):
                    if u + 1 < NU:
                        build_first(u + 1)
                    for n in range(NG):
                        exponentials(u, n)
                        if n == COPY and u >= 1:
                            copy_result(u - 1)
                        if n == FLUSH and u >= 1 and flush_of(u - 1):
                            k += 1
                            flush_copy(u - 1, k)
                        if n == TURN and u + 1 < NU:
                            maxima_rows(u + 1)
                copy_result(NU - 1)
                flush_copy(NU - 1, k + 1)
        signals.settle()

    def cross_stage(wname, bq, bk, bv, mask_src, mask_bool, heads, scale, fill, mask_tiles):
        wq, wk, wv = (W(wname, 128 * i, 128 * i + 128) for i in range(3))
        dh = P // heads
        halves = 2 if heads > 1 else 1
        G = heads // halves
        HB = min(G, 4)
        NB = G // HB
        N = NT * halves
        KP = 96
        (m_ld, kq, kq_used, kbd_done, q_ready, s_done, s_used, sh_done, filled, e_done, et_done, et_used, o_done,
         o_used, ot_done, ot_used, nb_done, v_ok, cleared) = (signals(n) for n in (
             "m_ld", "kq", "kq_used", "kbd_done", "q_ready", "s_done", "s_used", "sh_done", "filled", "e_done",
             "et_done", "et_used", "o_done", "o_used", "ot_done", "ot_used", "nb_done", "v_ok", "cleared"))
        step_sig = signals("dve_step")
        at = [T]

        def take(n):
            at[0] += n
            return flat[:, at[0] - n:at[0]]

        kbd = take(B * heads * SC).rearrange("p (b h k) -> p b h k", b=B, k=SC)
        v_ctx = take(B * heads * (dh + 1)).rearrange("p (b h d) -> p b h d", b=B, h=heads)
        k_ctx = take(B * SC)
        neg = take(NT * SC).rearrange("p (t k) -> p t k", k=SC)
        masks = take(NT * SC).rearrange("p (t k) -> p t k", k=SC)
        sc_flat = take(4 * max(G, 2) * SC)
        raw_mask = sc_flat[:, 0:NT * SC].rearrange("p (t k) -> p t k", k=SC)
        sc = sc_flat[:, 0:4 * G * SC].rearrange("p (s h k) -> p s h k", s=4, k=SC)
        et = probs[0:KP, :, :, :].rearrange("p a b c -> p (a b c)").rearrange("p (s h q) -> p s h q", s=4, q=P)

        def batch(i):
            return i // halves // QT

        def head(i, g):
            return (i % halves) * G + g

        def last_of_tile(i):
            return i >= 0 and i % halves == halves - 1

        def o_bank(t):
            return bank[:, 6 + t % 2, 0:heads * (dh + 1)].rearrange("p (h d) -> p h d", h=heads)

        def mask_of(table, i):
            return table[:, mask_tiles(i // halves), :]

        with nc.Block() as block:
            @block.sync
            def _(sp):
                n, dst = mask_src(raw_mask)
                sp.dma_start(dst, n).then_inc(*m_ld.up(16))

            @block.tensor
            def _(pe):
                pe.matmul(bank[:, 4, 0:B * SC], wk, ctx_feat[:, :], start=True, stop=True).then_inc(*kq.up())
                for b in range(B):
                    ins = pe.matmul(bank[0:SC, 5, b * P:(b + 1) * P], ctx_feat[:, b * SC:(b + 1) * SC], wv, start=True,
                                    stop=True)
                ins.then_inc(*kq.up())
                for hf in range(2):
                    pe.matmul(bank[:, 6 + hf, :], wq, x_feat[:, hf * HF:(hf + 1) * HF], start=True, stop=True
                              ).then_inc(*kq.up())
                pe.wait_ge(*q_ready.at(2))
                pe.wait_ge(*kbd_done.at(1))
                pe.wait_ge(*v_ok.at(1))

                def scores(i):
                    if i >= 2:
                        pe.wait_ge(*s_used.at(i - 1))
                    t = i // halves
                    for n in range(NB):
                        h = head(i, n * HB)
                        ins = pe.matmul(bank[:, 2 * (i % 2) + n, 0:HB * SC], q_feat[:, t * P:(t + 1) * P],
                                        kbd[:, batch(i), h:h + HB, :], start=True, stop=True)
                    ins.then_inc(*s_done.up())

                def turn(i):
                    pe.wait_ge(*e_done.at(i + 1))
                    for n in range(NB):
                        m = i * NB + n
                        if m >= 2:
                            pe.wait_ge(*et_used.at(m - 1))
                        for h in range(HB):
                            ins = pe.transpose(bank[0:SC, 4 + m % 2, h * P:(h + 1) * P], sc[:, i % 4, n * HB + h, :],
                                               ident)
                        ins.then_inc(*et_done.up())

                def values(i):
                    t = i // halves
                    pe.wait_ge(*et_used.at((i + 1) * NB))
                    if i % halves == 0:
                        if t >= 2:
                            pe.wait_ge(*o_used.at(t - 1))
                        if t == QT + 1:
                            pe.wait_ge(*ot_used.at(1))
                    for g in range(G):
                        h = head(i, g)
                        ins = pe.matmul(o_bank(t)[:, h, :], et[:, i % 4, g, :], v_ctx[0:KP, batch(i), h, :], start=True,
                                        stop=True)
                    ins.then_inc(*o_done.up())

                def turn_result(b):
                    pe.wait_ge(*o_used.at(QT * (b + 1)))
                    for q in range(QT):
                        ins = pe.transpose(bank[:, 7, q * P:(q + 1) * P], o_tok[:, b, q, :], ident)
                    ins.then_inc(*ot_done.up())

                for k in range(N + 5):
                    if k < N:
                        scores(k)
                    if 0 <= k - 2 < N:
                        turn(k - 2)
                    if k - 4 in (N // 2 - 1, N - 1):
                        turn_result(batch(k - 4))
                    if 0 <= k - 3 < N:
                        values(k - 3)

            @block.scalar
            def _(act):
                act.wait_ge(*kq.at(1))
                if bk is not None:
                    act.activation(k_ctx, bank[:, 4, 0:B * SC], ACT.Identity, bias=bk).then_inc(*kq_used.up())
                else:
                    act.copy(k_ctx, bank[:, 4, 0:B * SC]).then_inc(*kq_used.up())
                for hf in range(2):
                    act.wait_ge(*kq.at(3 + hf))
                    o = q_feat[:, hf * HF:(hf + 1) * HF]
                    if bq is not None:
                        act.activation(o, bank[:, 6 + hf, :], ACT.Identity, bias=bq).then_inc(*q_ready.up())
                    else:
                        act.copy(o, bank[:, 6 + hf, :]).then_inc(*q_ready.up())
                act.wait_ge(*cleared.at(1))
                for k in range(N + 5):
                    if 0 <= k - 1 < N:
                        i = k - 1
                        act.wait_ge(*sh_done.at(i + 1))
                        act.activation(sc[:, i % 4, :, :], sc[:, i % 4, :, :], ACT.Exp, scale=scale
                                       ).then_inc(*e_done.up())
                    if 0 <= k - 2 < N:
                        i = k - 2
                        if i >= 4:
                            act.wait_ge(*o_done.at(i - 3))
                        for n in range(NB):
                            m = i * NB + n
                            act.wait_ge(*et_done.at(m + 1))
                            act.copy(et[0:SC, i % 4, n * HB:(n + 1) * HB, :],
                                     bank[0:SC, 4 + m % 2, 0:HB * P].rearrange("p (h q) -> p h q", q=P)
                                     ).then_inc(*et_used.up())
                    if k - 4 in (N // 2 - 1, N - 1):
                        b = batch(k - 4)
                        act.wait_ge(*ot_done.at(b + 1))
                        act.copy(att_feat[:, 0, b * S:(b + 1) * S], bank[:, 7, :]).then_inc(*ot_used.up())

            @block.vector
            def _(dve):
                step = steps(dve, step_sig)
                dve.wait_ge(*kq.at(2))
                dve.wait_ge(*cleared.at(1))
                v_in = bank[0:SC, 5, 0:B * P].rearrange("p (b h d) -> p b h d", b=B, h=heads)
                for b in range(B):
                    o = v_ctx[0:SC, b, :, 0:dh]
                    if bv is not None:
                        dve.tensor_tensor(o, v_in[:, b, :, :], bv[0:SC, :].rearrange("p (h d) -> p h d", h=heads), ALU.add)
                    else:
                        dve.tensor_copy(o, v_in[:, b, :, :])
                dve.memset(v_ctx[0:SC, :, :, dh:dh + 1], 1.0).then_inc(*v_ok.up())
                dve.wait_ge(*kq_used.at(1))
                for b in range(B):
                    kb = k_ctx[:, b * SC:(b + 1) * SC]
                    if heads == 1:
                        ins = dve.tensor_copy(kbd[:, b, 0, :], kb)
                    else:
                        ins = dve.tensor_tensor(kbd[:, b, :, :], kb.unsqueeze(1).broadcast_to([P, heads, SC]),
                                                K("headmask").unsqueeze(2).broadcast_to([P, heads, SC]), ALU.mult)
                ins.then_inc(*kbd_done.up())
                dve.wait_ge(*m_ld.at(16))
                _, dst = mask_src(raw_mask)
                n_m = masks[:, 0:mask_count(mask_bool), :]
                step(dve.tensor_scalar(n_m, dst, 0.0, None, ALU.not_equal))
                step(dve.tensor_scalar(neg[:, 0:mask_count(mask_bool), :], n_m, 1.0, fill, ALU.subtract, ALU.mult))
                dve.sem_inc(*nb_done.up())

                def keep_unmasked(i):
                    dve.wait_ge(*s_done.at(i + 1))
                    if i >= 4:
                        dve.wait_ge(*et_done.at((i - 3) * NB))
                    src = bank[:, 2 * (i % 2):2 * (i % 2) + NB, 0:HB * SC].rearrange("p n (h k) -> p n h k", k=SC)
                    mm = mask_of(masks, i).unsqueeze(1).unsqueeze(1).broadcast_to([P, NB, HB, SC])
                    dve.tensor_tensor(sc[:, i % 4, :, :].rearrange("p (n h) k -> p n h k", h=HB), src, mm, ALU.mult
                                      ).then_inc(*s_used.up())

                def less_maxima(i):
                    x, mx = sc[:, i % 4, :, :], picked[:, i % 4, 0:G]
                    dve.wait_ge(*filled.at(i + 1))
                    step(dve.tensor_reduce(mx, x, X_AXIS, ALU.max))
                    dve.tensor_tensor(x, x, mx.unsqueeze(2).broadcast_to([P, G, SC]), ALU.subtract
                                      ).then_inc(*sh_done.up())

                def normalise(i):
                    t = i // halves
                    rs = picked[:, 4 + t % 2, 0:heads]
                    dve.wait_ge(*o_done.at(i + 1))
                    step(dve.reciprocal(rs, o_bank(t)[:, :, dh]))
                    dve.tensor_tensor(o_tok[:, t // QT, t % QT, :].rearrange("p (h d) -> p h d", h=heads),
                                      o_bank(t)[:, :, 0:dh], rs.unsqueeze(2).broadcast_to([P, heads, dh]), ALU.mult
                                      ).then_inc(*o_used.up())

                for k in range(N + 5):
                    if k < N:
                        keep_unmasked(k)
                    if 0 <= k - 1 < N:
                        less_maxima(k - 1)
                    if last_of_tile(k - 3) and k - 3 < N:
                        normalise(k - 3)

            @block.gpsimd
            def _(pool):
                step = steps(pool, signals("pool_step"))
                step(pool.memset(v_ctx[64:KP, :, :, :], 0.0))
                step(pool.memset(et[64:KP, :, :, :], 0.0))
                pool.sem_inc(*cleared.up())
                pool.wait_ge(*nb_done.at(1))
                for i in range(N):
                    pool.wait_ge(*s_used.at(i + 1))
                    pool.tensor_tensor(sc[:, i % 4, :, :], sc[:, i % 4, :, :],
                                       mask_of(neg, i).unsqueeze(1).broadcast_to([P, G, SC]), ALU.add
                                       ).then_inc(*filled.up())
        signals.settle()

    def mask_count(kind):
        return {"q": QT, "bq": NT, "b": B}[kind]

    def route_stage(terms, bias, experts, top_k, renormalise, distance=False, first_expert=None):
        E, EP = experts, max(experts, 8)
        ns = 8 - top_k
        (l_done, s_ready, x_done, g_done, gt_done, hi_ok, sq_done, kk_done, kk_ok) = (signals(n) for n in (
            "l_done", "s_ready", "x_done", "g_done", "gt_done", "hi_ok", "sq_done", "kk_done", "kk_ok"))
        step_sig = signals("dve_step")
        with nc.Block() as block:
            if first_expert is not None:
                @block.sync
                def _(sp):
                    for n in range(first_expert, first_expert + NW):
                        load_expert(sp, n)

                @block.gpsimd
                def _(pool):
                    split_expert(pool, first_expert)

            @block.tensor
            def _(pe):
                weights_here(pe)
                if distance:
                    pe.wait_ge(*kk_done.at(1))
                    pe.matmul(bank[:, 2, 0:16], ones128, kk_sq, start=True, stop=True).then_inc(*kk_ok.up())
                for t in range(NT):
                    for n, (operand, w) in enumerate(terms):
                        ins = pe.matmul(bank[:, 0, t * 16:t * 16 + E], operand[:, t * P:(t + 1) * P], w,
                                        start=(n == 0), stop=(n == len(terms) - 1))
                ins.then_inc(*l_done.up())
                pe.wait_ge(*g_done.at(1))
                for t in range(NT):
                    ins = pe.transpose(bank[0:16, 4 + t // QT, (t % QT) * P:(t % QT + 1) * P], gates[:, t, :], ident)
                ins.then_inc(*gt_done.up())

            @block.vector
            def _(dve):
                step = steps(dve, step_sig)
                if distance:
                    dve.wait_ge(loads["ld_w"], 16)
                    dve.tensor_tensor(kk_sq, W("l0_keys"), W("l0_keys"), ALU.mult).then_inc(*kk_done.up())
                    for t in range(NT):
                        ins = dve.tensor_tensor_reduce(out=sum_tok[:, t, :], in0=x_tok[:, t, :], in1=x_tok[:, t, :],
                                                       scale=1.0, scalar=0.0, op0=ALU.mult, op1=ALU.add,
                                                       accum_out=small[:, t, 0:1])
                    step(ins)
                    dve.wait_ge(*kk_ok.at(1))
                    step(dve.tensor_tensor(kk_row, bias, bank[:, 2, 0:16], ALU.subtract))
                step(dve.memset(gates[:, :, :], 0.0))
                dve.memset(lg[:, :, 0:EP], -HUGE)
                step(dve.memset(lg[:, :, EP:EP + ns], HUGE))
                step(dve.memset(top_in[:, :, :], HUGE))
                dve.wait_ge(*l_done.at(1))
                logit = bank[:, 0, 0:NT * 16].rearrange("p (t e) -> p t e", e=16)[:, :, 0:E]
                brow = (kk_row if distance else bias)
                if bias is not None:
                    step(dve.tensor_tensor(lg[:, :, 0:E], logit, brow.unsqueeze(1).broadcast_to([P, NT, E]), ALU.add))
                else:
                    step(dve.tensor_copy(lg[:, :, 0:E], logit))
                if distance:
                    step(dve.tensor_tensor(lg[:, :, 0:E], lg[:, :, 0:E], small[:, :, 0:1].broadcast_to([P, NT, E]),
                                           ALU.subtract))
                for t in range(NT):
                    ins = dve.max(top8[:, t, :], lg[:, t, 0:EP])
                step(ins)
                step(dve.tensor_copy(top_in[:, :, 0:top_k], top8[:, :, 0:top_k]))
                for t in range(NT):
                    ins = dve.match_replace(lg_rep[:, t, 0:EP + ns], top_in[:, t, :], lg[:, t, 0:EP + ns], -HUGE)
                step(ins)
                step(dve.tensor_tensor(picked[:, :, 0:E], lg_rep[:, :, 0:E], lg[:, :, 0:E], ALU.not_equal))
                dve.tensor_tensor(lg[:, :, 0:E], lg[:, :, 0:E], top8[:, :, 0:1].broadcast_to([P, NT, E]),
                                  ALU.subtract).then_inc(*s_ready.up())
                dve.wait_ge(*x_done.at(1))
                step(dve.tensor_tensor(picked[:, :, 0:E], picked[:, :, 0:E], lg[:, :, 0:E], ALU.mult))
                step(dve.tensor_reduce(small[:, :, 1], (picked if renormalise else lg)[:, :, 0:E], X_AXIS, ALU.add))
                step(dve.reciprocal(small[:, :, 1], small[:, :, 1]))
                step(dve.tensor_tensor(gates[:, :, 0:E], picked[:, :, 0:E],
                                       small[:, :, 1:2].broadcast_to([P, NT, E]), ALU.mult))
                dve.tensor_reduce(gate_sum[:, :], gates[:, :, 0:E], X_AXIS, ALU.add).then_inc(*g_done.up())
                dve.wait_ge(*hi_ok.at(1))
                dve.tensor_tensor(gate_parts[32:48, :], gate_rows, gate_parts[0:16, :].bitcast(F32),
                                  ALU.subtract)

            @block.scalar
            def _(act):
                act.wait_ge(*s_ready.at(1))
                act.activation(lg[:, :, 0:E], lg[:, :, 0:E], ACT.Exp).then_inc(*x_done.up())
                preload(act, ACT.Gelu if renormalise else ACT.Silu)
                act.wait_ge(*gt_done.at(1))
                rows16 = bank[0:16, 4:6, :].rearrange("p a n -> p (a n)")
                act.copy(gate_rows, rows16)
                act.copy(gate_parts[0:16, :], rows16).then_inc(*hi_ok.up())
        signals.settle()

    kk_sq = sb("kk_sq", [P, 16])[:, :]
    kk_row = sb("kk_row", [P, 16])[:, :]
    route_w = sb("route_w", [P, 16])
    ones128 = sb("ones128", [P, P])[:, :]

    GROUP = 16
    loaded, split_up, split_down, bias_in, bias_ready, dn_done = (signals(n) for n in (
        "loaded", "split_up", "split_down", "bias_in", "bias_ready", "dn_done"))
    expert_loaded = [nc.alloc_semaphore(f"expert_loaded{i}") for i in range(NW)]

    def affine_of(n):
        return (C("l2_g", n - GROUP), C("l2_b", n - GROUP)) if n >= GROUP else None

    def arrived(eng, n):
        eng.wait_ge(expert_loaded[n % NW], 16 * (n // NW + 1))

    def load_expert(sp, n):
        src = l0_experts[n, :, :] if n < GROUP else l2_experts[n - GROUP, :, :]
        sp.dma_start(wring[:, n % NW, :], src).then_inc(expert_loaded[n % NW], 16)

    def weight_part(n, i):
        return KS[:, n % 2, i, :]

    def split_expert(pool, n):
        step = steps(pool, signals("pool_step"))
        arrived(pool, n)
        if n >= 2:
            pool.wait_ge(*dn_done.absolute(8 * (n - 1)))
        w1, w2 = wring[:, n % NW, 0:HF], wring[:, n % NW, HF:2 * HF]
        if affine_of(n):
            step(pool.tensor_scalar(weight_part(n, 0), w1, affine_of(n)[0], None, ALU.mult))
            step(pool.tensor_scalar(scaled, w1, affine_of(n)[0], None, ALU.mult))
            w1 = scaled
        else:
            step(pool.tensor_copy(weight_part(n, 0), w1))
        pool.tensor_tensor(weight_part(n, 1), w1, weight_part(n, 0).bitcast(F32), ALU.subtract
                           ).then_inc(*split_up.up())
        step(pool.tensor_copy(weight_part(n, 2), w2))
        pool.tensor_tensor(weight_part(n, 3), w2, weight_part(n, 2).bitcast(F32), ALU.subtract
                           ).then_inc(*split_down.up())

    def shifted_input(pe, n):
        arrived(pe, n)
        m = n - GROUP
        if m >= 1:
            pe.wait_ge(*bias_ready.absolute(m))
        for f in range(4):
            ins = pe.matmul(bank[:, 3, 4 * (n % 2) + f:4 * (n % 2) + f + 1], wring[:, n % NW, f * P:(f + 1) * P],
                            affine_of(n)[1], start=True, stop=True)
        ins.then_inc(*bias_in.up())

    def shifted_bias(dve, n):
        m = n - GROUP
        dve.wait_ge(*bias_in.absolute(m + 1))
        at = C_AT["l2_b1"][0] + 4 * m
        dve.tensor_tensor(bias_buf[:, n % 2, :], bank[:, 3, 4 * (n % 2):4 * (n % 2) + 4], cols[:, at:at + 4], ALU.add
                          ).then_inc(*bias_ready.up())

    def expert_stage(source, first, experts, b2):
        NFT = 4
        seq = [(first + e, hf, f) for e in range(experts) for hf in range(2) for f in range(NFT)]
        N = len(seq)
        LAG = 3
        (up_done, gelu_done, gate_ok, gate_used, h_ready, hi_ok, lo_ok, xh_ok, x_ok, y_ok) = (signals(n) for n in (
            "up_done", "gelu_done", "gate_ok", "gate_used", "h_ready", "hi_ok", "lo_ok", "xh_ok", "x_ok", "y_ok"))
        g_buf = scratch[:, 0:3 * HF].rearrange("p (s n) -> p s n", n=HF)
        h_buf = scratch[:, 3 * HF:6 * HF].rearrange("p (s n) -> p s n", n=HF)
        h_part = operands[:, :, :].rearrange("p a t -> p (a t)").rearrange("p (s x n) -> p s x n", s=4, x=2)
        group_end = (first // GROUP + 1) * GROUP
        ahead = [n for n in range(first + 1, first + experts + 1) if n < group_end]
        dn_base = dn_done.total

        def halves(tile, hf):
            return tile[:, hf * HF:(hf + 1) * HF]

        with nc.Block() as block:
            @block.sync
            def _(sp):
                for n in range(first, first + experts):
                    if n + NW < group_end:
                        sp.wait_ge(*split_down.absolute(n + 1))
                        if n >= GROUP:
                            sp.wait_ge(*bias_in.absolute(n - GROUP + 1))
                        load_expert(sp, n + NW)

            @block.gpsimd
            def _(pool):
                for n in ahead:
                    split_expert(pool, n)

            @block.tensor
            def _(pe):
                if first == GROUP:
                    shifted_input(pe, first)
                for i in range(N + LAG):
                    if i < N:
                        n, hf, f = seq[i]
                        k = i // NFT
                        if hf == 0 and f == 0:
                            pe.wait_ge(*split_up.absolute(n + 1))
                        if f == 0:
                            if k >= 2:
                                pe.wait_ge(*gate_used.at(k - 1))
                            if k < 2:
                                pe.wait_ge(*x_ok.at(k + 1))
                            pe.matmul(bank[:, 4 + k % 2, :], sel[0:96, n - first, :], halves(gate_parts[0:96, :], hf),
                                      start=True, stop=True).then_inc(*gate_ok.up())
                        if i >= 3:
                            pe.wait_ge(*gelu_done.at(i - 2))
                        fs = slice(f * P, (f + 1) * P)
                        for w, x, at in ((0, x_hi, 0), (0, x_lo, 1), (1, x_hi, 2)):
                            ins = pe.matmul(bank[:, i % 3, :], weight_part(n, w)[:, fs], halves(x, hf),
                                            start=(at == 0), stop=(at == 2))
                        ins.then_inc(*up_done.up())
                        if hf == 1 and f == 0 and n + 1 in ahead and affine_of(n):
                            shifted_input(pe, n + 1)
                    if i >= LAG:
                        m = i - LAG
                        n, hf, f = seq[m]
                        if hf == 0 and f == 0:
                            pe.wait_ge(*split_down.absolute(n + 1))
                        pe.wait_ge(*lo_ok.at(m + 1))
                        fs = slice(f * P, (f + 1) * P)
                        for w, x, at in ((2, 0, 0), (2, 1, 1), (3, 0, 2)):
                            ins = pe.matmul(bank[:, 6 + hf, :], weight_part(n, w)[:, fs],
                                            h_part[:, m % 4, x, :].bitcast(F32R),
                                            start=(n == first and f == 0 and at == 0), stop=False,
                                            skip_group_check=True)
                        ins.then_inc(*dn_done.up())
                for hf in range(2):
                    pe.matmul(bank[:, 6 + hf, :], b2, halves(gate_rows, hf), start=False, stop=True,
                              skip_group_check=True).then_inc(*y_ok.up())

            @block.scalar
            def _(act):
                for hf in range(2):
                    act.copy(halves(x_hi, hf), halves(source, hf)).then_inc(*xh_ok.up())

                def high(i):
                    act.wait_ge(*h_ready.at(i + 1))
                    if i >= 4:
                        act.wait_ge(*dn_done.absolute(dn_base + i - 3))
                    act.copy(h_part[:, i % 4, 0, :].bitcast(F32R), h_buf[:, i % 3, :]).then_inc(*hi_ok.up())

                for i, (n, hf, f) in enumerate(seq):
                    if affine_of(n):
                        if hf == 0 and f == 0:
                            act.wait_ge(*bias_ready.absolute(n - GROUP + 1))
                        bias = bias_buf[:, n % 2, f:f + 1]
                    else:
                        bias = C("l0_b1", 4 * n + f)
                    act.wait_ge(*up_done.at(i + 1))
                    if i >= 3:
                        act.wait_ge(*h_ready.at(i - 2))
                    act.activation(g_buf[:, i % 3, :], bank[:, i % 3, :], ACT.Gelu, bias=bias
                                   ).then_inc(*gelu_done.up())
                    if i >= 1:
                        high(i - 1)
                high(N - 1)
                for hf in range(2):
                    act.wait_ge(*y_ok.at(hf + 1))
                    act.copy(halves(y_feat, hf), bank[:, 6 + hf, :])

            @block.vector
            def _(dve):
                for hf in range(2):
                    dve.wait_ge(*xh_ok.at(hf + 1))
                    dve.tensor_tensor(halves(x_lo, hf), halves(source, hf), halves(x_hi, hf).bitcast(F32),
                                      ALU.subtract).then_inc(*x_ok.up())
                if first == GROUP:
                    shifted_bias(dve, first)

                def low(i):
                    dve.wait_ge(*hi_ok.at(i + 1))
                    dve.tensor_tensor(h_part[:, i % 4, 1, :].bitcast(F32R), h_buf[:, i % 3, :], h_part[:, i % 4, 0, :],
                                      ALU.subtract).then_inc(*lo_ok.up())

                for i, (n, hf, f) in enumerate(seq):
                    k = i // NFT
                    dve.wait_ge(*gelu_done.at(i + 1))
                    if f == 0:
                        dve.wait_ge(*gate_ok.at(k + 1))
                    if i >= 3:
                        dve.wait_ge(*lo_ok.at(i - 2))
                    ins = dve.tensor_tensor(h_buf[:, i % 3, :], g_buf[:, i % 3, :], bank[:, 4 + k % 2, :], ALU.mult)
                    ins.then_inc(*h_ready.up())
                    if i >= 1:
                        low(i - 1)
                    if f == NFT - 1:
                        dve.wait_ge(*h_ready.at(i + 1))
                        dve.sem_inc(*gate_used.up())
                    if hf == 1 and f == 1 and n + 1 in ahead and affine_of(n):
                        shifted_bias(dve, n + 1)
                low(N - 1)
        signals.settle()

    def gated_stage():
        seq = [(p_, hf) for p_ in range(9) for hf in range(2)]
        (up_done, gelu_done, gate_ok, h_ready, dn_done, y_ok, t_ok) = (signals(n) for n in (
            "up_done", "gelu_done", "gate_ok", "h_ready", "dn_done", "y_ok", "t_ok"))
        g_buf = scratch[:, 0:3 * HF].rearrange("p (s n) -> p s n", n=HF)
        h_buf = scratch[:, 3 * HF:5 * HF].rearrange("p (s n) -> p s n", n=HF)
        t_buf = scratch[:, 5 * HF:7 * HF].rearrange("p (s n) -> p s n", n=HF)
        with nc.Block() as block:
            @block.tensor
            def _(pe):
                for i in range(len(seq) + 1):
                    if i < len(seq):
                        p_, hf = seq[i]
                        x = x_feat[:, hf * HF:(hf + 1) * HF]
                        if i >= 2:
                            pe.wait_ge(*h_ready.at(i - 1))
                        s = i % 2
                        if p_ < 8:
                            wu, wg = (W("l3_w1", p_ * 256 + a * 128, p_ * 256 + a * 128 + 128) for a in range(2))
                        else:
                            wu, wg = W("l3_ws1", 0, 128), W("l3_ws1", 128, 256)
                        pe.matmul(bank[:, 2 * s, :], wu, x, start=True, stop=True)
                        ins = pe.matmul(bank[:, 2 * s + 1, :], wg, x, start=True, stop=True)
                        ins.then_inc(*up_done.up())
                        if p_ < 8:
                            pe.matmul(bank[:, 4 + s, :], sel[0:96, p_, :],
                                      gate_parts[0:96, hf * HF:(hf + 1) * HF], start=True, stop=True
                                      ).then_inc(*gate_ok.up())
                    if i >= 1:
                        p_, hf = seq[i - 1]
                        pe.wait_ge(*h_ready.at(i))
                        w2 = W("l3_w2", p_ * 128, p_ * 128 + 128) if p_ < 8 else W("l3_ws2")
                        ins = pe.matmul(bank[:, 6 + hf, :], w2, h_buf[:, (i - 1) % 2, :], start=(p_ == 0),
                                        stop=(p_ == 8), skip_group_check=True)
                        ins.then_inc(*dn_done.up())

            @block.scalar
            def _(act):
                for i, (p_, hf) in enumerate(seq):
                    act.wait_ge(*up_done.at(i + 1))
                    if i >= 2:
                        act.wait_ge(*h_ready.at(i - 1))
                    act.activation(g_buf[:, i % 2, :], bank[:, 2 * (i % 2) + 1, :], ACT.Silu
                                   ).then_inc(*gelu_done.up())
                for hf in range(2):
                    act.wait_ge(*dn_done.at(17 + hf))
                    act.copy(y_feat[:, hf * HF:(hf + 1) * HF], bank[:, 6 + hf, :])

            @block.vector
            def _(dve):
                for i, (p_, hf) in enumerate(seq):
                    dve.wait_ge(*gelu_done.at(i + 1))
                    if i >= 2:
                        dve.wait_ge(*dn_done.at(i - 1))
                    if p_ < 8:
                        dve.tensor_tensor(t_buf[:, i % 2, :], g_buf[:, i % 2, :], bank[:, 2 * (i % 2), :], ALU.mult
                                          ).then_inc(*t_ok.up())
                        dve.wait_ge(*t_ok.at(i + 1))
                        dve.wait_ge(*gate_ok.at(i + 1))
                        dve.tensor_tensor(h_buf[:, i % 2, :], t_buf[:, i % 2, :], bank[:, 4 + i % 2, :], ALU.mult
                                          ).then_inc(*h_ready.up())
                    else:
                        dve.tensor_tensor(h_buf[:, i % 2, :], g_buf[:, i % 2, :], bank[:, 2 * (i % 2), :], ALU.mult
                                          ).then_inc(*h_ready.up())
        signals.settle()

    def memory_stage():
        TC = (SC - 4) // 4 + 1
        conv_ok, moved = signals("conv_ok"), signals("moved")
        with nc.Block() as block:
            @block.tensor
            def _(pe):
                for b in range(B):
                    for r in range(4):
                        lo = b * S + 256 + r
                        ins = pe.matmul(bank[:, 0, b * 32:b * 32 + TC], W("l0_conv", r * P, r * P + P),
                                        x_feat[:, lo:lo + 4 * (TC - 1) + 1:4], start=(r == 0), stop=(r == 3))
                ins.then_inc(*conv_ok.up())

            @block.gpsimd
            def _(pool):
                for b in range(B):
                    o = b * S
                    pool.tensor_copy(y_feat[:, o:o + 256 - TC], x_feat[:, o + TC:o + 256])
                    pool.tensor_copy(y_feat[:, o + 256:o + S - SC], x_feat[:, o + 256 + SC:o + S])
                    pool.tensor_copy(y_feat[:, o + S - SC:o + S], ctx_feat[:, b * SC:(b + 1) * SC])

            @block.scalar
            def _(act):
                act.wait_ge(*conv_ok.at(1))
                for b in range(B):
                    act.activation(y_feat[:, b * S + 256 - TC:b * S + 256], bank[:, 0, b * 32:b * 32 + TC],
                                   ACT.Identity, bias=C("conv_b"))
        signals.settle()

    def ternary_stage():
        w_ld, tq_done, wt_in, wt_done = (signals(n) for n in ("w_ld", "tq_done", "wt_in", "wt_done"))
        v_clear = signals("v_clear")
        step_sig = signals("dve_step")
        MAGIC = 1.5 * 2.0 ** 23
        amax, scl, inv = small[:, :, 0], small[:, :, 1], small[:, :, 2]
        with nc.Block() as block:
            @block.sync
            def _(sp):
                for s in range(4):
                    sp.dma_start(tern_i[32 * s:32 * s + 32, :], packed_in.rearrange("(o i) -> o i", i=P)
                                 ).then_inc(*w_ld.up(16))
                sp.dma_start(weights13[:, 0:W3_N], weights3_in).then_inc(loads["ld_w3"], 16)

            @block.gpsimd
            def _(pool):
                pool.memset(zeros[:, :], 0.0).then_inc(*v_clear.up())
                pool.memset(QM[:, :, :].bitcast(F32), 0.0)
                pool.memset(gate_parts[:, :].bitcast(F32), 0.0)
                pool.memset(v_aug[:, :, :, :], 0.0).then_inc(*v_clear.up())
                pool.wait_ge(*v_clear.at(2))
                pool.memset(v_aug[:, :, :, DH:DH + 1], 1.0)

            @block.vector
            def _(dve):
                step = steps(dve, step_sig)
                dve.wait_ge(*w_ld.at(64))
                for s in range(4):
                    r = slice(32 * s, 32 * s + 32)
                    ins = dve.tensor_scalar(tern_i[r, :], tern_i[r, :], 2 * s, 3, ALU.logical_shift_right,
                                            ALU.bitwise_and)
                step(ins)
                step(dve.tensor_copy(tern_f[:, :], tern_i[:, :]))
                dve.tensor_scalar(tern_f[:, :], tern_f[:, :], 1.0, R("l1f_scale"), ALU.subtract, ALU.mult
                                  ).then_inc(*wt_in.up())
                step(dve.tensor_reduce(amax, x_tok[:, :, :], X_AXIS, ALU.max, apply_absolute_value=True))
                step(dve.tensor_scalar(amax, amax, 1e-5, None, ALU.max))
                step(dve.reciprocal(scl, amax))
                step(dve.tensor_scalar(scl, scl, 127.0, None, ALU.mult))
                step(dve.reciprocal(inv, scl))
                for t in range(NT):
                    ins = dve.tensor_scalar(sum_tok[:, t, :], x_tok[:, t, :], scl[:, t:t + 1], MAGIC, ALU.mult,
                                            ALU.add)
                step(ins)
                step(dve.tensor_scalar(sum_tok[:, :, :], sum_tok[:, :, :], MAGIC, 127.0, ALU.subtract, ALU.min))
                for t in range(NT):
                    ins = dve.tensor_scalar(sum_tok[:, t, :], sum_tok[:, t, :], -128.0, inv[:, t:t + 1], ALU.max,
                                            ALU.mult)
                    if t % QT == QT - 1:
                        ins.then_inc(*tq_done.up())
                dve.wait_ge(*v_clear.at(1))
                constant_rows(dve)

            @block.tensor
            def _(pe):
                pe.wait_ge(*wt_in.at(1))
                pe.transpose(bank[:, 0, 0:P], tern_f[:, :], ident).then_inc(*wt_done.up())
                for hf in range(2):
                    pe.wait_ge(*tq_done.at(hf + 1))
                    for q in range(QT):
                        ins = pe.transpose(bank[:, 1 + hf, q * P:(q + 1) * P], sum_tok[:, hf * QT + q, :], ident)
                    ins.then_inc(*wt_done.up())

            @block.scalar
            def _(act):
                act.wait_ge(*wt_done.at(1))
                act.copy(tern_w[:, :], bank[:, 0, 0:P])
                for hf in range(2):
                    act.wait_ge(*wt_done.at(2 + hf))
                    act.copy(y_feat[:, hf * HF:(hf + 1) * HF], bank[:, 1 + hf, :])
        signals.settle()

    tern_i = scratch[:, 0:P].bitcast(I32)
    tern_f = scratch[:, P:2 * P]
    tern_w = sb("tern_w", [P, P])

    def prepare_stage():
        with nc.Block() as block:
            @block.vector
            def _(dve):
                step = steps(dve, signals("dve_step"))
                dve.wait_ge(loads["ld_w"], 16)
                step(dve.memset(ones128[:, :], 1.0))
                dve.scalar_tensor_tensor(out=route_w[:, :], in0=W("l0_keys"), scalar=2.0, in1=W("l0_rw"),
                                         op0=ALU.mult, op1=ALU.add)

        signals.settle()

    def pair_stage():
        with nc.Block() as block:
            @block.vector
            def _(dve):
                for p_ in range(8):
                    for a in range(2):
                        dve.tensor_scalar(sel[:, p_, a * 64:(a + 1) * 64], ones128[:, 0:64],
                                          K("sel")[:, 2 * p_ + a:2 * p_ + a + 1], None, ALU.mult)

    prepare_stage()
    rsD = float(DH) ** -0.5

    norm_stage(hat=(C("l0_g"), C("l0_b")))
    project_stage(hat_feat, W("l0_qkv", 0, 128), W("l0_qkv", 128, 256), W("l0_qkv", 256, 384), C("l0_bqkv", 0),
                  C("l0_bqkv", 1), R("l0_bv"))
    attention_stage(rsD, guard=True)
    norm_stage([(att_feat[:, 0, :], W("l0_proj"))], bias=R("l0_bproj"))
    memory_stage()
    norm_stage([(y_feat, None)])
    route_stage([(x_feat, route_w[:, :])], R("l0_rb"), 16, 4, True, distance=True, first_expert=0)
    expert_stage(x_feat, 0, 16, W("l0_b2")[0:16, :])
    norm_stage([(y_feat, None)], hat=(C("l1_g"), None))

    layer_loads.append("ld_w1")
    wide_stage()
    norm_stage([(att_feat[:, p_, :], W("l1_wo", p_ * P, p_ * P + P)) for p_ in range(8)])
    cross_stage("l1x", C("l1x_bq"), C("l1x_bk"), R("l1x_bv"),
                lambda raw: (mask1_in.rearrange("a b (t p) k -> p (a b t) k", p=P), raw[:, 0:QT, :].bitcast(I32)),
                "q", H, rsD, 1e9 / rsD, lambda t: t % QT)
    norm_stage([(att_feat[:, 0, :], W("l1x", 384, 512))], bias=R("l1x_bo"))
    ternary_stage()
    norm_stage([(y_feat, tern_w[:, :])], bias=R("l1f_bias"))

    project_stage(x_feat, W("l2_attn", 0, 128), W("l2_attn", 128, 256), W("l2_attn", 256, 384), None, None, None,
                  K("l2_cos"), K("l2_sin"))
    attention_stage(rsD, causal=True)
    norm_stage([(att_feat[:, 0, :], W("l2_attn", 384, 512))])
    cross_stage("l2x", None, None, None,
                lambda raw: (mask2_in.rearrange("a b (t p) k -> p (a b t) k", p=P), raw[:, :, :].bitcast(I32)),
                "bq", H, D ** -0.5, 1e20, lambda t: t)
    norm_stage([(att_feat[:, 0, :], W("l2x", 384, 512))], bias=R("l2x_bo"), hat=(None, None), keep=True)
    for l in range(4):
        route_stage([(x_feat, W("l2_rw", 4 * l, 4 * l + 4))], R("l2_rb", 4 * l, 4 * l + 4), 4, 2, True,
                    first_expert=GROUP if l == 0 else None)
        expert_stage(hat_feat, GROUP + 4 * l, 4, W("l2_b2", l * P, l * P + P)[0:16, :])
        norm_stage([(y_feat, None)], residual_scale=gate_sum, norm=(l == 3),
                   plus=x_keep if l == 3 else None, hat=(None, None) if l < 3 else None)

    layer_loads.append("ld_w3")
    project_stage(x_feat, W("l3_qkv", 0, 128), W("l3_qkv", 128, 256), W("l3_qkv", 256, 384), C("l3_bqkv", 0),
                  C("l3_bqkv", 1), R("l3_bv"), K("l3_cos").broadcast_to([P, HF]), K("l3_sin").broadcast_to([P, HF]),
                  restore=True)
    attention_stage(rsD)
    norm_stage([(att_feat[:, 0, :], W("l3_fc"))], bias=R("l3_bfc"))
    cross_stage("l3x", C("l3x_bq"), C("l3x_bk"), R("l3x_bv"),
                lambda raw: (mask3_in.rearrange("b k -> (b k)").partition_broadcast(P),
                             raw[:, 0, :].bitcast(U8)[:, 0:B * SC]),
                "b", 1, D ** -0.5, 1e9 * D ** 0.5, lambda t: t // QT)
    norm_stage([(att_feat[:, 0, :], W("l3x", 384, 512))], bias=R("l3x_bo"))
    route_stage([(x_feat, W("l3_wg"))], None, 16, 2, False)
    pair_stage()
    gated_stage()
    norm_stage([(y_feat, None)], store=True)
    ctx.close()



def pack(parts, values, shape):
    out = np.zeros(shape, np.float32)
    at = 0
    for name, n in parts:
        v = values[name]
        out[:v.shape[0], at:at + n] = v
        at += n
    return out


def kernel(**inputs):
    import concourse.bacc as bacc
    from concourse.bass_utils import run_bass_kernel_spmd as run

    a = {n: np.asarray(v) for n, v in inputs.items()}

    def chunks(w):
        return w.reshape(-1, P, w.shape[-1]).transpose(1, 0, 2).reshape(P, -1)

    bil = np.zeros((P, 8, P), np.float32)
    for p_ in range(8):
        bil[0:64, p_, 0:64] = a["L1_attn_W_bilinear"][2 * p_]
        bil[64:128, p_, 64:128] = a["L1_attn_W_bilinear"][2 * p_ + 1]
    w1 = a["L3_ffn_W1"].reshape(8, 2, P, 2, 64).transpose(2, 0, 3, 1, 4).reshape(P, -1)
    b2 = np.zeros((P, 4, P), np.float32)
    b2[0:4] = a["L2_ffn_b2"].transpose(1, 0, 2)
    weights = {
        "l0_qkv": a["L0_attn_W_qkv"], "l0_proj": a["L0_attn_W_proj"], "l0_conv": chunks(a["L0_xattn_conv_w"].reshape(512, P)),
        "l0_keys": a["L0_ffn_keys"].T, "l0_rw": a["L0_ffn_rw"].T, "l0_b2": a["L0_ffn_b2"],
        "l1_wq": a["L1_attn_Wq"], "l1_wk": a["L1_attn_Wkv"][:, :1024], "l1_wv": a["L1_attn_Wkv"][:, 1024:],
        "l1_bil": bil.reshape(P, -1), "l1_wo": chunks(a["L1_attn_Wo"]),
        "l1x": np.concatenate([a[f"L1_xattn_W{n}"].T for n in "qkvo"], 1),
        "l2_attn": np.concatenate([a[f"L2_attn_{n}w"] for n in "qkvo"], 1),
        "l2x": np.concatenate([a[f"L2_xattn_W{n}"].T for n in "qkvo"], 1),
        "l2_rw": a["L2_ffn_router_w"].transpose(1, 0, 2).reshape(P, 16), "l2_b2": b2.reshape(P, -1),
        "l3_qkv": a["L3_attn_w_qkv"], "l3_fc": a["L3_attn_w_fc"],
        "l3x": np.concatenate([a[f"L3_xattn_W{n}"] for n in "qkvo"], 1),
        "l3_wg": a["L3_ffn_Wg"].T, "l3_w1": w1, "l3_w2": chunks(a["L3_ffn_W2"].reshape(1024, P)),
        "l3_ws1": a["L3_ffn_Ws1"], "l3_ws2": a["L3_ffn_Ws2"],
    }
    cols = {
        "l0_g": a["L0_attn_ln_gamma"], "l0_b": a["L0_attn_ln_beta"], "l0_bqkv": a["L0_attn_b_qkv"],
        "conv_b": a["L0_xattn_conv_b"], "l0_b1": a["L0_ffn_b1"], "l1_g": a["L1_attn_gamma"],
        "l1x_bq": a["L1_xattn_bq"], "l1x_bk": a["L1_xattn_bk"], "l2_g": a["L2_ffn_ln_g"], "l2_b": a["L2_ffn_ln_b"],
        "l2_b1": a["L2_ffn_b1"], "l3_bqkv": a["L3_attn_b_qkv"], "l3x_bq": a["L3_xattn_bq"],
        "l3x_bk": a["L3_xattn_bk"],
    }
    cols = {n: v.reshape(-1, P).T for n, v in cols.items()}
    rows = {
        "l0_bv": a["L0_attn_b_qkv"][256:], "l0_bproj": a["L0_attn_b_proj"], "l0_rb": a["L0_ffn_rb"],
        "l1x_bv": a["L1_xattn_bv"], "l1x_bo": a["L1_xattn_bo"], "l1f_bias": a["L1_ffn_bias"],
        "l1f_scale": a["L1_ffn_weight_scale"], "l2x_bo": a["L2_xattn_bo"], "l2_rb": a["L2_ffn_router_b"].reshape(-1),
        "l3_bv": a["L3_attn_b_qkv"][256:], "l3_bfc": a["L3_attn_b_fc"], "l3x_bv": a["L3_xattn_bv"],
        "l3x_bo": a["L3_xattn_bo"],
    }
    w2_0 = a["L0_ffn_w2"].transpose(0, 2, 1).reshape(16, 4, P, P).transpose(0, 2, 1, 3).reshape(16, P, 512)
    w2_2 = a["L2_ffn_w2"].reshape(16, 4, P, P).transpose(0, 2, 1, 3).reshape(16, P, 512)
    arrays = {
        "x": a["x"], "context": a["ctx_1024"], "mask1": a["mask_1x1xSxS2_if1"], "mask2": a["mask_Bx1xSxS2_ik1"],
        "mask3": a["mask_BxS2_bk0"], "packed": a["L1_ffn_packed_weight"],
        "constants": shape_constants(), "weights": pack(WEIGHTS, weights, (P, W_N)),
        "weights1": pack(WEIGHTS_1, weights, (P, W1_N)), "weights3": pack(WEIGHTS_3, weights, (P, W3_N)),
        "cols": pack(COLS, cols, (P, C_N)), "rows": np.concatenate([rows[n] for n, _ in ROWS]),
        "experts0": np.concatenate([a["L0_ffn_w1"].transpose(0, 2, 1), w2_0], 2),
        "experts2": np.concatenate([a["L2_ffn_w1"].reshape(16, P, 512), w2_2], 2),
    }
    nc = bacc.Bacc("TRN2", target_bir_lowering=False, num_devices=1)
    arrays = {f"in_{n}": np.ascontiguousarray(v) for n, v in arrays.items()}
    args = [nc.dram_tensor(n, v.shape, mybir.dt.from_np(v.dtype), kind="ExternalInput").ap()
            for n, v in arrays.items()]
    out = nc.dram_tensor("out_x", (B, S, D), F32, kind="ExternalOutput").ap()
    build(nc, *args, out)
    return run(nc, [arrays], core_ids=[0]).results[0]["out_x"]
```
